# Optimizing a Trainium2 kernel written in Bass

```python
import numpy as np
import jax
import jax.numpy as jnp

def _softmax(x, axis=-1):
    return jax.nn.softmax(x, axis=axis)

def _gelu(x):
    return jax.nn.gelu(x, approximate=True)

def _silu(x):
    return jax.nn.silu(x)

def _sigmoid(x):
    return jax.nn.sigmoid(x)

def _layernorm(x, axis=-1, eps=1e-05):
    m = jnp.mean(x, axis=axis, keepdims=True)
    v = jnp.var(x, axis=axis, keepdims=True)
    return (x - m) / jnp.sqrt(v + eps)

def _scatter_add(tgt, idx, src, axis=0):
    return tgt.at[idx].add(src)

def _segment_sum(src, seg, n):
    return jax.ops.segment_sum(src, seg, n)
kernel_name = 'mk_recurrent_d2_jaxref_r8_599468'

def setup_inputs(seed: int=0):
    np.random.seed(seed)
    _w = jnp.asarray

    def _L0_attn_setup():
        import jax, jax.numpy as jnp
        import numpy as np
        D_MODEL = 128
        N_HEADS = 16
        HEAD_DIM = D_MODEL // N_HEADS
        MAX_REL = 128
        B, S = (8, 128)
        key = jax.random.key(seed)
        ks = jax.random.split(key, 12)
        sc = 1.0 / np.sqrt(D_MODEL)
        return {'hidden_states': jax.random.normal(ks[0], (B, S, D_MODEL), jnp.float32), 'Wq': jax.random.normal(ks[1], (D_MODEL, D_MODEL), jnp.float32) * sc, 'bq': jnp.zeros((D_MODEL,), jnp.float32), 'Wk': jax.random.normal(ks[2], (D_MODEL, D_MODEL), jnp.float32) * sc, 'bk': jnp.zeros((D_MODEL,), jnp.float32), 'Wv': jax.random.normal(ks[3], (D_MODEL, D_MODEL), jnp.float32) * sc, 'bv': jnp.zeros((D_MODEL,), jnp.float32), 'Wo': jax.random.normal(ks[4], (D_MODEL, D_MODEL), jnp.float32) * sc, 'bo': jnp.zeros((D_MODEL,), jnp.float32), 'rel_emb': jax.random.normal(ks[5], (2 * MAX_REL + 1, HEAD_DIM), jnp.float32) * 0.02, 'M': jax.random.uniform(ks[6], (N_HEADS, HEAD_DIM, HEAD_DIM), jnp.float32), 'z': jax.random.uniform(ks[7], (N_HEADS, HEAD_DIM), jnp.float32), 'gate_alpha': jnp.float32(0.5)}
    _L0_attn_in = _L0_attn_setup()

    def _L0_ffn_setup():
        import jax, jax.numpy as jnp
        import numpy as np
        EXPERTS = 8
        TOP_K = 2

        def swiglu(x, w1, w2, w3):
            h = x @ w1
            return h * jax.nn.sigmoid(h) * (x @ w2) @ w3
        key = jax.random.key(seed)
        ks = jax.random.split(key, 9)
        B, S, D = (4, 256, 128)
        H = 2 * D
        s = 0.02
        x = jax.random.normal(ks[0], (B, S, D), dtype=jnp.float32)
        gate_w = jax.random.normal(ks[1], (D, EXPERTS), dtype=jnp.float32) * s
        ew1 = jax.random.normal(ks[2], (EXPERTS, D, H), dtype=jnp.float32) * s
        ew2 = jax.random.normal(ks[3], (EXPERTS, D, H), dtype=jnp.float32) * s
        ew3 = jax.random.normal(ks[4], (EXPERTS, H, D), dtype=jnp.float32) * s
        sw1 = jax.random.normal(ks[5], (D, H), dtype=jnp.float32) * s
        sw2 = jax.random.normal(ks[6], (D, H), dtype=jnp.float32) * s
        sw3 = jax.random.normal(ks[7], (H, D), dtype=jnp.float32) * s
        return {'x': x, 'gate_w': gate_w, 'ew1': ew1, 'ew2': ew2, 'ew3': ew3, 'sw1': sw1, 'sw2': sw2, 'sw3': sw3}
    _L0_ffn_in = _L0_ffn_setup()

    def _L1_attn_setup():
        import jax, jax.numpy as jnp
        import numpy as np
        import math
        D_MODEL = 128
        N_HEAD = 16
        HEAD_DIM = D_MODEL // N_HEAD

        def _split_heads(t):
            B, S, _ = t.shape
            return t.reshape(B, S, N_HEAD, HEAD_DIM).transpose(0, 2, 1, 3)
        key = jax.random.key(seed)
        ks = jax.random.split(key, 9)
        B, S = (2, 256)
        x = jax.random.normal(ks[0], (B, S, D_MODEL), dtype=jnp.float32)
        w = lambda k, std: jax.random.normal(k, (D_MODEL, D_MODEL), dtype=jnp.float32) * std
        return {'x': x, 'Wq_amp': w(ks[1], 0.02), 'Wk_amp': w(ks[2], 0.02), 'Wq_phi': w(ks[3], 0.005), 'Wk_phi': w(ks[4], 0.005), 'Wv': w(ks[5], 0.02), 'Wo': w(ks[6], 0.02), 'score_log_scale': jnp.zeros((N_HEAD,), dtype=jnp.float32)}
    _L1_attn_in = _L1_attn_setup()

    def _L1_ffn_setup():
        import jax, jax.numpy as jnp
        import numpy as np
        D = 128
        H = 128
        E = 8
        K = 2
        I = 2 * 128
        ROUTE_SCALE = 1.0
        key = jax.random.key(seed)
        ks = jax.random.split(key, 12)
        s = lambda *sh: 1.0 / np.sqrt(sh[-1])
        return {'x': jax.random.normal(ks[0], (1, 256, D), jnp.float32), 'gate_w': jax.random.normal(ks[1], (E, D), jnp.float32) * s(E, D), 'w1': jax.random.normal(ks[2], (E, H, D), jnp.float32) * s(H, D), 'b1': jax.random.normal(ks[3], (E, H), jnp.float32) * 0.01, 'w2': jax.random.normal(ks[4], (E, D, H), jnp.float32) * s(D, H), 'b2': jax.random.normal(ks[5], (E, D), jnp.float32) * 0.01, 'w3': jax.random.normal(ks[6], (E, H, D), jnp.float32) * s(H, D), 'b3': jax.random.normal(ks[7], (E, H), jnp.float32) * 0.01, 'sw1': jax.random.normal(ks[8], (I, D), jnp.float32) * s(I, D), 'sw2': jax.random.normal(ks[9], (I, D), jnp.float32) * s(I, D), 'sw3': jax.random.normal(ks[10], (D, I), jnp.float32) * s(D, I)}
    _L1_ffn_in = _L1_ffn_setup()
    _d = {'L0_attn_hidden_states': _L0_attn_in['hidden_states'], 'L0_attn_Wq': _L0_attn_in['Wq'], 'L0_attn_bq': _L0_attn_in['bq'], 'L0_attn_Wk': _L0_attn_in['Wk'], 'L0_attn_bk': _L0_attn_in['bk'], 'L0_attn_Wv': _L0_attn_in['Wv'], 'L0_attn_bv': _L0_attn_in['bv'], 'L0_attn_Wo': _L0_attn_in['Wo'], 'L0_attn_bo': _L0_attn_in['bo'], 'L0_attn_rel_emb': _L0_attn_in['rel_emb'], 'L0_attn_M': _L0_attn_in['M'], 'L0_attn_z': _L0_attn_in['z'], 'L0_attn_gate_alpha': _L0_attn_in['gate_alpha'], 'L0_ffn_gate_w': _L0_ffn_in['gate_w'], 'L0_ffn_ew1': _L0_ffn_in['ew1'], 'L0_ffn_ew2': _L0_ffn_in['ew2'], 'L0_ffn_ew3': _L0_ffn_in['ew3'], 'L0_ffn_sw1': _L0_ffn_in['sw1'], 'L0_ffn_sw2': _L0_ffn_in['sw2'], 'L0_ffn_sw3': _L0_ffn_in['sw3'], 'L1_attn_Wq_amp': _L1_attn_in['Wq_amp'], 'L1_attn_Wk_amp': _L1_attn_in['Wk_amp'], 'L1_attn_Wq_phi': _L1_attn_in['Wq_phi'], 'L1_attn_Wk_phi': _L1_attn_in['Wk_phi'], 'L1_attn_Wv': _L1_attn_in['Wv'], 'L1_attn_Wo': _L1_attn_in['Wo'], 'L1_attn_score_log_scale': _L1_attn_in['score_log_scale'], 'L1_ffn_gate_w': _L1_ffn_in['gate_w'], 'L1_ffn_w1': _L1_ffn_in['w1'], 'L1_ffn_b1': _L1_ffn_in['b1'], 'L1_ffn_w2': _L1_ffn_in['w2'], 'L1_ffn_b2': _L1_ffn_in['b2'], 'L1_ffn_w3': _L1_ffn_in['w3'], 'L1_ffn_b3': _L1_ffn_in['b3'], 'L1_ffn_sw1': _L1_ffn_in['sw1'], 'L1_ffn_sw2': _L1_ffn_in['sw2'], 'L1_ffn_sw3': _L1_ffn_in['sw3']}
    _x0 = _d['L0_attn_hidden_states']
    _d['L0_attn_hidden_states'] = jax.random.normal(jax.random.fold_in(jax.random.key(seed), 1), (4, 512, 128), dtype=_x0.dtype)
    del _x0
    return _d

def reference(L0_attn_hidden_states, L0_attn_Wq, L0_attn_bq, L0_attn_Wk, L0_attn_bk, L0_attn_Wv, L0_attn_bv, L0_attn_Wo, L0_attn_bo, L0_attn_rel_emb, L0_attn_M, L0_attn_z, L0_attn_gate_alpha, L0_ffn_gate_w, L0_ffn_ew1, L0_ffn_ew2, L0_ffn_ew3, L0_ffn_sw1, L0_ffn_sw2, L0_ffn_sw3, L1_attn_Wq_amp, L1_attn_Wk_amp, L1_attn_Wq_phi, L1_attn_Wk_phi, L1_attn_Wv, L1_attn_Wo, L1_attn_score_log_scale, L1_ffn_gate_w, L1_ffn_w1, L1_ffn_b1, L1_ffn_w2, L1_ffn_b2, L1_ffn_w3, L1_ffn_b3, L1_ffn_sw1, L1_ffn_sw2, L1_ffn_sw3):

    def _L0_attn_ref(hidden_states, Wq, bq, Wk, bk, Wv, bv, Wo, bo, rel_emb, M, z, gate_alpha):
        import jax, jax.numpy as jnp
        import numpy as np
        D_MODEL = 128
        N_HEADS = 16
        HEAD_DIM = D_MODEL // N_HEADS
        MAX_REL = 128
        B, S = (8, 128)
        b, s, _ = hidden_states.shape

        def proj(W, bias):
            y = hidden_states @ W.T + bias
            return y.reshape(b, s, N_HEADS, HEAD_DIM).transpose(0, 2, 1, 3)
        q = proj(Wq, bq)
        k = proj(Wk, bk)
        v = proj(Wv, bv)
        dist = jnp.arange(s)[:, None] - jnp.arange(s)[None, :]
        dist = jnp.clip(dist, -MAX_REL, MAX_REL) + MAX_REL
        rel_pos = rel_emb[dist]
        scores = jnp.einsum('bhqd,bhkd->bhqk', q, k)
        scores = scores + jnp.einsum('bhqd,qkd->bhqk', q, rel_pos)
        scores = scores / np.sqrt(HEAD_DIM).astype(np.float32)
        attn = jax.nn.softmax(scores, axis=-1)
        local_ctx = jnp.einsum('bhqk,bhkd->bhqd', attn, v)
        sigma_q = jax.nn.elu(q) + 1.0
        num = jnp.einsum('bhqk,hkv->bhqv', sigma_q, M)
        den = jnp.einsum('bhqk,hk->bhq', sigma_q, z) + 1e-06
        global_attn = num / den[..., None]
        gate = jax.nn.sigmoid(gate_alpha)
        combined = gate * local_ctx + (1.0 - gate) * global_attn
        out = combined.transpose(0, 2, 1, 3).reshape(b, s, D_MODEL)
        return out @ Wo.T + bo

    def _L0_ffn_ref(x, gate_w, ew1, ew2, ew3, sw1, sw2, sw3):
        import jax, jax.numpy as jnp
        import numpy as np
        EXPERTS = 8
        TOP_K = 2

        def swiglu(x, w1, w2, w3):
            h = x @ w1
            return h * jax.nn.sigmoid(h) * (x @ w2) @ w3
        B, S, D = x.shape
        gate_out = x @ gate_w
        top_v, top_i = jax.lax.top_k(gate_out, TOP_K)
        masked = jnp.full_like(gate_out, -1e+20)
        bi = jnp.arange(B)[:, None, None]
        si = jnp.arange(S)[None, :, None]
        masked = masked.at[bi, si, top_i].set(top_v)
        probs = jax.nn.softmax(masked, axis=-1)
        chosen = jnp.zeros_like(gate_out, dtype=bool).at[bi, si, top_i].set(True)
        w = jnp.where(chosen, probs, 0.0)

        def one_expert(w1, w2, w3, we):
            return swiglu(x, w1, w2, w3) * we[..., None]
        out = jax.vmap(one_expert, in_axes=(0, 0, 0, 2))(ew1, ew2, ew3, w).sum(0)
        out = out + swiglu(x, sw1, sw2, sw3)
        return out

    def _L1_attn_ref(x, Wq_amp, Wk_amp, Wq_phi, Wk_phi, Wv, Wo, score_log_scale):
        import jax, jax.numpy as jnp
        import numpy as np
        import math
        D_MODEL = 128
        N_HEAD = 16
        HEAD_DIM = D_MODEL // N_HEAD

        def _split_heads(t):
            B, S, _ = t.shape
            return t.reshape(B, S, N_HEAD, HEAD_DIM).transpose(0, 2, 1, 3)
        B, S, _ = x.shape
        eps = 1e-06
        q_amp = _split_heads(jax.nn.softplus(x @ Wq_amp.T))
        k_amp = _split_heads(jax.nn.softplus(x @ Wk_amp.T))
        q_phi = _split_heads(math.pi * jnp.tanh(x @ Wq_phi.T))
        k_phi = _split_heads(math.pi * jnp.tanh(x @ Wk_phi.T))
        q_amp = q_amp / jnp.sqrt(jnp.mean(q_amp * q_amp, axis=-1, keepdims=True) + eps)
        k_amp = k_amp / jnp.sqrt(jnp.mean(k_amp * k_amp, axis=-1, keepdims=True) + eps)
        q_cos = q_amp * jnp.cos(q_phi)
        q_sin = q_amp * jnp.sin(q_phi)
        k_cos = k_amp * jnp.cos(k_phi)
        k_sin = k_amp * jnp.sin(k_phi)
        scores = (jnp.einsum('bhqd,bhkd->bhqk', q_cos, k_cos) + jnp.einsum('bhqd,bhkd->bhqk', q_sin, k_sin)) / math.sqrt(HEAD_DIM)
        scores = scores * jnp.exp(score_log_scale)[None, :, None, None]
        mask = jnp.tril(jnp.ones((S, S), dtype=bool))
        scores = jnp.where(mask[None, None], scores, -jnp.inf)
        attn = jax.nn.softmax(scores, axis=-1)
        v = _split_heads(x @ Wv.T)
        out = jnp.einsum('bhqk,bhkd->bhqd', attn, v)
        out = out.transpose(0, 2, 1, 3).reshape(B, S, D_MODEL)
        return out @ Wo.T

    def _L1_ffn_ref(x, gate_w, w1, b1, w2, b2, w3, b3, sw1, sw2, sw3):
        import jax, jax.numpy as jnp
        import numpy as np
        D = 128
        H = 128
        E = 8
        K = 2
        I = 2 * 128
        ROUTE_SCALE = 1.0
        B, S, _ = x.shape
        xt = x.reshape(-1, D)
        logits = xt @ gate_w.T
        scores = jax.nn.softmax(logits.astype(jnp.float32), axis=-1)
        top_vals, idx = jax.lax.top_k(scores, K)
        weights = jnp.take_along_axis(scores, idx, axis=1).astype(x.dtype) * ROUTE_SCALE
        xs = xt[:, None, :] * weights[:, :, None]
        y = jnp.zeros_like(xt)
        for e in range(E):
            mask = (idx == e).astype(x.dtype)
            h = jax.nn.silu(jnp.einsum('tkd,hd->tkh', xs, w1[e]) + b1[e])
            x2 = jnp.einsum('tkh,dh->tkd', h, w2[e]) + b2[e]
            x3 = jnp.einsum('tkd,hd->tkh', xs, w3[e]) + b3[e]
            y = y + jnp.sum(x2 * x3 * mask[:, :, None], axis=1)
        z = jax.nn.silu(xt @ sw1.T) * (xt @ sw2.T) @ sw3.T
        return (y + z).reshape(B, S, D)
    x = L0_attn_hidden_states
    xn = _layernorm(x, axis=-1)
    s = _L0_attn_ref(xn, L0_attn_Wq, L0_attn_bq, L0_attn_Wk, L0_attn_bk, L0_attn_Wv, L0_attn_bv, L0_attn_Wo, L0_attn_bo, L0_attn_rel_emb, L0_attn_M, L0_attn_z, L0_attn_gate_alpha)
    g = _silu(_L0_ffn_ref(xn, L0_ffn_gate_w, L0_ffn_ew1, L0_ffn_ew2, L0_ffn_ew3, L0_ffn_sw1, L0_ffn_sw2, L0_ffn_sw3))
    x = x + s * g
    xn = _layernorm(x, axis=-1)
    s = _L1_attn_ref(xn, L1_attn_Wq_amp, L1_attn_Wk_amp, L1_attn_Wq_phi, L1_attn_Wk_phi, L1_attn_Wv, L1_attn_Wo, L1_attn_score_log_scale)
    g = _silu(_L1_ffn_ref(xn, L1_ffn_gate_w, L1_ffn_w1, L1_ffn_b1, L1_ffn_w2, L1_ffn_b2, L1_ffn_w3, L1_ffn_b3, L1_ffn_sw1, L1_ffn_sw2, L1_ffn_sw3))
    x = x + s * g
    return x

_drawn_inputs = setup_inputs


def setup_inputs(seed=0):
    import zlib

    import numpy as np

    out = dict(_drawn_inputs(seed))
    spreads = {'L0_attn_bq': (0.0, 0.8),
     'L0_attn_bk': (0.0, 2.0),
     'L0_attn_bv': (0.0, 0.8),
     'L0_attn_bo': (0.0, 0.8),
     'L1_attn_score_log_scale': (0.0, 0.8)}
    factors = {'L0_attn_Wq': 8.0,
     'L0_attn_Wk': 8.0,
     'L0_attn_Wv': 8.0,
     'L0_attn_Wo': 8.0,
     'L0_attn_rel_emb': 8.0,
     'L0_attn_M': 8.0,
     'L0_attn_z': 8.0,
     'L0_ffn_gate_w': 8.0,
     'L0_ffn_ew1': 8.0,
     'L0_ffn_ew2': 8.0,
     'L0_ffn_ew3': 8.0,
     'L0_ffn_sw1': 8.0,
     'L0_ffn_sw2': 8.0,
     'L0_ffn_sw3': 8.0,
     'L1_attn_Wq_amp': 8.0,
     'L1_attn_Wk_amp': 8.0,
     'L1_attn_Wq_phi': 8.0,
     'L1_attn_Wk_phi': 8.0,
     'L1_attn_Wv': 8.0,
     'L1_attn_Wo': 8.0,
     'L1_ffn_gate_w': 8.0,
     'L1_ffn_w1': 8.0,
     'L1_ffn_b1': 64.0,
     'L1_ffn_w2': 8.0,
     'L1_ffn_b2': 200.0,
     'L1_ffn_w3': 8.0,
     'L1_ffn_b3': 64.0,
     'L1_ffn_sw1': 8.0,
     'L1_ffn_sw2': 8.0,
     'L1_ffn_sw3': 8.0}
    for name, (base, spread) in spreads.items():
        noise = np.random.default_rng([zlib.crc32(name.encode()), seed]).standard_normal(out[name].shape)
        drawn = base * np.exp(spread * noise) if base else spread * noise
        out[name] = jnp.asarray(drawn.astype(out[name].dtype))
    for name, factor in factors.items():
        out[name] = (out[name] * factor).astype(out[name].dtype)
    return out
```

```python
from contextlib import ExitStack
from math import pi, sqrt

import numpy as np
import concourse.bass as bass
from concourse import mybir

F32 = mybir.dt.float32
BF16 = mybir.dt.bfloat16
ALU = mybir.AluOpType
ACT = mybir.ActivationFunctionType
AX = mybir.AxisListType

P = 128
B, S, D = 4, 512, 128
H, HD = 16, 8
T = S // P
E = 8
F0 = 256
HID = 128
REL = 128
NQ = 32
SLOTS = 6
ROWS = 2 * SLOTS * HD
Q_RUNS = ((0, 3), (3, 2), (5, 1))
K_RUNS = ((0, 3, 0), (3, 2, 1), (5, 1, 2))
RING = 7
TILE = H * P
NEG = -1e30
LN_EPS = 1e-5

B_H, B_U, B_O, B_PV, B_MISC, B_S = 0, 1, 2, 3, 4, 5
NSB = 3

COLS_A = [("WqT", D), ("WkT", D), ("WvT", D), ("gate0", E), ("Mbd", D), ("Zbd", D), ("ident", P), ("idx", E),
          ("bq", 1), ("bk", 1), ("bv", 1), ("e_near", 1), ("e_far", 1), ("alpha", 1), ("sls", 1), ("halfpi", 1),
          ("b1", E), ("b2", E), ("b3", E), ("seld", P), ("mean8", P), ("maskn", P), ("maskt", P), ("bo", D),
          ("WoT", D), ("WoP", 2 * D), ("sw1", F0), ("sw2", F0), ("sw3", 2 * D)]
COLS_B = [("ew1", E * F0), ("ew2", E * F0), ("ew3", E * 2 * D)]
COLS_C = [("Wqa", D), ("Wka", D), ("Wqp", D), ("Wkp", D), ("Wv1", D), ("WoP1", 2 * D), ("gate1", E),
          ("tw1", E * HID), ("tw2", E * D), ("tw3", E * HID), ("tsw1", F0), ("tsw2", F0), ("tsw3", 2 * D)]


def offsets(cols):
    at, out = 0, {}
    for name, n in cols:
        out[name] = (at, n)
        at += n
    return out, at


OFF_A, NA = offsets(COLS_A)
OFF_B, NB = offsets(COLS_B)
OFF_C, NC = offsets(COLS_C)

NSLOT0 = 24
AT_MAX, AT_SUB, AT_PV, AT_EVAC, AT_ALIGN, AT_OUT = 4, 5, 6, 9, 10, 11
FFN_BEFORE = 6
FFN_AT = {1: 6, 3: 7, 5: 8, 7: 9, 9: 10, 11: 11, 13: 12, 15: 13, 16: 14, 17: 15, 18: 16, 19: 17}


def program(nc, x, wa, wb, wc, etab, out):
    ctx = ExitStack()
    with ctx:
        def sb(name, shape, dt=F32):
            return ctx.enter_context(nc.sbuf_tensor(name, shape, dt))

        def sem(name):
            s = ctx.enter_context(nc.semaphore(name))
            return s

        per_batch = []

        def bsem(name):
            s = sem(name)
            per_batch.append(s)
            return s

        WA = sb("WA", [P, NA])
        WB = sb("WB", [P, NB])
        WC = sb("WC", [P, NC])

        def w(name, a=0, n=None):
            for off, t in ((OFF_A, WA), (OFF_B, WB), (OFF_C, WC)):
                if name in off:
                    at, width = off[name]
                    return t[:, at + a:at + a + (width if n is None else n)]

        ET = sb("ET", [ROWS, 4 * P], BF16)
        QBD = sb("QBD", [ROWS, H // 2, 2, S], BF16)
        KS = sb("KS", [P, 2, H // 2, S], BF16)
        QR = sb("QR", [P, H, S], BF16)
        KL = KS[:, :, :, :].rearrange("p a b s -> p (a b) s")
        QL = QR
        VP = sb("VP", [P, T, H, 32])
        RG = sb("RG", [P, RING * TILE])
        MB = sb("MB", [P, TILE])
        X = sb("X", [P, T, D])
        XN = sb("XN", [P, T, D])
        XT = sb("XT", [P, S])
        G = sb("G", [P, S])
        TH = sb("TH", [P, S])
        AA = sb("AA", [P, S])
        HH = sb("HH", [P, 2, 2, S])
        ACC = sb("ACC", [P, T, D])
        SS = sb("SS", [P, T, D])
        R1 = sb("R1", [P, T, H * T])
        M1 = sb("M1", [P, H * T])
        M2 = sb("M2", [H * T, NQ])
        NM = sb("NM", [H * T, P])
        NR = sb("NR", [H * T, P])
        NMP = sb("NMP", [H * T, 3, P], BF16)
        CTX = sb("CTX", [P, 2 * P])
        RDN = sb("RDN", [P, 2 * P])
        CN = sb("CN", [P, 2 * P])
        IDB = sb("IDB", [P, P], BF16)
        MKN = sb("MKN", [P, P], BF16)
        MKT = sb("MKT", [P, P], BF16)
        half = sb("half", [P, T])
        st = sb("st", [P, T, 6])
        mv = sb("mv", [P, T, 2])
        ve = sb("ve", [P, T])
        rs = sb("rs", [P, T])
        cols = sb("cols", [P, 8])
        gate_e, gate_s, gate, omg, gbv, esl = (cols[:, i:i + 1] for i in range(6))
        LG, EQ, KEY, OH1, OH2, W8, WM = (sb(f"rt{i}", [P, T, E]) for i in range(7))
        m1, m2, km, dm, e2, w1, w2 = (sb(f"rv{i}", [P, T]) for i in range(7))
        WMK = sb("WMK", [P, T, 2 * E])
        WT = SS[0:2 * E, :, :].rearrange("p t d -> p (t d)")
        hb1 = sb("hb1", [P, E])

        def region(at, n, dt=F32):
            v = RG[:, at:at + n]
            return v if dt is F32 else v.bitcast(dt)

        F3 = region(0, 3 * S).rearrange("p (a s) -> p a s", a=3)
        R3 = region(3 * S, 3 * S).rearrange("p (a s) -> p a s", a=3)
        PARTS = region(6 * S, 9 * S // 2, BF16).rearrange("p (a c s) -> p a c s", a=3, c=3)
        QEO = region(11 * S, 3 * S, BF16).rearrange("p (a c s) -> p a c s", a=2, c=3)
        QMIN, QEX, SG, DEN, RDEN = (region((14 + i) * S, S) for i in range(5))
        Z, TP, NAB, EX, U1, C1, LNU, SQ, RT = (region(2 * S * i, 2 * S) for i in range(9))
        CS4 = region(18 * S, 4 * S).rearrange("p (t c s) -> p t c s", t=2, c=2)
        R4 = region(0, 4 * S).rearrange("p (t c s) -> p t c s", t=2, c=2)
        PARTS1 = region(4 * S, 6 * S, BF16).rearrange("p (t c u s) -> p t c u s", t=2, c=3, u=2)
        PCOL = (0, 512, 896, 1152)
        PH = 1280
        PL = region(0, 2 * 4 * PH).rearrange("p (b j n) -> p b j n", b=2, j=4)
        CT1 = region(20 * S, 2 * S).rearrange("p (a s) -> p a s", a=2)
        RD1 = region(22 * S, 2 * S).rearrange("p (a s) -> p a s", a=2)
        CN1 = region(24 * S, 2 * S).rearrange("p (a s) -> p a s", a=2)
        XS = region(26 * S, 2 * S).rearrange("p (a s) -> p a s", a=2)
        YT = G
        C3 = HH[:, 0, 0, :]
        HE = HH[:, 0, 1, :]
        CC = HH[:, 1, :, :]
        MBE = MB[:, :].rearrange("p (b a s) -> p b a s", b=2, a=2)

        PS = ctx.enter_context(nc.psum_tensor("PS", [P, 8, 512], F32))

        def bank(i, n=512, a=0):
            return PS[:, i, a:a + n]

        d_q = nc.dram_tensor("d_q", [3, HD, H, S], BF16).ap()
        d_k = nc.dram_tensor("d_k", [2, SLOTS, HD, H, S], BF16).ap()
        d_e = nc.dram_tensor("d_e", [6, HD, H, S], BF16).ap()
        d_m = nc.dram_tensor("d_m", [2, H * T, NQ], F32).ap()
        d_c = nc.dram_tensor("d_c", [2, 3, 2, HD, H, S], BF16).ap()
        d_n = nc.dram_tensor("d_n", [3, H * T, P], BF16).ap()
        d_w = nc.dram_tensor("d_w", [2 * E, S], F32).ap()
        d_t = nc.dram_tensor("d_t", [3, 2 * HD, 4 * P], BF16).ap()

        s_wa, s_wb, s_wc, s_et, s_etd, s_etl = (sem(n) for n in ("wa_in", "wb_in", "wc_in", "etab_in", "etab_out", "etab_set"))
        s_pre_pool, s_pre_dve, s_gexp, s_etp = (sem(n) for n in ("pool_set", "dve_set", "gate_exp", "etab_parts"))
        s_arrived, s_cleared = sem("sequence_ended"), sem("semaphores_cleared")
        chain_dve, chain_act, chain_pool = sem("dve_step"), sem("act_step"), sem("pool_step")
        x_in, var_ready, rstd_ready, xn_ready, xt_ps, xt_ready = (bsem(n) for n in ("x_in", "var", "rstd", "xn", "xt_psum", "xt"))
        proj_q, proj_k, proj_v, logit_ps, qk_sb, v_set, logits_read = (
            bsem(n) for n in ("q_psum", "k_psum", "v_psum", "logits_psum", "qk_sbuf", "v_set", "logits_read"))
        qeo_zero, parts_ready, qeo_ready, dq_out, de_out, qk_in, rel_in = (
            bsem(n) for n in ("qeo_zero", "parts", "qeo", "parts_in_dram", "qeo_in_dram", "qk_stacked", "qrel_stacked"))
        qmin_ready, qexp_ready, sg_ready, glob_ps, g_ready = (bsem(n) for n in ("qmin", "qexp", "sigma", "global_psum", "global"))
        rdm_ready, rexp_ready = bsem("route_diff"), bsem("route_exp")
        hu_ps, th_ready, hh_ready, fo_ps, fo_used = (bsem(n) for n in ("hu_psum", "tanh", "hh", "ffn_psum", "ffn_added"))
        sc_ps, sc_copied, red_done, m1_ready, mt_ps, m2_ready = (
            bsem(n) for n in ("scores_psum", "scores_copied", "maxed", "max_of_keys", "max_transposed", "max_rows"))
        dm_out, mb_in, sub_dve, sub_pool, p_ready, pv_done = (
            bsem(n) for n in ("max_in_dram", "max_spread", "shifted_dve", "shifted_pool", "probs", "pv"))
        ctx_ready, al_ps, cn_ready, at_ps, ss_ready = (bsem(n) for n in ("ctx", "den_psum", "ctx_normed", "attn_psum", "attn"))
        ga_ready, x1_ready = bsem("gelu_tanh0"), bsem("x1")
        var1, rstd1, xn1, xt_ps1, xt1 = (bsem(n) for n in ("var1", "rstd1", "xn1", "xt_psum1", "xt1"))
        amp_ps, phi_ps, v_ps1, lg_ps1, z_sb, tp_sb, v_set1, lg_read1 = (
            bsem(n) for n in ("amp_psum", "phi_psum", "v_psum1", "logits_psum1", "amp_sbuf", "phase", "v_set1", "logits_read1"))
        nab_r, ex_r, u_r, ln_r, amp_r, sq_r, msq_ps, rt_r, abs_r, cos_r, parts1, dc_out, l1_in = (
            bsem(n) for n in ("neg_abs", "exp_abs", "one_plus", "ln", "amp", "amp_sq", "meansq_psum", "rms", "phase_abs",
                              "cos_sin", "parts1", "parts1_in_dram", "stacked1"))
        lge_r, lgx_r, wm_r, wt_ps, wt_r, dw_out, wb_in0, wb_in1, xs_r = (
            bsem(n) for n in ("l1_route_diff", "l1_route_exp", "weights1", "weights_psum", "weights_t", "weights_in_dram",
                              "expert_spread_even", "expert_spread_odd", "xs"))
        wb_in = (wb_in0, wb_in1)
        hu1_ps, th1_r, h1_r, fo1_ps, y_c, y_add, yt_ps, yn_r = (
            bsem(n) for n in ("hu1_psum", "tanh1", "hh1", "ffn1_psum", "expert_term", "y_added", "y_psum", "y_used"))
        s1_ps, s1_max, nmt_ps, nm_r, dn_out, nm_in = (
            bsem(n) for n in ("s1_psum", "s1_maxed", "max1_transposed", "neg_max", "neg_max_in_dram", "neg_max_in"))
        s2_ps, p1_r, pv1, ctx1, al1_ps, cn1, at1_ps, ga1, xo_r, out_done = (
            bsem(n) for n in ("s2_psum", "probs1", "pv1", "ctx1", "den1_psum", "ctx1_normed", "attn1_psum",
                              "gelu_tanh1", "x_out", "out_written"))

        groups = {}
        names = ("sync", "gpsimd", "tensor", "vector", "scalar")
        for i, s in enumerate(per_batch):
            groups.setdefault(names[i % 5], []).append(s)

        def end_sequence(eng, name, b, own=None):
            eng.sem_inc(s_arrived, 1)
            eng.wait_ge(s_arrived, (b + 1) * 5)
            eng.nop(nofuse=True)
            for s in groups[name] + ([own] if own is not None else []):
                eng.sem_clear(s)
            eng.sem_inc(s_cleared, 1)
            eng.wait_ge(s_cleared, (b + 1) * 5)
            eng.nop(nofuse=True)

        block = ctx.enter_context(nc.Block())

        @block.sync
        def _(sp):
            sp.dma_start(WA[:, :], wa).then_inc(s_wa, 16)
            sp.dma_start(TH[0:2 * HD, :], etab).then_inc(s_et, 16)
            sp.dma_start(WB[:, :], wb).then_inc(s_wb, 16)
            sp.wait_ge(s_etp, 1)
            sp.dma_start(d_t.rearrange("c r n -> r c n"), HH[0:2 * HD, 0, :, :].rearrange("p a s -> p (a s)")
                         .bitcast(BF16)[:, 0:3 * S].rearrange("p (c s) -> p c s", c=3)).then_inc(s_etd, 16)
            sp.wait_ge(s_etd, 16)
            for two in range(2):
                for first, n, part in K_RUNS:
                    for j in range(n):
                        r = two * SLOTS * HD + (first + j) * HD
                        sp.dma_start(ET[r:r + HD, :], d_t[part, two * HD:(two + 1) * HD, :]).then_inc(s_etl, 16)
            sp.dma_start(WC[:, :], wc).then_inc(s_wc, 16)
            with sp.Fori(0, B) as b:
                sp.dma_start(X[:, :, :], x[bass.ds(b * S, S), :].rearrange("(t p) d -> p t d", p=P)).then_inc(x_in, 16)
                sp.wait_ge(parts_ready, 1)
                sp.dma_start(d_q.rearrange("c d h s -> (d h) c s"), PARTS[:, 0, :, :]).then_inc(dq_out, 16)
                for t in range(2):
                    for first, n, part in K_RUNS:
                        sp.dma_start(d_k[t, first:first + n].rearrange("c d h s -> (d h) c s"),
                                     PARTS[:, 1 + t, part:part + 1, :].to_broadcast([P, n, S])).then_inc(dq_out, 16)
                sp.wait_ge(dq_out, 16 * 7)
                for two in range(2):
                    for first, n in Q_RUNS:
                        r = two * SLOTS * HD + first * HD
                        sp.dma_start(QBD[r:r + n * HD, :, two, :],
                                     d_q[0:n].rearrange("c d (a t) s -> t (c d) a s", t=2)[two]).then_inc(qk_in, 16)
                    r = two * SLOTS * HD
                    for t in range(2):
                        sp.dma_start(KS[r:r + SLOTS * HD, t, :, :],
                                     d_k[t].rearrange("c d (a t) s -> t (c d) a s", t=2)[two]).then_inc(qk_in, 16)
                sp.wait_ge(qeo_ready, 1)
                sp.dma_start(d_e.rearrange("c d h s -> (d h) c s"), QEO.rearrange("p a c s -> p (a c) s")).then_inc(de_out, 16)
                sp.wait_ge(de_out, 16)
                for two in range(2):
                    for first, n in Q_RUNS:
                        r = two * SLOTS * HD + first * HD
                        sp.dma_start(QR[r:r + n * HD, :, :],
                                     d_e[3 * two:3 * two + n].rearrange("c d h s -> (c d) h s")).then_inc(rel_in, 16)
                for u in range(T):
                    sp.wait_ge(m2_ready, u + 1)
                    sp.dma_start(d_m[u % 2], M2[:, :]).then_inc(dm_out, 16)
                    sp.wait_ge(dm_out, 16 * (u + 1))
                    if u:
                        sp.wait_ge(sub_dve, u)
                        sp.wait_ge(sub_pool, 3 * u)
                    sp.dma_start(MB[:, :], d_m[u % 2].rearrange("c i -> (c i)")[None, :].to_broadcast([P, TILE])
                                 ).then_inc(mb_in, 16)
                sp.wait_ge(wt_r, 1)
                sp.dma_start(d_w, WT[:, :]).then_inc(dw_out, 16)
                sp.wait_ge(dw_out, 16)

                def spread(e):
                    if e >= 2:
                        sp.wait_ge(y_c, e - 1)
                        sp.wait_ge(xs_r, e - 1)
                    for a in range(2):
                        sp.dma_start(MBE[:, e % 2, a, :], d_w[a * E + e:a * E + e + 1, :].to_broadcast([P, S])
                                     ).then_inc(wb_in[e % 2], 16)

                sp.wait_ge(sub_dve, T)
                sp.wait_ge(sub_pool, 3 * T)
                spread(0)
                spread(1)
                sp.wait_ge(parts1, 1)
                sp.dma_start(d_c.rearrange("t c u d h s -> (d h) (t c u) s"),
                             PARTS1.rearrange("p t c u s -> p (t c u) s")).then_inc(dc_out, 16)
                sp.wait_ge(dc_out, 16)
                for first, n in Q_RUNS:
                    sp.dma_start(QL[2 * first * HD:2 * (first + n) * HD, :, :],
                                 d_c[0, 0:n].rearrange("c u d h s -> (c u d) h s")).then_inc(l1_in, 16)
                for first, n, part in K_RUNS:
                    r = 2 * first * HD
                    sp.dma_start(KL[r:r + 2 * n * HD, :, :],
                                 d_c[1, part:part + 1].rearrange("c u d h s -> c (u d) (h s)")
                                 .to_broadcast([n, 2 * HD, H * S])).then_inc(l1_in, 16)
                for e in range(2, E - 1):
                    spread(e)
                sp.wait_ge(nm_r, 1)
                sp.dma_start(d_n.rearrange("c r n -> r c n"), NMP[:, :, :]).then_inc(dn_out, 16)
                sp.wait_ge(dn_out, 16)
                sp.dma_start(QL[ROWS:ROWS + 3, :, :], d_n.rearrange("c (h t) n -> c h (t n)", h=H)).then_inc(nm_in, 16)
                spread(E - 1)
                sp.wait_ge(xo_r, 1)
                sp.dma_start(out[bass.ds(b * S, S), :].rearrange("(t p) d -> p t d", p=P), X[:, :, :]).then_inc(out_done, 16)
                sp.wait_ge(out_done, 16)
                end_sequence(sp, "sync", b)

        @block.gpsimd
        def _(pool):
            nc.gpsimd.memset(QBD[:, :, :, :], 0.0).then_inc(s_pre_pool, 1)
            nc.gpsimd.memset(VP[:, :, :, :], 0.0).then_inc(s_pre_pool, 1)
            nc.gpsimd.memset(half[:, :], -0.5).then_inc(s_pre_pool, 1)
            pool.wait_ge(s_pre_pool, 3)
            v2 = VP[:, :, :, :].rearrange("p t (a two) c -> p (t a) two c", two=2)
            for two in range(2):
                nc.gpsimd.memset(v2[:, :, two, 16 + 8 * two:24 + 8 * two], 1.0).then_inc(s_pre_pool, 1)
            pool.wait_ge(s_pre_pool, 5)
            with pool.Fori(0, B) as b:
                nc.gpsimd.memset(QEO.rearrange("p a c s -> p (a c s)").bitcast(F32), 0.0).then_inc(qeo_zero, 1)
                pool.wait_ge(var_ready, 1)
                nc.gpsimd.tensor_tensor(rs[:, :], ve[:, :], half[:, :], ALU.pow).then_inc(rstd_ready, 1)
                for u in range(T):
                    pool.wait_ge(mb_in, 16 * (u + 1))
                    for kb in range(1, T):
                        tile = region((4 * u + kb) % RING * TILE, TILE)
                        pool.wait_ge(red_done, 4 * u + kb + 1)
                        nc.gpsimd.tensor_tensor(tile, tile, MB[:, :], ALU.subtract).then_inc(sub_pool, 1)
                pool.wait_ge(var1, 1)
                nc.gpsimd.tensor_tensor(rs[:, :], ve[:, :], half[:, :], ALU.pow).then_inc(rstd1, 1)
                pool.wait_ge(xt1, 1)

                def weighted(e):
                    pool.wait_ge(wb_in[e % 2], 32 * (e // 2 + 1))
                    if e == 0:
                        pool.wait_ge(dc_out, 16)
                    if e >= 2:
                        pool.wait_ge(hu1_ps, 2 + e - 1)
                    nc.gpsimd.tensor_tensor(XS[:, e % 2, :], XT[:, :], MBE[:, e % 2, 0, :], ALU.mult).then_inc(xs_r, 1)

                def added(e):
                    pool.wait_ge(y_c, e + 1)
                    if e:
                        pool.wait_ge(y_add, e)
                    nc.gpsimd.tensor_tensor(YT[:, :], YT[:, :], CC[:, e % 2, :], ALU.add).then_inc(y_add, 1)

                weighted(0)
                weighted(1)
                for e in range(E):
                    added(e)
                    if e + 2 < E:
                        weighted(e + 2)
                end_sequence(pool, "gpsimd", b)

        @block.tensor
        def _(pe):
            mm = nc.tensor.matmul
            pe.wait_ge(s_wa, 16)
            pe.wait_ge(s_wb, 16)
            pe.wait_ge(s_wc, 16)
            pe.wait_ge(s_etl, 16 * 12)
            pe.wait_ge(s_pre_pool, 5)
            pe.wait_ge(s_pre_dve, 1)

            def transpose_tiles(done):
                for t in range(T):
                    last = nc.tensor.transpose(bank(B_MISC, P, t * P), XN[:, t, :], w("ident"))
                last.then_inc(done, 1)

            def ffn_step(s):
                e, fi = s // 2, s % 2
                a, c = (w("sw1", fi * P, P), w("sw2", fi * P, P)) if e == 0 else (
                    w("ew1", (e - 1) * F0 + fi * P, P), w("ew2", (e - 1) * F0 + fi * P, P))
                if s:
                    pe.wait_ge(hh_ready, s)
                mm(bank(B_H), a, XT[:, :], start=True, stop=True)
                mm(bank(B_U), c, XT[:, :], start=True, stop=True).then_inc(hu_ps, 1)

            def ffn_out(e):
                pe.wait_ge(hh_ready, 2 * e + 2)
                if e:
                    pe.wait_ge(fo_used, e)
                else:
                    pe.wait_ge(v_set, 1)
                for t in range(T):
                    for fi in range(2):
                        a = w("sw3", fi * D, D) if e == 0 else w("ew3", ((e - 1) * 2 + fi) * D, D)
                        last = mm(bank(B_O, P, t * P), HH[:, e % 2, fi, t * P:(t + 1) * P], a, start=fi == 0, stop=fi == 1)
                last.then_inc(fo_ps, 1)

            def ffn_one(s):
                ffn_step(s)
                if s >= 2 and s % 2 == 0:
                    ffn_out(s // 2 - 1)

            def score_tile(i):
                u, kb = i // T, i % T
                far = abs(u - kb) >= 2
                for g in range(T):
                    n = T * i + g
                    ps = bank(B_S + n % NSB)
                    q0 = u * P + g * NQ
                    if n >= NSB:
                        pe.wait_ge(sc_copied, n - NSB + 1)
                    for a in range(H // 2):
                        last = mm(ps[:, a * 2 * NQ:(a + 1) * 2 * NQ], KS[0:ROWS, int(far), a, kb * P:(kb + 1) * P],
                                  QBD[:, a, :, q0:q0 + NQ], start=a == 0, stop=far and a == H // 2 - 1,
                                  skip_group_check=True)
                    if not far:
                        v = ps.rearrange("p (h q) -> p h q", h=H)
                        for j in range(NQ // 2):
                            at = kb * P - (q0 + 2 * j) + 2 * P
                            last = mm(v[:, :, 2 * j:2 * j + 2], ET[:, at:at + P], QR[0:ROWS, :, q0 + 2 * j:q0 + 2 * j + 2],
                                      start=False, stop=j == NQ // 2 - 1, skip_group_check=True)
                    last.then_inc(sc_ps, 1)

            def max_transpose(v):
                pe.wait_ge(m1_ready, v + 1)
                if v >= 2:
                    pe.wait_ge(ss_ready, v - 1)
                nc.tensor.transpose(PS[0:H * T, B_MISC, 0:P], M1[:, :], w("ident")).then_inc(mt_ps, 1)

            def pv(v, kb):
                pe.wait_ge(p_ready, T * v + kb + 1)
                if kb == 0:
                    if v:
                        pe.wait_ge(ctx_ready, v)
                    else:
                        pe.wait_ge(logits_read, 1)
                tile = region((4 * v + kb) % RING * TILE, TILE).rearrange("p (h q) -> p h q", h=H)
                for half_ in range(2):
                    for two in range(2):
                        for j in range(4):
                            h = half_ * 8 + 2 * j + two
                            last = mm(PS[32 * j:32 * j + 32, B_PV, half_ * P:(half_ + 1) * P], VP[:, kb, h, :], tile[:, h, :],
                                      start=kb == 0 and half_ == 0 and two == 0, stop=kb == T - 1, skip_group_check=True)
                last.then_inc(pv_done, 1)

            def align(v):
                pe.wait_ge(ctx_ready, v + 1)
                if v < T - 1:
                    pe.wait_ge(m2_ready, v + 2)
                else:
                    pe.wait_ge(ss_ready, v)
                mm(bank(B_MISC, 2 * P), w("seld"), CTX[:, :], start=True, stop=True).then_inc(al_ps, 1)

            def attn_out(v):
                pe.wait_ge(cn_ready, v + 1)
                o = bank(B_MISC, P)
                mm(o, CN[:, 0:P], w("WoP", 0, D), start=True, stop=False)
                mm(o, CN[:, P:2 * P], w("WoP", D, D), start=False, stop=False)
                mm(o, G[:, v * P:(v + 1) * P], w("WoT"), start=False, stop=True).then_inc(at_ps, 1)

            def ffn1_shared(s):
                if s:
                    pe.wait_ge(h1_r, s)
                else:
                    pe.wait_ge(z_sb, 1)
                mm(bank(B_H), w("tsw1", s * P, P), XT[:, :], start=True, stop=True)
                mm(bank(B_U), w("tsw2", s * P, P), XT[:, :], start=True, stop=True).then_inc(hu1_ps, 1)

            def ffn1_shared_out():
                pe.wait_ge(h1_r, 2)
                pe.wait_ge(v_set1, 1)
                mm(bank(B_O), w("tsw3", 0, D), HH[:, 0, 0, :], start=True, stop=False)
                mm(bank(B_O), w("tsw3", D, D), HH[:, 0, 1, :], start=False, stop=True).then_inc(fo1_ps, 1)

            def expert1_in(e):
                pe.wait_ge(xs_r, e + 1)
                pe.wait_ge(h1_r, 2 + 2 * e)
                mm(bank(B_H), w("tw1", e * HID, HID), XS[:, e % 2, :], start=True, stop=True)
                mm(bank(B_U), w("tw3", e * HID, HID), XS[:, e % 2, :], start=True, stop=True).then_inc(hu1_ps, 1)

            def expert1_out(e):
                pe.wait_ge(h1_r, 2 + 2 * e + 2)
                pe.wait_ge(y_c, e) if e else pe.wait_ge(yn_r, 1)
                mm(bank(B_O), w("tw2", e * D, D), HE, start=True, stop=True).then_inc(fo1_ps, 1)

            def s1_bank(n, tile, heads):
                if n >= NSB:
                    pe.wait_ge(s1_max, n - NSB + 1)
                width = (tile + 1) * P
                ps = bank(B_S + n % NSB)
                for a, h in enumerate(heads):
                    o = ps[:, a * width:(a + 1) * width]
                    mm(o, QL[0:ROWS, h, tile * P:(tile + 1) * P], KL[0:ROWS, h, 0:width], start=a == 0, stop=False,
                       skip_group_check=True)
                    last = mm(o[:, tile * P:width], IDB[:, :], MKN[:, :], start=False, stop=True, skip_group_check=True)
                last.then_inc(s1_ps, 1)

            def s2_banks(n, h):
                for c, kbs in enumerate(((0,), (1,), (2, 3))):
                    i = 3 * n + c
                    if i >= NSB:
                        pe.wait_ge(p1_r, i - NSB + 1)
                    at = 0
                    for kb in kbs:
                        width = S - kb * P
                        o = bank(B_S + c, width, at)
                        mm(o, KL[0:ROWS + 3, h, kb * P:(kb + 1) * P], QL[0:ROWS + 3, h, kb * P:S], start=at == 0, stop=False,
                           skip_group_check=True)
                        last = mm(o[:, 0:P], IDB[:, :], MKT[:, :], start=False, stop=True, skip_group_check=True)
                        at += width
                    last.then_inc(s2_ps, 1)

            def pv1_group(gq):
                half_, two = gq // 2, gq % 2
                pe.wait_ge(p1_r, 12 * (gq + 1))
                if gq == 2:
                    pe.wait_ge(ctx1, 1)
                if gq == 0:
                    pe.wait_ge(lg_read1, 1)
                for kb in range(T):
                    for j in range(4):
                        h = half_ * 8 + 2 * j + two
                        last = mm(PS[32 * j:32 * j + 32, B_PV, kb * P:S], VP[:, kb, h, :],
                                  PL[:, gq % 2, j, PCOL[kb]:PCOL[kb] + S - kb * P],
                                  start=two == 0 and kb == 0, stop=two == 1 and kb == T - 1, skip_group_check=True)
                last.then_inc(pv1, 1)

            with pe.Fori(0, B) as b:
                pe.wait_ge(xn_ready, 1)
                transpose_tiles(xt_ps)
                pe.wait_ge(xt_ready, 1)
                mm(bank(B_H), w("WqT"), XT[:, :], start=True, stop=True).then_inc(proj_q, 1)
                mm(bank(B_U), w("WkT"), XT[:, :], start=True, stop=True).then_inc(proj_k, 1)
                for t in range(T):
                    last = mm(bank(B_O, P, t * P), XT[:, t * P:(t + 1) * P], w("WvT"), start=True, stop=True)
                last.then_inc(proj_v, 1)
                for t in range(T):
                    last = mm(bank(B_PV, E, t * E), XT[:, t * P:(t + 1) * P], w("gate0"), start=True, stop=True)
                last.then_inc(logit_ps, 1)
                pe.wait_ge(qk_sb, 2)
                ffn_one(0)
                ffn_one(1)
                pe.wait_ge(sg_ready, 1)
                mm(bank(B_S), w("Mbd"), SG, start=True, stop=True)
                mm(bank(B_S + 1), w("Zbd"), SG, start=True, stop=True).then_inc(glob_ps, 1)
                for s in range(2, FFN_BEFORE):
                    ffn_one(s)
                pe.wait_ge(g_ready, 1)
                pe.wait_ge(qk_in, 16 * (6 + 4))
                pe.wait_ge(rel_in, 16 * 6)
                for i in range(NSLOT0):
                    if i < T * T:
                        score_tile(i)
                    for v in range(T):
                        if i == T * v + AT_MAX:
                            max_transpose(v)
                        if 0 <= i - T * v - AT_PV < T:
                            pv(v, i - T * v - AT_PV)
                    if i in FFN_AT:
                        ffn_one(FFN_AT[i])
                    for v in range(T):
                        if i == T * v + AT_ALIGN:
                            align(v)
                        if i == T * v + AT_OUT:
                            attn_out(v)
                ffn_out(E)

                pe.wait_ge(xn1, 1)
                transpose_tiles(xt_ps1)
                pe.wait_ge(xt1, 1)
                mm(bank(B_H), w("Wqa"), XT[:, :], start=True, stop=True)
                mm(bank(B_U), w("Wka"), XT[:, :], start=True, stop=True).then_inc(amp_ps, 1)
                mm(bank(B_S), w("Wqp"), XT[:, :], start=True, stop=True)
                mm(bank(B_S + 1), w("Wkp"), XT[:, :], start=True, stop=True).then_inc(phi_ps, 1)
                for t in range(T):
                    last = mm(bank(B_PV, E, t * E), XT[:, t * P:(t + 1) * P], w("gate1"), start=True, stop=True)
                last.then_inc(lg_ps1, 1)
                for t in range(T):
                    last = mm(bank(B_O, P, t * P), XT[:, t * P:(t + 1) * P], w("Wv1"), start=True, stop=True)
                last.then_inc(v_ps1, 1)
                ffn1_shared(0)
                ffn1_shared(1)
                pe.wait_ge(wm_r, 1)
                for t in range(T):
                    last = nc.tensor.transpose(PS[0:2 * E, B_MISC, t * P:(t + 1) * P], WMK[:, t, :], w("ident"))
                last.then_inc(wt_ps, 1)
                ffn1_shared_out()
                pe.wait_ge(tp_sb, 1)
                pe.wait_ge(sq_r, 1)
                for a in range(2):
                    last = mm(bank(B_S + a), w("mean8"), SQ[:, a * S:(a + 1) * S], start=True, stop=True)
                last.then_inc(msq_ps, 1)
                expert1_in(0)
                expert1_out(0)
                expert1_in(1)
                expert1_out(1)
                pe.wait_ge(rt_r, 1)
                pe.wait_ge(l1_in, 16 * 6)
                n = 0
                for tile in range(T):
                    per = (4, 2, 1, 1)[tile]
                    for h0 in range(0, H, per):
                        s1_bank(n, tile, range(h0, h0 + per))
                        n += 1
                        if n % 11 == 5:
                            expert1_in(2 + n // 11)
                        if n % 11 == 9:
                            expert1_out(2 + n // 11)
                pe.wait_ge(s1_max, n)
                pe.wait_ge(wt_r, 1)
                nc.tensor.transpose(PS[0:H * T, B_MISC, 0:P], M1[:, :], w("ident")).then_inc(nmt_ps, 1)
                expert1_in(6)
                expert1_out(6)
                pe.wait_ge(nm_in, 16)
                for gq in range(4):
                    half_, two = gq // 2, gq % 2
                    for j in range(4):
                        s2_banks(4 * gq + j, half_ * 8 + 2 * j + two)
                    if gq == 0:
                        expert1_in(7)
                    if gq:
                        pv1_group(gq - 1)
                    if gq == 1:
                        expert1_out(7)
                pv1_group(3)
                for a in range(2):
                    pe.wait_ge(ctx1, a + 1)
                    mm(bank(B_MISC) if a == 0 else bank(B_H), w("seld"), CT1[:, a, :], start=True, stop=True).then_inc(al1_ps, 1)
                pe.wait_ge(y_add, E)
                pe.wait_ge(y_c, E)
                for t in range(T):
                    last = nc.tensor.transpose(bank(B_O, P, t * P), YT[:, t * P:(t + 1) * P], w("ident"))
                last.then_inc(yt_ps, 1)
                pe.wait_ge(cn1, 2)
                for t in range(T):
                    for a in range(2):
                        last = mm(bank(B_U, P, t * P), CN1[:, a, t * P:(t + 1) * P], w("WoP1", a * D, D), start=a == 0, stop=a == 1)
                last.then_inc(at1_ps, 1)
                end_sequence(pe, "tensor", b)

        @block.scalar
        def _(act):
            A = nc.scalar.activation
            act.wait_ge(s_wa, 16)
            A(gate_e, w("alpha"), ACT.Exp, scale=-1.0).then_inc(s_gexp, 1)
            A(esl, w("sls"), ACT.Exp).then_inc(s_gexp, 1)

            def ffn_tanh(s):
                act.wait_ge(hu_ps, s + 1)
                if s:
                    act.wait_ge(hh_ready, s)
                A(TH[:, :], bank(B_H), ACT.Tanh, scale=0.5).then_inc(th_ready, 1)

            def exp_tile(v, kb):
                if kb == 0:
                    act.wait_ge(sub_dve, v + 1)
                else:
                    act.wait_ge(sub_pool, 3 * v + kb)
                tile = region((4 * v + kb) % RING * TILE, TILE)
                A(tile, tile, ACT.Exp, scale=1.0 / sqrt(HD)).then_inc(p_ready, 1)

            with act.Fori(0, B) as b:
                act.wait_ge(proj_q, 1)
                A(F3[:, 0, :], bank(B_H), ACT.Identity, bias=w("bq")).then_inc(qk_sb, 1)
                act.wait_ge(proj_k, 1)
                A(F3[:, 1, :], bank(B_U), ACT.Identity, bias=w("bk")).then_inc(qk_sb, 1)
                act.wait_ge(qmin_ready, 1)
                A(QEX, QMIN, ACT.Exp).then_inc(qexp_ready, 1)
                ffn_tanh(0)
                act.wait_ge(parts_ready, 1)
                act.wait_ge(qeo_zero, 1)
                for a in range(2):
                    last = A(QEO[:, a, :, a::2], PARTS[:, 0, :, a::2], ACT.Copy)
                last.then_inc(qeo_ready, 1)
                ffn_tanh(1)
                ffn_tanh(2)
                act.wait_ge(rdm_ready, 1)
                A(e2[:, :], dm[:, :], ACT.Exp).then_inc(rexp_ready, 1)
                for s in range(3, FFN_BEFORE):
                    ffn_tanh(s)
                for i in range(NSLOT0):
                    if i < T * T:
                        tile = region(i % RING * TILE, TILE).rearrange("p (h q) -> p h q", h=H)
                        if i >= RING:
                            act.wait_ge(pv_done, i - RING + 1)
                        for g in range(T):
                            n = T * i + g
                            act.wait_ge(sc_ps, n + 1)
                            A(tile[:, :, g * NQ:(g + 1) * NQ], bank(B_S + n % NSB).rearrange("p (h q) -> p h q", h=H),
                              ACT.Copy).then_inc(sc_copied, 1)
                    for v in range(T):
                        if 0 <= i - T * v - AT_SUB < T:
                            exp_tile(v, i - T * v - AT_SUB)
                        if i == T * v + AT_EVAC:
                            act.wait_ge(pv_done, T * v + T)
                            if v:
                                act.wait_ge(cn_ready, v)
                            A(CTX[:, :], bank(B_PV, 2 * P), ACT.Copy).then_inc(ctx_ready, 1)
                    if i in FFN_AT:
                        ffn_tanh(FFN_AT[i])
                act.wait_ge(fo_used, E + 1)
                A(TH[:, :], ACC[:, :, :].rearrange("p t d -> p (t d)"), ACT.Tanh, scale=0.5).then_inc(ga_ready, 1)

                act.wait_ge(amp_ps, 1)
                A(Z.rearrange("p (a s) -> p a s", a=2), PS[:, B_H:B_H + 2, :], ACT.Copy).then_inc(z_sb, 1)
                act.wait_ge(phi_ps, 1)
                A(TP.rearrange("p (a s) -> p a s", a=2), PS[:, B_S:B_S + 2, :], ACT.Tanh).then_inc(tp_sb, 1)
                act.wait_ge(nab_r, 1)
                A(EX, NAB, ACT.Exp).then_inc(ex_r, 1)
                act.wait_ge(lge_r, 1)
                A(EQ[:, :, :], KEY[:, :, :], ACT.Exp).then_inc(lgx_r, 1)

                def tanh1(s, bias=None):
                    act.wait_ge(hu1_ps, s + 1)
                    if s >= 1:
                        act.wait_ge(h1_r, s if s < 3 else 2 + 2 * (s - 2))
                    A(TH[:, :], bank(B_H), ACT.Tanh, scale=0.5, **({} if bias is None else {"bias": bias})).then_inc(th1_r, 1)

                tanh1(0)
                tanh1(1)
                act.wait_ge(u_r, 1)
                A(LNU, U1, ACT.Ln).then_inc(ln_r, 1)
                act.wait_ge(amp_r, 1)
                A(SQ, EX, ACT.Square).then_inc(sq_r, 1)
                act.wait_ge(msq_ps, 1)
                A(RT.rearrange("p (a s) -> p a s", a=2), PS[:, B_S:B_S + 2, :], ACT.Sqrt, bias=cols[:, 6:7]).then_inc(rt_r, 1)
                act.wait_ge(abs_r, 1)
                A(U1, TP, ACT.Sin, scale=pi).then_inc(cos_r, 1)
                A(C1, NAB, ACT.Sin, scale=-pi, bias=w("halfpi")).then_inc(cos_r, 1)
                for e in range(2):
                    tanh1(2 + e, hb1[:, e:e + 1])
                for e in range(2, 6):
                    tanh1(2 + e, hb1[:, e:e + 1])
                tanh1(2 + 6, hb1[:, 6:7])

                def exp1(n):
                    for c, (at, width) in enumerate(((0, 512), (512, 384), (896, 384))):
                        act.wait_ge(s2_ps, 3 * n + c + 1)
                        if n >= 8 and c == 0:
                            act.wait_ge(pv1, n // 4 - 1)
                        A(PL[:, n // 4 % 2, n % 4, at:at + width], bank(B_S + c, width), ACT.Exp).then_inc(p1_r, 1)

                for gq in range(4):
                    for j in range(4):
                        exp1(4 * gq + j)
                    if gq == 0:
                        tanh1(2 + 7, hb1[:, 7:8])
                    if gq == 2:
                        act.wait_ge(pv1, 2)
                        A(CT1[:, 0, :], bank(B_PV), ACT.Copy).then_inc(ctx1, 1)
                act.wait_ge(pv1, 4)
                A(CT1[:, 1, :], bank(B_PV), ACT.Copy).then_inc(ctx1, 1)
                act.wait_ge(yt_ps, 1)
                act.wait_ge(h1_r, 2 + 2 * E)
                A(TH[:, :], bank(B_O), ACT.Tanh, scale=0.5).then_inc(ga1, 1)
                end_sequence(act, "scalar", b)

        @block.vector
        def _(dve):
            V = nc.vector
            steps = [0]

            def link(ins):
                steps[0] += 1
                ins.then_inc(chain_dve, 1)
                dve.wait_ge(chain_dve, steps[0])

            dve.wait_ge(s_wa, 16)
            dve.wait_ge(s_gexp, 2)
            link(V.tensor_scalar(gate_s, gate_e, 1.0, None, ALU.add))
            link(V.reciprocal(gate, gate_s))
            V.tensor_scalar(omg, gate, -1.0, 1.0, ALU.mult, ALU.add)
            V.tensor_scalar(gbv, w("bv"), gate, None, ALU.mult)
            V.tensor_scalar(esl, esl, 1.0 / sqrt(HD), None, ALU.mult)
            V.memset(cols[:, 6:7], 1e-6)
            V.memset(KS[ROWS:P, :, :, :], 1.0)
            V.tensor_scalar(hb1[:, :], w("b1"), 0.5, None, ALU.mult)
            V.tensor_copy(IDB[:, :], w("ident"))
            V.tensor_copy(MKN[:, :], w("maskn"))
            link(V.tensor_copy(MKT[:, :], w("maskt")))
            dve.wait_ge(s_et, 16)
            ep = HH[0:2 * HD, 0, :, :].rearrange("p a s -> p (a s)").bitcast(BF16)[:, 0:3 * S].rearrange("p (c s) -> p c s", c=3)
            e_f, e_r = TH[0:2 * HD, :], AA[0:2 * HD, :]
            link(V.tensor_copy(ep[:, 0, :], e_f))
            link(V.tensor_tensor(e_r, e_f, ep[:, 0, :], ALU.subtract))
            link(V.tensor_copy(ep[:, 1, :], e_r))
            V.tensor_tensor(ep[:, 2, :], e_r, ep[:, 1, :], ALU.subtract).then_inc(s_etp, 1)
            dve.wait_ge(s_etp, 1)
            dve.wait_ge(s_etd, 16)
            V.engine_nop().then_inc(s_pre_dve, 1)
            dve.wait_ge(s_pre_dve, 1)
            dve.wait_ge(s_pre_pool, 5)
            pre = steps[0]
            dve.nop(nofuse=True)
            dve.sem_clear(chain_dve)
            steps[0] = 0

            def norm_stats(done):
                for t in range(T):
                    last = V.bn_stats(st[:, t, :], X[:, t, :])
                link(last)
                for t in range(T):
                    last = V.bn_aggr(mv[:, t, :], st[:, t, :])
                link(last)
                V.tensor_scalar(ve[:, :], mv[:, :, 1], LN_EPS, None, ALU.add).then_inc(done, 1)

            def norm_apply(rstd, done):
                dve.wait_ge(rstd, 1)
                for t in range(T):
                    last = V.tensor_scalar(XN[:, t, :], X[:, t, :], mv[:, t, 0:1], rs[:, t:t + 1], ALU.subtract, ALU.mult)
                last.then_inc(done, 1)

            def set_v(ready, done):
                dve.wait_ge(ready, 1)
                v = bank(B_O).rearrange("p (a two d) -> p a two d", two=2, d=HD)
                o = VP[:, :, :, :].rearrange("p t (a two) c -> p (t a) two c", two=2)
                for two in range(2):
                    last = V.tensor_copy(o[:, :, two, 8 * two:8 * two + 8], v[:, :, two, :])
                last.then_inc(done, 1)

            def over(v):
                return v[:, :, None].to_broadcast([P, T, E])

            idx = w("idx")[:, None, :].to_broadcast([P, T, E])

            def first_max(a, m, oh):
                link(V.tensor_reduce(m, a, AX.X, ALU.max))
                link(V.tensor_tensor(KEY[:, :, :], a, over(m), ALU.is_equal))
                link(V.tensor_tensor(KEY[:, :, :], KEY[:, :, :], idx, ALU.mult))
                link(V.tensor_reduce(km[:, :], KEY[:, :, :], AX.X, ALU.max))
                link(V.tensor_tensor(oh, KEY[:, :, :], over(km), ALU.is_equal))

            def without(a, oh):
                link(V.scalar_tensor_tensor(out=a, in0=oh, scalar=-3e38, in1=a, op0=ALU.mult, op1=ALU.add))

            def split(full, rest, parts):
                link(V.tensor_copy(parts[0], full))
                link(V.tensor_tensor(rest, full, parts[0], ALU.subtract))
                link(V.tensor_copy(parts[1], rest))
                return V.tensor_tensor(parts[2], rest, parts[1], ALU.subtract)

            def ffn_hh(s):
                e, fi = s // 2, s % 2
                dve.wait_ge(th_ready, s + 1)
                link(V.scalar_tensor_tensor(out=AA[:, :], in0=TH[:, :], scalar=1.0, in1=bank(B_H), op0=ALU.add, op1=ALU.mult))
                if e >= 2:
                    dve.wait_ge(fo_ps, e - 1)
                V.tensor_tensor(HH[:, e % 2, fi, :], AA[:, :], bank(B_U), ALU.mult).then_inc(hh_ready, 1)
                dve.wait_ge(hh_ready, s + 1)

            def ffn_acc(e):
                dve.wait_ge(fo_ps, e + 1)
                if e == 0:
                    link(V.tensor_scalar(ACC[:, :, :].rearrange("p t d -> p (t d)"), bank(B_O), 0.5, None, ALU.mult))
                else:
                    for t in range(T):
                        last = V.scalar_tensor_tensor(out=ACC[:, t, :], in0=bank(B_O, P, t * P), scalar=W8[:, t, e - 1:e],
                                                      in1=ACC[:, t, :], op0=ALU.mult, op1=ALU.add)
                    link(last)
                V.engine_nop().then_inc(fo_used, 1)

            def ffn_dve(s):
                ffn_hh(s)
                if s >= 2 and s % 2 == 0:
                    ffn_acc(s // 2 - 1)

            def silu_mix(th_done, f, s_attn, done):
                dve.wait_ge(th_done, 1)
                link(V.scalar_tensor_tensor(out=AA[:, :], in0=TH[:, :], scalar=1.0, in1=f, op0=ALU.add, op1=ALU.mult))
                link(V.tensor_tensor(AA[:, :], AA[:, :], s_attn, ALU.mult))
                xf = X[:, :, :].rearrange("p t d -> p (t d)")
                return V.scalar_tensor_tensor(out=xf, in0=AA[:, :], scalar=0.5, in1=xf, op0=ALU.mult, op1=ALU.add)

            with dve.Fori(0, B) as b:
                steps[0] = 0
                dve.wait_ge(x_in, 16)
                norm_stats(var_ready)
                norm_apply(rstd_ready, xn_ready)
                dve.wait_ge(xt_ps, 1)
                V.tensor_copy(XT[:, :], bank(B_MISC)).then_inc(xt_ready, 1)
                dve.wait_ge(qk_sb, 2)
                V.tensor_scalar(QMIN, F3[:, 0, :], 0.0, None, ALU.min).then_inc(qmin_ready, 1)
                V.tensor_scalar(F3[:, 2, 0:S // 2], F3[:, 1, 0:S // 2], w("e_near"), None, ALU.add)
                link(V.tensor_scalar(F3[:, 2, S // 2:S], F3[:, 1, S // 2:S], w("e_far"), None, ALU.add))
                split(F3, R3, [PARTS[:, :, c, :] for c in range(3)]).then_inc(parts_ready, 1)
                set_v(proj_v, v_set)
                ffn_dve(0)
                dve.wait_ge(qexp_ready, 1)
                V.scalar_tensor_tensor(out=SG, in0=F3[:, 0, :], scalar=0.0, in1=QEX, op0=ALU.max, op1=ALU.add).then_inc(sg_ready, 1)
                ffn_dve(1)
                dve.wait_ge(logit_ps, 1)
                V.tensor_copy(LG[:, :, :], bank(B_PV, T * E).rearrange("p (t e) -> p t e", e=E)).then_inc(logits_read, 1)
                dve.wait_ge(logits_read, 1)
                first_max(LG[:, :, :], m1[:, :], OH1[:, :, :])
                without(LG[:, :, :], OH1[:, :, :])
                first_max(LG[:, :, :], m2[:, :], OH2[:, :, :])
                V.tensor_tensor(dm[:, :], m2[:, :], m1[:, :], ALU.subtract).then_inc(rdm_ready, 1)
                ffn_dve(2)
                dve.wait_ge(rexp_ready, 1)
                link(V.tensor_scalar(w1[:, :], e2[:, :], 1.0, 2.0, ALU.add, ALU.mult))
                link(V.reciprocal(w1[:, :], w1[:, :]))
                link(V.tensor_tensor(w2[:, :], w1[:, :], e2[:, :], ALU.mult))
                link(V.tensor_tensor(OH1[:, :, :], OH1[:, :, :], over(w1), ALU.mult))
                link(V.tensor_tensor(OH2[:, :, :], OH2[:, :, :], over(w2), ALU.mult))
                link(V.tensor_tensor(W8[:, :, :], OH1[:, :, :], OH2[:, :, :], ALU.add))
                dve.wait_ge(glob_ps, 1)
                link(V.tensor_scalar(DEN, bank(B_S + 1), 1e-6, None, ALU.add))
                link(V.reciprocal(RDEN, DEN))
                link(V.tensor_tensor(G[:, :], RDEN, bank(B_S), ALU.mult))
                V.tensor_scalar(G[:, :], G[:, :], omg, gbv, ALU.mult, ALU.add).then_inc(g_ready, 1)
                for s in range(3, FFN_BEFORE):
                    ffn_dve(s)
                for i in range(NSLOT0):
                    if i < T * T:
                        u, kb = i // T, i % T
                        tile = region(i % RING * TILE, TILE)
                        dve.wait_ge(sc_copied, T * (i + 1))
                        if kb == 0 and u:
                            dve.wait_ge(m1_ready, u)
                        V.tensor_reduce(R1[:, kb, :], tile.rearrange("p (a c) -> p a c", c=32), AX.X, ALU.max,
                                        apply_transpose=True).then_inc(red_done, 1)
                        if kb == T - 1:
                            dve.wait_ge(red_done, i + 1)
                            if u:
                                dve.wait_ge(mt_ps, u)
                            V.tensor_reduce(M1[:, :], R1[:, :, :].rearrange("p k c -> p c k"), AX.X, ALU.max).then_inc(m1_ready, 1)
                    for v in range(T):
                        if i == T * v + AT_MAX:
                            dve.wait_ge(mt_ps, v + 1)
                            if v:
                                dve.wait_ge(dm_out, 16 * v)
                            V.tensor_reduce(M2[:, :], PS[0:H * T, B_MISC, 0:P].rearrange("c (a i) -> c i a", i=NQ),
                                            AX.X, ALU.max).then_inc(m2_ready, 1)
                        if i == T * v + AT_SUB:
                            tile = region(4 * v % RING * TILE, TILE)
                            dve.wait_ge(mb_in, 16 * (v + 1))
                            V.tensor_tensor(tile, tile, MB[:, :], ALU.subtract).then_inc(sub_dve, 1)
                    if i in FFN_AT:
                        ffn_dve(FFN_AT[i])
                    for v in range(T):
                        if i == T * v + AT_ALIGN:
                            dve.wait_ge(al_ps, v + 1)
                            link(V.reciprocal(RDN[:, :], bank(B_MISC, 2 * P)))
                            if v:
                                dve.wait_ge(at_ps, v)
                            V.scalar_tensor_tensor(out=CN[:, :], in0=CTX[:, :], scalar=gate, in1=RDN[:, :],
                                                   op0=ALU.mult, op1=ALU.mult).then_inc(cn_ready, 1)
                        if i == T * v + AT_OUT:
                            dve.wait_ge(at_ps, v + 1)
                            V.tensor_tensor(SS[:, v, :], bank(B_MISC, P), w("bo"), ALU.add).then_inc(ss_ready, 1)
                ffn_acc(E)
                dve.wait_ge(ss_ready, T)
                link(silu_mix(ga_ready, ACC[:, :, :].rearrange("p t d -> p (t d)"), SS[:, :, :].rearrange("p t d -> p (t d)"), None))

                norm_stats(var1)
                norm_apply(rstd1, xn1)
                dve.wait_ge(xt_ps1, 1)
                V.tensor_copy(XT[:, :], bank(B_MISC)).then_inc(xt1, 1)
                dve.wait_ge(z_sb, 1)
                V.scalar_tensor_tensor(out=NAB, in0=Z, scalar=-1.0, in1=Z, op0=ALU.mult, op1=ALU.min).then_inc(nab_r, 1)
                dve.wait_ge(lg_ps1, 1)
                V.tensor_copy(LG[:, :, :], bank(B_PV, T * E).rearrange("p (t e) -> p t e", e=E)).then_inc(lg_read1, 1)
                dve.wait_ge(lg_read1, 1)
                link(V.tensor_reduce(m1[:, :], LG[:, :, :], AX.X, ALU.max))
                V.tensor_tensor(KEY[:, :, :], LG[:, :, :], over(m1), ALU.subtract).then_inc(lge_r, 1)
                dve.wait_ge(ex_r, 1)
                link(V.tensor_scalar(U1, EX, 1.0, None, ALU.add))
                V.tensor_scalar(C1, U1, -1.0, None, ALU.add).then_inc(u_r, 1)
                dve.wait_ge(u_r, 1)
                link(V.tensor_tensor(C1, EX, C1, ALU.subtract))
                dve.wait_ge(lgx_r, 1)
                link(V.tensor_reduce(m2[:, :], EQ[:, :, :], AX.X, ALU.add))
                link(V.reciprocal(m2[:, :], m2[:, :]))
                link(V.tensor_tensor(LG[:, :, :], EQ[:, :, :], over(m2), ALU.mult))
                link(V.tensor_copy(WM[:, :, :], LG[:, :, :]))
                first_max(LG[:, :, :], m1[:, :], OH1[:, :, :])
                without(LG[:, :, :], OH1[:, :, :])
                first_max(LG[:, :, :], m2[:, :], OH2[:, :, :])
                link(V.tensor_tensor(WMK[:, :, E:2 * E], OH1[:, :, :], OH2[:, :, :], ALU.add))
                V.tensor_tensor(WMK[:, :, 0:E], WM[:, :, :], WMK[:, :, E:2 * E], ALU.mult).then_inc(wm_r, 1)
                set_v(v_ps1, v_set1)

                def shared_hh(s):
                    dve.wait_ge(th1_r, s + 1)
                    link(V.scalar_tensor_tensor(out=AA[:, :], in0=TH[:, :], scalar=1.0, in1=bank(B_H), op0=ALU.add, op1=ALU.mult))
                    link(V.tensor_scalar(AA[:, :], AA[:, :], 0.5, None, ALU.mult))
                    V.tensor_tensor(HH[:, 0, s, :], AA[:, :], bank(B_U), ALU.mult).then_inc(h1_r, 1)
                    dve.wait_ge(h1_r, s + 1)

                shared_hh(0)
                dve.wait_ge(wt_ps, 1)
                V.tensor_copy(WT[:, :], PS[0:2 * E, B_MISC, :]).then_inc(wt_r, 1)
                shared_hh(1)
                dve.wait_ge(ln_r, 1)
                link(V.tensor_tensor(C1, C1, LNU, ALU.add))
                link(V.scalar_tensor_tensor(out=C1, in0=Z, scalar=0.0, in1=C1, op0=ALU.max, op1=ALU.add))
                V.tensor_copy(EX, C1).then_inc(amp_r, 1)
                dve.wait_ge(amp_r, 1)
                V.scalar_tensor_tensor(out=NAB, in0=TP, scalar=-1.0, in1=TP, op0=ALU.mult, op1=ALU.max).then_inc(abs_r, 1)
                dve.wait_ge(fo1_ps, 1)
                V.tensor_copy(YT[:, :], bank(B_O)).then_inc(yn_r, 1)
                dve.wait_ge(rt_r, 1)
                link(V.reciprocal(SQ, RT))
                link(V.tensor_tensor(EX, EX, SQ, ALU.mult))
                link(V.tensor_scalar(EX[:, 0:S], EX[:, 0:S], esl, None, ALU.mult))
                dve.wait_ge(cos_r, 2)
                ex2 = EX.rearrange("p (t s) -> p t s", t=2)
                V.tensor_tensor(CS4[:, :, 0, :], ex2, C1.rearrange("p (t s) -> p t s", t=2), ALU.mult)
                link(V.tensor_tensor(CS4[:, :, 1, :], ex2, U1.rearrange("p (t s) -> p t s", t=2), ALU.mult))
                for t in range(2):
                    last = split(CS4[:, t, :, :], R4[:, t, :, :], [PARTS1[:, t, c, :, :] for c in range(3)])
                    if t == 0:
                        link(last)
                last.then_inc(parts1, 1)

                def expert_h(e):
                    dve.wait_ge(th1_r, 3 + e)
                    link(V.tensor_scalar(AA[:, :], TH[:, :], 0.5, 0.5, ALU.mult, ALU.add))
                    if e:
                        dve.wait_ge(fo1_ps, e + 1)
                    V.scalar_tensor_tensor(out=HE, in0=bank(B_H), scalar=w("b1", e, 1), in1=AA[:, :],
                                           op0=ALU.add, op1=ALU.mult).then_inc(h1_r, 1)
                    V.scalar_tensor_tensor(out=C3, in0=bank(B_U), scalar=w("b3", e, 1), in1=MBE[:, e % 2, 1, :],
                                           op0=ALU.add, op1=ALU.mult).then_inc(h1_r, 1)
                    dve.wait_ge(h1_r, 2 + 2 * e + 2)

                def expert_y(e):
                    dve.wait_ge(fo1_ps, e + 2)
                    if e >= 2:
                        dve.wait_ge(y_add, e - 1)
                    V.scalar_tensor_tensor(out=CC[:, e % 2, :], in0=bank(B_O), scalar=w("b2", e, 1), in1=C3,
                                           op0=ALU.add, op1=ALU.mult).then_inc(y_c, 1)
                    dve.wait_ge(y_c, e + 1)

                for e in range(2):
                    expert_h(e)
                    expert_y(e)
                n = 0
                for tile in range(T):
                    per = (4, 2, 1, 1)[tile]
                    for h0 in range(0, H, per):
                        width = (tile + 1) * P
                        dve.wait_ge(s1_ps, n + 1)
                        V.tensor_reduce(M1[:, :].rearrange("p (h t) -> p h t", t=T)[:, h0:h0 + per, tile],
                                        bank(B_S + n % NSB, per * width).rearrange("p (a k) -> p a k", k=width),
                                        AX.X, ALU.max).then_inc(s1_max, 1)
                        n += 1
                        if n % 11 == 5:
                            expert_h(2 + n // 11)
                        if n % 11 == 9:
                            expert_y(2 + n // 11)
                dve.wait_ge(nmt_ps, 1)
                link(V.tensor_scalar(NM[:, :], PS[0:H * T, B_MISC, 0:P], -1.0, None, ALU.mult))
                split(NM[:, :], NR[:, :], [NMP[:, c, :] for c in range(3)]).then_inc(nm_r, 1)
                expert_h(6)
                expert_y(6)
                expert_h(7)
                expert_y(7)
                for a in range(2):
                    dve.wait_ge(al1_ps, a + 1)
                    link(V.reciprocal(RD1[:, a, :], bank(B_MISC) if a == 0 else bank(B_H)))
                    V.tensor_tensor(CN1[:, a, :], CT1[:, a, :], RD1[:, a, :], ALU.mult).then_inc(cn1, 1)
                dve.wait_ge(ga1, 1)
                dve.wait_ge(at1_ps, 1)
                link(V.scalar_tensor_tensor(out=AA[:, :], in0=TH[:, :], scalar=1.0, in1=bank(B_O), op0=ALU.add, op1=ALU.mult))
                link(V.tensor_tensor(AA[:, :], AA[:, :], bank(B_U), ALU.mult))
                xf = X[:, :, :].rearrange("p t d -> p (t d)")
                V.scalar_tensor_tensor(out=xf, in0=AA[:, :], scalar=0.5, in1=xf, op0=ALU.mult, op1=ALU.add).then_inc(xo_r, 1)
                dve.wait_ge(xo_r, 1)
                end_sequence(dve, "vector", b, chain_dve)


def kernel(**inputs):
    import concourse.bacc as bacc
    from concourse.bass_utils import run_bass_kernel_spmd as run

    g = {k: np.asarray(v) for k, v in inputs.items()}

    def col(v):
        return np.asarray(v).reshape(P, 1)

    by_dim = np.arange(D).reshape(H, HD).T.ravel()

    def a0(n):
        return g["L0_attn_" + n]

    def f0(n):
        return g["L0_ffn_" + n]

    def a1(n):
        return g["L1_attn_" + n]

    def f1(n):
        return g["L1_ffn_" + n]

    zero = np.zeros((), np.float32)
    mbd = np.zeros((P, P), np.float32)
    zbd = np.zeros((P, P), np.float32)
    for h in range(H):
        r = slice(h * HD, h * HD + HD)
        mbd[r, r] = a0("M")[h]
        zbd[r, r] = np.repeat(a0("z")[h][:, None], HD, 1)

    def padded(wo):
        p = np.zeros((P, 2, D), np.float32)
        for h in range(H):
            r = 32 * (h % 8 // 2) + 8 * (h % 2)
            p[r:r + HD, h // 8] = wo.T[h * HD:h * HD + HD]
        return p.reshape(P, 2 * D)

    seld = np.zeros((P, P), np.float32)
    for j in range(4):
        for c in range(16):
            seld[32 * j + 16 + c, 32 * j + c] = 1
            seld[32 * j + 16 + c, 32 * j + 16 + c] = 1
    mean8 = np.kron(np.full((HD, HD), 1 / HD), np.eye(H)).astype(np.float32)
    maskn = np.triu(np.full((P, P), NEG, np.float32), 1)

    def rows(v):
        return np.broadcast_to(v[None, :], (P, v.shape[0]))

    def two(v):
        return v.reshape(2, P, -1).transpose(1, 0, 2).reshape(P, -1)

    rel = a0("rel_emb")
    parts = {
        "WqT": a0("Wq").T[:, by_dim], "WkT": a0("Wk").T[:, by_dim], "WvT": a0("Wv").T, "gate0": f0("gate_w"), "Mbd": mbd[by_dim], "Zbd": zbd[by_dim],
        "ident": np.eye(P, dtype=np.float32), "idx": rows(np.arange(E, 0, -1).astype(np.float32)),
        "bq": col(a0("bq")[by_dim]), "bk": col(a0("bk")[by_dim]), "bv": col(a0("bv")),
        "e_near": col(np.repeat(rel[2 * REL], H)), "e_far": col(np.repeat(rel[0], H)),
        "alpha": np.broadcast_to(a0("gate_alpha").reshape(1, 1), (P, 1)), "sls": col(np.tile(a1("score_log_scale"), HD)),
        "halfpi": np.full((P, 1), pi / 2, np.float32),
        "b1": f1("b1").T, "b2": f1("b2").T, "b3": f1("b3").T, "seld": seld, "mean8": mean8, "maskn": maskn, "maskt": maskn.T,
        "bo": rows(a0("bo")), "WoT": a0("Wo").T, "WoP": padded(a0("Wo")),
        "sw1": f0("sw1"), "sw2": f0("sw2"), "sw3": two(f0("sw3")),
        "ew1": f0("ew1").transpose(1, 0, 2).reshape(D, -1), "ew2": f0("ew2").transpose(1, 0, 2).reshape(D, -1),
        "ew3": f0("ew3").reshape(E, 2, P, D).transpose(2, 0, 1, 3).reshape(P, -1),
        "Wqa": a1("Wq_amp").T[:, by_dim], "Wka": a1("Wk_amp").T[:, by_dim], "Wqp": a1("Wq_phi").T[:, by_dim],
        "Wkp": a1("Wk_phi").T[:, by_dim], "Wv1": a1("Wv").T,
        "WoP1": padded(a1("Wo")), "gate1": f1("gate_w").T,
        "tw1": f1("w1").transpose(2, 0, 1).reshape(D, -1), "tw2": f1("w2").transpose(2, 0, 1).reshape(HID, -1),
        "tw3": f1("w3").transpose(2, 0, 1).reshape(D, -1),
        "tsw1": f1("sw1").T, "tsw2": f1("sw2").T, "tsw3": two(f1("sw3").T),
    }

    def pack(cols):
        return np.ascontiguousarray(np.concatenate([parts[n].reshape(P, k) for n, k in cols], 1, dtype=np.float32))

    j = np.arange(4 * P)
    etab = np.concatenate([rel[np.clip(q - (j - 2 * P), -REL, REL) + REL].T for q in range(2)], 0)
    arrays = {
        "x": np.ascontiguousarray(a0("hidden_states").reshape(B * S, D)), "wa": pack(COLS_A), "wb": pack(COLS_B),
        "wc": pack(COLS_C), "etab": np.ascontiguousarray(etab),
    }
    nc = bacc.Bacc("TRN2", target_bir_lowering=False, num_devices=1)
    args = [nc.dram_tensor(n, a.shape, mybir.dt.from_np(a.dtype), kind="ExternalInput").ap() for n, a in arrays.items()]
    args.append(nc.dram_tensor("out", (B * S, D), F32, kind="ExternalOutput").ap())
    program(nc, *args)
    r = run(nc, [arrays], core_ids=[0])
    return r.results[0]["out"].reshape(B, S, D)
```

```python
from contextlib import ExitStack
from math import log, pi, sqrt

import numpy as np
import concourse.bass as bass
from concourse import mybir

F32 = mybir.dt.float32
BF16 = mybir.dt.bfloat16
ALU = mybir.AluOpType
ACT = mybir.ActivationFunctionType
AX = mybir.AxisListType

P = 128
B, S, D = 4, 512, 128
H, HD = 16, 8
T = S // P
E = 8
F0 = 256
HID = 128
REL = 128
NQ = 32
UQ = 64
NU = S // UQ
G2 = UQ // NQ
SLOTS = 6
ROWS = 2 * SLOTS * HD
Q_RUNS = ((0, 3), (3, 2), (5, 1))
K_RUNS = ((0, 3, 0), (3, 2, 1), (5, 1, 2))
RING = 14
TILE = H * UQ
NEG = -1e30
LN_EPS = 1e-5

B_H, B_U, B_O, B_PV, B_MISC, B_S = 0, 1, 2, 3, 4, 5
NSB = 3
AMP_BANK = (B_S + 2, B_MISC)

COLS_A = [("WqT", D), ("WkT", D), ("WvT", D), ("gate0", E), ("MZ", D + H), ("ident", P), ("idx", E),
          ("bq", 1), ("bk", 1), ("e_near", 1), ("e_far", 1), ("alpha", 1), ("sls", 1), ("halfpi", 1),
          ("b1", E), ("b2", E), ("b3", E), ("mean8", P), ("maskn", P), ("maskt", P), ("bo", D), ("bv", D),
          ("WoT", D), ("sw1", F0), ("sw2", F0), ("sw3", 2 * D)]
COLS_B = [("ew1", E * F0), ("ew2", E * F0), ("ew3", E * 2 * D)]
COLS_C = [("Wqa", D), ("Wka", D), ("Wqp", D), ("Wkp", D), ("Wv1", D), ("WoT1", D), ("gate1", E),
          ("tw1", E * HID), ("tw2", E * D), ("tw3", E * HID), ("tsw1", F0), ("tsw2", F0), ("tsw3", 2 * D)]


def ffn_banks(s):
    return (B_S + 2, B_MISC) if s < FFN_BEFORE and s % 2 else (B_H, B_U)


def offsets(cols):
    at, out = 0, {}
    for name, n in cols:
        out[name] = (at, n)
        at += n
    return out, at


OFF_A, NA = offsets(COLS_A)
OFF_B, NB = offsets(COLS_B)
OFF_C, NC = offsets(COLS_C)

SLOTS0 = NU * T
AT_MAX, AT_SUB, AT_EXP, AT_PV, AT_EVAC = 4, 7, 8, 9, 12
AT_NATURAL, AT_BACK, AT_OUT = 17, 18, 19
NSLOT0 = (NU - 2) * T + AT_OUT + 1
FFN_BEFORE = 10
ORDER1 = (1, 0)
PASS1_AT = {2: (3, 6, 8, 9), 3: (15, 18, 20, 21), 4: (28, 31, 33, 34)}
PASS2_AT = {6: (1, 3, 5), 7: (6, 8, 10)}
FFN_AT = {6: 10, 14: 11, 22: 12, 28: 13, 32: 14, 34: 15, 36: 16, 38: 17}


def program(nc, x, wa, wb, wc, etab, out):
    ctx = ExitStack()
    with ctx:
        def sb(name, shape, dt=F32):
            return ctx.enter_context(nc.sbuf_tensor(name, shape, dt))

        def sem(name):
            s = ctx.enter_context(nc.semaphore(name))
            return s

        of_layer = ([], [])

        def sem0(name):
            s = sem(name)
            of_layer[0].append(s)
            return s

        def sem1(name):
            s = sem(name)
            of_layer[1].append(s)
            return s

        WA = sb("WA", [P, NA])
        WB = sb("WB", [P, NB])
        WC = sb("WC", [P, NC])

        def w(name, a=0, n=None):
            for off, t in ((OFF_A, WA), (OFF_B, WB), (OFF_C, WC)):
                if name in off:
                    at, width = off[name]
                    return t[:, at + a:at + a + (width if n is None else n)]

        ET = sb("ET", [P, 4 * P], BF16)
        QBD = sb("QBD", [P, H // 2, 2, S], BF16)
        KS = sb("KS", [P, 2, H // 2, S], BF16)
        QR = sb("QR", [P, H, S], BF16)
        KL = KS[:, :, :, :].rearrange("p a b s -> p (a b) s")
        QL = QR
        VP = sb("VP", [P, T, H, 32])
        RG = sb("RG", [P, RING * TILE])
        MB = sb("MB", [P, 2, TILE])
        X = sb("X", [P, T, D])
        XN = sb("XN", [P, T, D])
        XT = sb("XT", [P, S])
        G = sb("G", [P, T, D])
        TH = sb("TH", [P, S])
        AA = sb("AA", [P, S])
        HH = sb("HH", [P, 2, 2, S])
        ACC = sb("ACC", [P, T, D])
        SS = sb("SS", [P, T, D])
        R1 = sb("R1", [P, T, H * G2])
        M1 = sb("M1", [P, H * T])
        M2 = sb("M2", [H * G2, NQ])
        NM = sb("NM", [H * T, P])
        NR = sb("NR", [H * T, P])
        NMP = sb("NMP", [H * T, 3, P], BF16)
        CTX = sb("CTX", [P, 2, P])
        RDN = sb("RDN", [P, 4 * H])
        CN = sb("CN", [P, D])
        CT = sb("CT", [P, P])
        GBV = sb("GBV", [P, D])
        IDB = sb("IDB", [P, P], BF16)
        MKN = sb("MKN", [P, P], BF16)
        MKT = sb("MKT", [P, P], BF16)
        half = sb("half", [P, T])
        st = sb("st", [P, T, 6])
        mv = sb("mv", [P, T, 2])
        ve = sb("ve", [P, T])
        rs = sb("rs", [P, T])
        cols = sb("cols", [P, 8])
        gate_e, gate_s, gate, omg, epsc, qbias, halfc = (cols[:, i:i + 1] for i in range(7))
        LG, EQ, KEY, OH1, OH2, W8, WM = (sb(f"rt{i}", [P, T, E]) for i in range(7))
        m1, m2, km, dm, e2, w1, w2 = (sb(f"rv{i}", [P, T]) for i in range(7))
        WMK = sb("WMK", [P, T, 2 * E])
        WT = SS[0:2 * E, :, :].rearrange("p t d -> p (t d)")
        hb1 = sb("hb1", [P, E])

        def region(at, n, dt=F32):
            v = RG[:, at:at + n]
            return v if dt is F32 else v.bitcast(dt)

        F3 = region(0, 3 * S).rearrange("p (a s) -> p a s", a=3)
        R3 = region(3 * S, 3 * S).rearrange("p (a s) -> p a s", a=3)
        PARTS = region(6 * S, 9 * S // 2, BF16).rearrange("p (a c s) -> p a c s", a=3, c=3)
        QEO = region(11 * S, 3 * S, BF16).rearrange("p (a c s) -> p a c s", a=2, c=3)
        QMIN, QEX, SG, QMAX = (region((14 + i) * S, S) for i in range(4))
        NAB, EX, U1, C1, LNU, TP, ATP, SQ, RT = (region(2 * S * i, 2 * S).rearrange("p (t s) -> p t s", t=2) for i in range(9))
        SI, CO = (region((22 + 2 * i) * S, 2 * S).rearrange("p (t s) -> p t s", t=2) for i in range(2))
        CS4 = region(18 * S, 4 * S).rearrange("p (t c s) -> p t c s", t=2, c=2)
        R4 = region(0, 4 * S).rearrange("p (t c s) -> p t c s", t=2, c=2)
        PARTS1 = region(4 * S, 6 * S, BF16).rearrange("p (t c u s) -> p t c u s", t=2, c=3, u=2)
        PCOL = (0, 512, 896, 1152)
        PH = 1280
        PL = region(0, 2 * 4 * PH).rearrange("p (b j n) -> p b j n", b=2, j=4)
        CT1 = region(20 * S, 2 * S).rearrange("p (a s) -> p a s", a=2)
        CN1 = region(22 * S, S).rearrange("p (t d) -> p t d", t=T)
        CTT = region(23 * S, S)
        XZ = region(24 * S, S).rearrange("p (t d) -> p t d", t=T)
        XS = region(26 * S, 2 * S).rearrange("p (a s) -> p a s", a=2)
        YT = G[:, :, :].rearrange("p t d -> p (t d)")
        C3 = (HH[:, 0, 0, :], ACC[:, :, :].rearrange("p t d -> p (t d)"))
        HE = HH[:, 0, 1, :]
        CC = HH[:, 1, :, :]
        MBE = MB[:, :, :].rearrange("p b (a s) -> p b a s", a=2)

        PS = ctx.enter_context(nc.psum_tensor("PS", [P, 8, 512], F32))

        def bank(i, n=512, a=0):
            return PS[:, i, a:a + n]

        d_q = nc.dram_tensor("d_q", [3, HD, H, S], BF16).ap()
        d_k = nc.dram_tensor("d_k", [2, SLOTS, HD, H, S], BF16).ap()
        d_e = nc.dram_tensor("d_e", [6, HD, H, S], BF16).ap()
        d_m = nc.dram_tensor("d_m", [2, H * G2, NQ], F32).ap()
        d_c = nc.dram_tensor("d_c", [2, 3, 2, HD, H, S], BF16).ap()
        d_n = nc.dram_tensor("d_n", [3, H * T, P], BF16).ap()
        d_w = nc.dram_tensor("d_w", [2 * E, S], F32).ap()
        d_t = nc.dram_tensor("d_t", [3, 2 * HD, 4 * P], BF16).ap()

        s_wa, s_wb, s_wc, s_et, s_etd, s_etl = (sem(n) for n in ("wa_in", "wb_in", "wc_in", "etab_in", "etab_out", "etab_set"))
        s_pre_pool, s_pre_dve, s_gexp, s_etp = (sem(n) for n in ("pool_set", "dve_set", "gate_exp", "etab_parts"))
        x_first, first_norm = sem("x_first_in"), sem("first_norm")
        s_ended, s_l0_ended, s_l1_cleared, out_done = (
            sem(n) for n in ("sequence_ended", "layer0_ended", "layer1_cleared", "out_written"))
        chain_dve = sem("dve_step")
        qr_zero, x_kept = sem0("rows_above_zero"), sem0("x_kept")
        proj_q, proj_k, proj_v, logit_ps, qk_sb, v_set, logits_read = (
            sem0(n) for n in ("q_psum", "k_psum", "v_psum", "logits_psum", "qk_sbuf", "v_set", "logits_read"))
        qeo_zero, parts_ready, qeo_ready, dq_out, de_out, qk_in, rel_in = (
            sem0(n) for n in ("qeo_zero", "parts", "qeo", "parts_in_dram", "qeo_in_dram", "qk_stacked", "qrel_stacked"))
        qmin_ready, qexp_ready, sg_ready, glob_ps, g_ready = (sem0(n) for n in ("qmin", "qexp", "sigma", "global_psum", "global"))
        rdm_ready, rexp_ready = sem0("route_diff"), sem0("route_exp")
        hu_ps, th_ready, hh_ready, fo_ps, fo_used = (sem0(n) for n in ("hu_psum", "tanh", "hh", "ffn_psum", "ffn_added"))
        sc_ps, sc_copied, red_done, m1_ready, mt_ps, m2_ready = (
            sem0(n) for n in ("scores_psum", "scores_copied", "maxed", "max_of_keys", "max_transposed", "max_rows"))
        dm_out, mb_in0, mb_in1, sub_dve, sub_pool, p_ready, pv_done = (
            sem0(n) for n in ("max_in_dram", "max_spread_even", "max_spread_odd", "shifted_dve", "shifted_pool", "probs", "pv"))
        mb_in = (mb_in0, mb_in1)
        ctx_ready, nat_ps, cn_ready, back_ps, ct_ready, at_ps, ss_ready = (
            sem0(n) for n in ("ctx", "ctx_natural", "ctx_normed", "ctx_back_psum", "ctx_back", "attn_psum", "attn"))
        rest2_ready = sem0("rests_of_q_k")
        qmax_ready, kf_ready, hi_ready, rest_ready, mid_ready, kparts_ready, gn_ready = (
            sem0(n) for n in ("qmax", "k_far", "hi_parts", "rests", "mid_parts", "k_far_parts", "global_scaled"))
        ga_ready = sem0("gelu_tanh0")
        var1, rstd1, xn1, xt_ps1, xt1 = (sem1(n) for n in ("var1", "rstd1", "xn1", "xt_psum1", "xt1"))
        amp_ps, phi_ps, v_ps1, lg_ps1, tp_sb, v_set1, lg_read1 = (
            sem1(n) for n in ("amp_psum", "phi_psum", "v_psum1", "logits_psum1", "phase", "v_set1", "logits_read1"))
        ex_r, u_r, ln_r, amp_r, sq_r, msq_ps, rt_r, abs_r, cos_r, parts1, dc_out, l1_in = (
            sem1(n) for n in ("exp_abs", "one_plus", "ln", "amp", "amp_sq", "meansq_psum", "rms", "phase_abs",
                              "cos_sin", "parts1", "parts1_in_dram", "stacked1"))
        lge_r, lgx_r, wm_r, wt_ps, wt_r, dw_out, wb_in0, wb_in1, xs_r = (
            sem1(n) for n in ("l1_route_diff", "l1_route_exp", "weights1", "weights_psum", "weights_t", "weights_in_dram",
                              "expert_spread_even", "expert_spread_odd", "xs"))
        wb_in = (wb_in0, wb_in1)
        hu1_ps, th1_r, h1_r, fo1_ps, y_c, y_add, yt_ps, yn_r = (
            sem1(n) for n in ("hu1_psum", "tanh1", "hh1", "ffn1_psum", "expert_term", "y_added", "y_psum", "y_used"))
        s1_ps, s1_max, nmt_ps, nm_r, dn_out, nm_in = (
            sem1(n) for n in ("s1_psum", "s1_maxed", "max1_transposed", "neg_max", "neg_max_in_dram", "neg_max_in"))
        s2_ps, p1_r, pv1, ctx1, nat1_ps, cn1, back1_ps, ctt_r, at1_ps, ga1, xo_r = (
            sem1(n) for n in ("s2_psum", "probs1", "pv1", "ctx1", "ctx1_natural", "ctx1_normed", "ctx1_back_psum",
                              "ctx1_back", "attn1_psum", "gelu_tanh1", "x_out"))
        cs_r = sem1("cos_sin_scaled")
        x_next, var_next, rstd_next, xn_next, xt_next_ps, xt_next = (
            sem1(n) for n in ("x_next_in", "var_next", "rstd_next", "xn_next", "xt_next_psum", "xt_next"))
        abz_r, hi1_r, rest1_r, mid1_r = (sem1(n) for n in ("amp_abs", "hi_parts1", "rests1", "mid_parts1"))
        c1_r, lnsq_r, dc_q, he_r, c3_r, c3m_r, sig1_r, y1_r = (
            sem1(n) for n in ("softplus_rest", "ln_meansq", "q_parts1_in_dram", "hidden1", "gate1_rows", "gate1_masked", "sigmoid1", "silu1"))

        def from_layer0_to_1(eng, b):
            eng.sem_inc(s_l0_ended, 1)
            eng.wait_ge(s_l1_cleared, b + 1)
            eng.nop(nofuse=True)

        def end_sequence(eng, b):
            eng.sem_inc(s_ended, 1)
            eng.wait_ge(s_ended, (b + 1) * 5)
            eng.nop(nofuse=True)

        block = ctx.enter_context(nc.Block())

        @block.sync
        def _(sp):
            sp.dma_start(XN[:, :, :], x[0:S, :].rearrange("(t p) d -> p t d", p=P)).then_inc(x_first, 16)
            sp.dma_start(WA[:, :], wa).then_inc(s_wa, 16)
            sp.dma_start(TH[0:2 * HD, :], etab).then_inc(s_et, 16)
            sp.dma_start(WB[:, :], wb).then_inc(s_wb, 16)
            sp.wait_ge(s_etp, 1)
            sp.dma_start(d_t.rearrange("c r n -> r c n"), HH[0:2 * HD, 0, :, :].rearrange("p a s -> p (a s)")
                         .bitcast(BF16)[:, 0:3 * S].rearrange("p (c s) -> p c s", c=3)).then_inc(s_etd, 16)
            sp.wait_ge(s_etd, 16)
            for two in range(2):
                for first, n, part in K_RUNS:
                    for j in range(n):
                        r = two * SLOTS * HD + (first + j) * HD
                        sp.dma_start(ET[r:r + HD, :], d_t[part, two * HD:(two + 1) * HD, :]).then_inc(s_etl, 16)
            sp.dma_start(WC[:, :], wc).then_inc(s_wc, 16)
            with sp.Fori(0, B) as b:
                for s in of_layer[1]:
                    sp.sem_clear(s)
                sp.sem_inc(s_l1_cleared, 1)
                sp.wait_ge(parts_ready, 1)
                sp.dma_start(d_q.rearrange("c d h s -> (d h) c s"), PARTS[:, 0, :, :]).then_inc(dq_out, 16)
                for t in range(2):
                    if t:
                        sp.wait_ge(kparts_ready, 1)
                    for first, n, part in K_RUNS:
                        sp.dma_start(d_k[t, first:first + n].rearrange("c d h s -> (d h) c s"),
                                     PARTS[:, 1 + t, part:part + 1, :].to_broadcast([P, n, S])).then_inc(dq_out, 16)
                sp.wait_ge(qeo_ready, 1)
                sp.dma_start(d_e.rearrange("c d h s -> (d h) c s"), QEO.rearrange("p a c s -> p (a c) s")).then_inc(de_out, 16)
                sp.wait_ge(dq_out, 16 * 7)
                for two in range(2):
                    for first, n in Q_RUNS:
                        r = two * SLOTS * HD + first * HD
                        sp.dma_start(QBD[r:r + n * HD, :, two, :],
                                     d_q[0:n].rearrange("c d (a t) s -> t (c d) a s", t=2)[two]).then_inc(qk_in, 16)
                    r = two * SLOTS * HD
                    for t in range(2):
                        sp.dma_start(KS[r:r + SLOTS * HD, t, :, :],
                                     d_k[t].rearrange("c d (a t) s -> t (c d) a s", t=2)[two]).then_inc(qk_in, 16)
                sp.wait_ge(de_out, 16)
                for two in range(2):
                    for first, n in Q_RUNS:
                        r = two * SLOTS * HD + first * HD
                        sp.dma_start(QR[r:r + n * HD, :, :],
                                     d_e[3 * two:3 * two + n].rearrange("c d h s -> (c d) h s")).then_inc(rel_in, 16)
                for u in range(NU):
                    sp.wait_ge(m2_ready, u + 1)
                    sp.dma_start(d_m[u % 2], M2[:, :]).then_inc(dm_out, 16)
                    sp.wait_ge(dm_out, 16 * (u + 1))
                    if u >= 2:
                        sp.wait_ge(sub_dve, u - 1)
                        sp.wait_ge(sub_pool, 3 * (u - 1))
                    sp.dma_start(MB[:, u % 2, :], d_m[u % 2].rearrange("c i -> (c i)")[None, :].to_broadcast([P, TILE])
                                 ).then_inc(mb_in[u % 2], 16)
                sp.wait_ge(sub_dve, NU)
                sp.wait_ge(sub_pool, 3 * NU)
                sp.wait_ge(s_l0_ended, (b + 1) * 4)
                sp.nop(nofuse=True)
                for s in of_layer[0]:
                    sp.sem_clear(s)
                sp.wait_ge(wt_r, 1)
                sp.dma_start(d_w, WT[:, :]).then_inc(dw_out, 16)
                sp.wait_ge(dw_out, 16)

                def spread(e):
                    if e >= 2:
                        sp.wait_ge(c3m_r, e - 1)
                        sp.wait_ge(xs_r, e - 1)
                    for a in range(2):
                        sp.dma_start(MBE[:, e % 2, a, :], d_w[a * E + e:a * E + e + 1, :].to_broadcast([P, S])
                                     ).then_inc(wb_in[e % 2], 16)

                spread(0)
                spread(1)
                for n, t in enumerate(ORDER1):
                    sp.wait_ge(parts1, n + 1)
                    sp.dma_start(d_c[t].rearrange("c u d h s -> (d h) (c u) s"),
                                 PARTS1[:, t, :, :, :].rearrange("p c u s -> p (c u) s")).then_inc((dc_q, dc_out)[t], 16)
                sp.wait_ge(dc_out, 16)
                for first, n, part in K_RUNS:
                    r = 2 * first * HD
                    sp.dma_start(KL[r:r + 2 * n * HD, :, :],
                                 d_c[1, part:part + 1].rearrange("c u d h s -> c (u d) (h s)")
                                 .to_broadcast([n, 2 * HD, H * S])).then_inc(l1_in, 16)
                sp.wait_ge(dc_q, 16)
                for first, n in Q_RUNS:
                    sp.dma_start(QL[2 * first * HD:2 * (first + n) * HD, :, :],
                                 d_c[0, 0:n].rearrange("c u d h s -> (c u d) h s")).then_inc(l1_in, 16)
                sp.wait_ge(xt_ps1, 1)
                sp.dma_start(XN[:, :, :], x[bass.ds((b + 1) * S, S), :].rearrange("(t p) d -> p t d", p=P)).then_inc(x_next, 16)
                for e in range(2, 6):
                    spread(e)
                sp.wait_ge(nm_r, 1)
                sp.dma_start(d_n.rearrange("c r n -> r c n"), NMP[:, :, :]).then_inc(dn_out, 16)
                sp.wait_ge(dn_out, 16)
                sp.dma_start(QL[ROWS:ROWS + 3, :, :], d_n.rearrange("c (h t) n -> c h (t n)", h=H)).then_inc(nm_in, 16)
                spread(6)
                spread(7)
                sp.wait_ge(xo_r, 1)
                sp.dma_start(out[bass.ds(b * S, S), :].rearrange("(t p) d -> p t d", p=P), X[:, :, :]).then_inc(out_done, 16)
                end_sequence(sp, b)
            sp.wait_ge(out_done, 16 * B)

        @block.gpsimd
        def _(pool):
            nc.gpsimd.memset(QBD[:, :, :, :], 0.0).then_inc(s_pre_pool, 1)
            nc.gpsimd.memset(VP[:, :, :, :], 0.0).then_inc(s_pre_pool, 1)
            nc.gpsimd.memset(half[:, :], -0.5).then_inc(s_pre_pool, 1)
            pool.wait_ge(s_pre_pool, 3)
            v2 = VP[:, :, :, :].rearrange("p t (a two) c -> p (t a) two c", two=2)
            for two in range(2):
                nc.gpsimd.memset(v2[:, :, two, 16 + 8 * two:24 + 8 * two], 1.0).then_inc(s_pre_pool, 1)
            pool.wait_ge(s_pre_pool, 5)
            pool.wait_ge(first_norm, 1)
            nc.gpsimd.tensor_tensor(rs[:, :], ve[:, :], half[:, :], ALU.pow).then_inc(first_norm, 1)
            with pool.Fori(0, B) as b:
                nc.gpsimd.memset(QEO.rearrange("p a c s -> p (a c s)").bitcast(F32), 0.0).then_inc(qeo_zero, 1)
                pool.wait_ge(qeo_zero, 1)
                nc.gpsimd.memset(QR[ROWS:P, :, :].rearrange("p h s -> p (h s)").bitcast(F32), 0.0).then_inc(qr_zero, 1)
                pool.wait_ge(qr_zero, 1)
                pool.wait_ge(qk_sb, 2)
                nc.gpsimd.tensor_scalar(QMIN, F3[:, 0, :], 0.0, None, ALU.min).then_inc(qmin_ready, 1)
                nc.gpsimd.tensor_scalar(F3[:, 2, 0:S // 2], F3[:, 1, 0:S // 2], w("e_near"), None, ALU.add).then_inc(kf_ready, 1)
                nc.gpsimd.tensor_scalar(F3[:, 2, S // 2:S], F3[:, 1, S // 2:S], w("e_far"), None, ALU.add).then_inc(kf_ready, 1)
                pool.wait_ge(hi_ready, 3)
                nc.gpsimd.tensor_tensor(R3[:, 2, :], F3[:, 2, :], PARTS[:, 2, 0, :], ALU.subtract).then_inc(rest_ready, 1)
                pool.wait_ge(mid_ready, 2)
                nc.gpsimd.tensor_tensor(PARTS[:, 2, 2, :], R3[:, 2, :], PARTS[:, 2, 1, :], ALU.subtract).then_inc(kparts_ready, 1)
                nc.gpsimd.tensor_scalar(QMAX, F3[:, 0, :], 0.0, None, ALU.max).then_inc(qmax_ready, 1)
                pool.wait_ge(qexp_ready, 1)
                pool.wait_ge(qmax_ready, 1)
                nc.gpsimd.tensor_tensor(SG, QMAX, QEX, ALU.add).then_inc(sg_ready, 1)
                pool.wait_ge(gn_ready, 1)
                nc.gpsimd.tensor_tensor(G[:, :, :], G[:, :, :], GBV[:, None, :].to_broadcast([P, T, D]), ALU.add).then_inc(g_ready, 1)
                for u in range(NU):
                    pool.wait_ge(mb_in[u % 2], 16 * (u // 2 + 1))
                    for kb in range(1, T):
                        tile = region((T * u + kb) % RING * TILE, TILE)
                        pool.wait_ge(red_done, T * u + kb + 1)
                        nc.gpsimd.tensor_tensor(tile, tile, MB[:, u % 2, :], ALU.subtract).then_inc(sub_pool, 1)
                from_layer0_to_1(pool, b)
                pool.wait_ge(var1, 1)
                nc.gpsimd.tensor_tensor(rs[:, :], ve[:, :], half[:, :], ALU.pow).then_inc(rstd1, 1)
                pool.wait_ge(xt1, 1)

                def weighted(e):
                    pool.wait_ge(wb_in[e % 2], 32 * (e // 2 + 1))
                    if e >= 2:
                        pool.wait_ge(hu1_ps, 2 + e - 1)
                    nc.gpsimd.tensor_tensor(XS[:, e % 2, :], XT[:, :], MBE[:, e % 2, 0, :], ALU.mult).then_inc(xs_r, 1)

                def added(e):
                    pool.wait_ge(y_c, e + 1)
                    if e:
                        pool.wait_ge(y_add, e)
                    nc.gpsimd.tensor_tensor(YT[:, :], YT[:, :], CC[:, e % 2, :], ALU.add).then_inc(y_add, 1)

                def masked(e):
                    pool.wait_ge(c3_r, e + 1)
                    nc.gpsimd.tensor_tensor(C3[e % 2], C3[e % 2], MBE[:, e % 2, 1, :], ALU.mult).then_inc(c3m_r, 1)

                weighted(0)
                weighted(1)
                for e in range(E):
                    masked(e)
                    if e:
                        added(e - 1)
                    if e + 2 < E:
                        weighted(e + 2)
                added(E - 1)
                pool.wait_ge(var_next, 1)
                nc.gpsimd.tensor_tensor(rs[:, :], ve[:, :], half[:, :], ALU.pow).then_inc(rstd_next, 1)
                end_sequence(pool, b)

        @block.tensor
        def _(pe):
            mm = nc.tensor.matmul
            pe.wait_ge(s_wa, 16)
            pe.wait_ge(s_pre_pool, 5)
            pe.wait_ge(s_pre_dve, 1)

            def transpose_tiles(done, src=XN, to=B_MISC):
                for t in range(T):
                    last = nc.tensor.transpose(bank(to, P, t * P), src[:, t, :], w("ident"))
                last.then_inc(done, 1)

            def ffn_hidden(s):
                e, fi = s // 2, s % 2
                if s > FFN_BEFORE:
                    pe.wait_ge(hh_ready, s)
                elif s >= 2:
                    pe.wait_ge(hh_ready, s - 1)
                mm(bank(ffn_banks(s)[0]), w("sw1", fi * P, P) if e == 0 else w("ew1", (e - 1) * F0 + fi * P, P), XT[:, :],
                   start=True, stop=True)

            def ffn_gate(s):
                e, fi = s // 2, s % 2
                mm(bank(ffn_banks(s)[1]), w("sw2", fi * P, P) if e == 0 else w("ew2", (e - 1) * F0 + fi * P, P), XT[:, :],
                   start=True, stop=True).then_inc(hu_ps, 1)

            def ffn_out(e, tiles=range(T)):
                if tiles[0] == 0:
                    pe.wait_ge(hh_ready, 2 * e + 2)
                    if e:
                        pe.wait_ge(fo_used, e)
                    else:
                        pe.wait_ge(v_set, 1)
                for t in tiles:
                    for fi in range(2):
                        a = w("sw3", fi * D, D) if e == 0 else w("ew3", ((e - 1) * 2 + fi) * D, D)
                        last = mm(bank(B_O, P, t * P), HH[:, e % 2, fi, t * P:(t + 1) * P], a, start=fi == 0, stop=fi == 1)
                if tiles[-1] == T - 1:
                    last.then_inc(fo_ps, 1)

            def out_after(s):
                return s // 2 - 1 if s >= 2 and s % 2 == 0 else None

            def ffn_one(s):
                ffn_hidden(s)
                ffn_gate(s)
                if out_after(s) is not None:
                    ffn_out(out_after(s))

            def ffn_piece(i, second):
                if i in FFN_AT:
                    (ffn_gate if second else ffn_hidden)(FFN_AT[i])
                if i - 1 in FFN_AT and out_after(FFN_AT[i - 1]) is not None:
                    ffn_out(out_after(FFN_AT[i - 1]), range(2, T) if second else range(2))

            def score_tile(i):
                u, kb = i // T, i % T
                far = abs(u * UQ // P - kb) >= 2
                for g in range(G2):
                    n = G2 * i + g
                    ps = bank(B_S + n % NSB)
                    q0 = u * UQ + g * NQ
                    if n >= NSB:
                        pe.wait_ge(sc_copied, n - NSB + 1)
                    elif n == NSB - 1:
                        pe.wait_ge(hh_ready, FFN_BEFORE)
                    for a in range(H // 2):
                        last = mm(ps[:, a * 2 * NQ:(a + 1) * 2 * NQ], KS[:, int(far), a, kb * P:(kb + 1) * P],
                                  QBD[:, a, :, q0:q0 + NQ], start=a == 0, stop=far and a == H // 2 - 1,
                                  skip_group_check=True)
                    if not far:
                        v = ps.rearrange("p (h q) -> p h q", h=H)
                        for j in range(NQ // 2):
                            at = kb * P - (q0 + 2 * j) + 2 * P
                            last = mm(v[:, :, 2 * j:2 * j + 2], ET[:, at:at + P], QR[:, :, q0 + 2 * j:q0 + 2 * j + 2],
                                      start=False, stop=j == NQ // 2 - 1, skip_group_check=True)
                    last.then_inc(sc_ps, 1)
                    if g == 0:
                        ffn_piece(i, False)

            def max_transpose(v):
                pe.wait_ge(m1_ready, v + 1)
                if v >= 4 and v % 2 == 0:
                    pe.wait_ge(ss_ready, (v - 4) // 2 + 1)
                elif v:
                    pe.wait_ge(m2_ready, v)
                nc.tensor.transpose(PS[0:H * G2, B_MISC, 0:P], M1[:, 0:H * G2], w("ident")).then_inc(mt_ps, 1)

            def pv(v, kb):
                pe.wait_ge(p_ready, T * v + kb + 1)
                if kb == 0:
                    if v:
                        pe.wait_ge(ctx_ready, v)
                    else:
                        pe.wait_ge(logits_read, 1)
                tile = region((T * v + kb) % RING * TILE, TILE).rearrange("p (h q) -> p h q", h=H)
                for half_ in range(2):
                    for two in range(2):
                        for j in range(4):
                            h = half_ * 8 + 2 * j + two
                            last = mm(PS[32 * j:32 * j + 32, B_PV, half_ * UQ:(half_ + 1) * UQ], VP[:, kb, h, :], tile[:, h, :],
                                      start=kb == 0 and half_ == 0 and two == 0, stop=kb == T - 1, skip_group_check=True)
                last.then_inc(pv_done, 1)

            def natural(c):
                pe.wait_ge(ctx_ready, 2 * c + 2)
                if c < T - 1:
                    pe.wait_ge(m2_ready, 2 * c + 4)
                else:
                    pe.wait_ge(ss_ready, c)
                for a in range(2):
                    last = nc.tensor.transpose(bank(B_MISC, P, a * P), CTX[:, a, :], w("ident"))
                last.then_inc(nat_ps, 1)

            def back(c):
                pe.wait_ge(cn_ready, c + 1)
                nc.tensor.transpose(bank(B_MISC, P), CN[:, :], w("ident")).then_inc(back_ps, 1)

            def attn_out(c):
                pe.wait_ge(ct_ready, c + 1)
                mm(bank(B_MISC, P), CT[:, :], w("WoT"), start=True, stop=True).then_inc(at_ps, 1)

            def ffn1_shared(s):
                pe.wait_ge(s_wc, 16)
                if s:
                    pe.wait_ge(h1_r, s)
                mm(bank(B_H), w("tsw1", s * P, P), XT[:, :], start=True, stop=True)
                mm(bank(B_U), w("tsw2", s * P, P), XT[:, :], start=True, stop=True).then_inc(hu1_ps, 1)

            def ffn1_shared_out():
                pe.wait_ge(h1_r, 2)
                pe.wait_ge(v_set1, 1)
                mm(bank(B_O), w("tsw3", 0, D), HH[:, 0, 0, :], start=True, stop=False)
                mm(bank(B_O), w("tsw3", D, D), HH[:, 0, 1, :], start=False, stop=True).then_inc(fo1_ps, 1)

            def expert1_in(e):
                pe.wait_ge(xs_r, e + 1)
                pe.wait_ge(he_r, e) if e else pe.wait_ge(h1_r, 2)
                if e:
                    pe.wait_ge(c3_r, e)
                mm(bank(B_H), w("tw1", e * HID, HID), XS[:, e % 2, :], start=True, stop=True)
                mm(bank(B_U), w("tw3", e * HID, HID), XS[:, e % 2, :], start=True, stop=True).then_inc(hu1_ps, 1)

            def expert1_out(e):
                pe.wait_ge(he_r, e + 1)
                pe.wait_ge(y_c, e) if e else pe.wait_ge(yn_r, 1)
                mm(bank(B_O), w("tw2", e * D, D), HE, start=True, stop=True).then_inc(fo1_ps, 1)

            def s1_bank(n, tile, heads):
                if n >= NSB:
                    pe.wait_ge(s1_max, n - NSB + 1)
                width = (tile + 1) * P
                ps = bank(B_S + n % NSB)
                for a, h in enumerate(heads):
                    o = ps[:, a * width:(a + 1) * width]
                    mm(o, QL[:, h, tile * P:(tile + 1) * P], KL[:, h, 0:width], start=a == 0, stop=False,
                       skip_group_check=True)
                    last = mm(o[:, tile * P:width], IDB[:, :], MKN[:, :], start=False, stop=True, skip_group_check=True)
                last.then_inc(s1_ps, 1)

            def s2_banks(n, h):
                for c, kbs in enumerate(((0,), (1,), (2, 3))):
                    i = 3 * n + c
                    if i >= NSB:
                        pe.wait_ge(p1_r, i - NSB + 1)
                    at = 0
                    for kb in kbs:
                        width = S - kb * P
                        o = bank(B_S + c, width, at)
                        mm(o, KL[:, h, kb * P:(kb + 1) * P], QL[:, h, kb * P:S], start=at == 0, stop=False,
                           skip_group_check=True)
                        last = mm(o[:, 0:P], IDB[:, :], MKT[:, :], start=False, stop=True, skip_group_check=True)
                        at += width
                    last.then_inc(s2_ps, 1)

            def pv1_group(gq):
                half_, two = gq // 2, gq % 2
                pe.wait_ge(p1_r, 12 * (gq + 1))
                if gq == 2:
                    pe.wait_ge(ctx1, 1)
                if gq == 0:
                    pe.wait_ge(wt_r, 1)
                for kb in range(T):
                    for j in range(4):
                        h = half_ * 8 + 2 * j + two
                        last = mm(PS[32 * j:32 * j + 32, B_PV, kb * P:S], VP[:, kb, h, :],
                                  PL[:, gq % 2, j, PCOL[kb]:PCOL[kb] + S - kb * P],
                                  start=two == 0 and kb == 0, stop=two == 1 and kb == T - 1, skip_group_check=True)
                last.then_inc(pv1, 1)

            pe.wait_ge(first_norm, 3)
            transpose_tiles(first_norm, XZ, B_U)
            pe.wait_ge(first_norm, 5)
            with pe.Fori(0, B) as b:
                mm(bank(B_H), w("WqT"), XT[:, :], start=True, stop=True).then_inc(proj_q, 1)
                mm(bank(B_U), w("WkT"), XT[:, :], start=True, stop=True).then_inc(proj_k, 1)
                for t in range(T):
                    last = mm(bank(B_O, P, t * P), XT[:, t * P:(t + 1) * P], w("WvT"), start=True, stop=True)
                last.then_inc(proj_v, 1)
                for t in range(T):
                    last = mm(bank(B_PV, E, t * E), XT[:, t * P:(t + 1) * P], w("gate0"), start=True, stop=True)
                last.then_inc(logit_ps, 1)
                pe.wait_ge(qk_sb, 2)
                ffn_one(0)
                ffn_one(1)
                pe.wait_ge(s_wb, 16)
                ffn_one(2)
                pe.wait_ge(sg_ready, 1)
                for t in range(T):
                    last = mm(bank(B_S + t // 2, D + H, t % 2 * (D + H)), SG[:, t * P:(t + 1) * P], w("MZ"), start=True, stop=True)
                last.then_inc(glob_ps, 1)
                for s in range(3, FFN_BEFORE):
                    ffn_one(s)
                pe.wait_ge(gn_ready, 1)
                pe.wait_ge(s_etl, 16 * 12)
                pe.wait_ge(qk_in, 16 * (6 + 4))
                pe.wait_ge(rel_in, 16 * 6)
                pe.wait_ge(qr_zero, 1)
                for i in range(NSLOT0):
                    if i < SLOTS0:
                        score_tile(i)
                    else:
                        ffn_piece(i, False)
                    ffn_piece(i, True)
                    for v in range(NU):
                        if i == T * v + AT_MAX:
                            max_transpose(v)
                        if 0 <= i - T * v - AT_PV < T:
                            pv(v, i - T * v - AT_PV)
                    for c in range(T):
                        if i == 2 * T * c + AT_NATURAL:
                            natural(c)
                        if i == 2 * T * c + AT_BACK:
                            back(c)
                        if i == 2 * T * c + AT_OUT:
                            attn_out(c)
                ffn_out(E)

                from_layer0_to_1(pe, b)
                pe.wait_ge(xn1, 1)
                transpose_tiles(xt_ps1)
                pe.wait_ge(xt1, 1)
                pe.wait_ge(s_wc, 16)
                for n, t in enumerate(ORDER1):
                    mm(bank(B_S + n), w(("Wqp", "Wkp")[t]), XT[:, :], start=True, stop=True).then_inc(phi_ps, 1)
                for n, t in enumerate(ORDER1):
                    mm(bank(AMP_BANK[t]), w(("Wqa", "Wka")[t]), XT[:, :], start=True, stop=True).then_inc(amp_ps, 1)
                for t in range(T):
                    last = mm(bank(B_PV, E, t * E), XT[:, t * P:(t + 1) * P], w("gate1"), start=True, stop=True)
                last.then_inc(lg_ps1, 1)
                ffn1_shared(0)
                for t in range(T):
                    last = mm(bank(B_O, P, t * P), XT[:, t * P:(t + 1) * P], w("Wv1"), start=True, stop=True)
                last.then_inc(v_ps1, 1)
                ffn1_shared(1)
                for n, t in enumerate(ORDER1):
                    pe.wait_ge(tp_sb, n + 1)
                    pe.wait_ge(sq_r, n + 1)
                    mm(bank(B_S + n), w("mean8"), SQ[:, t, :], start=True, stop=True).then_inc(msq_ps, 1)
                pe.wait_ge(wm_r, 1)
                for t in range(T):
                    last = nc.tensor.transpose(PS[0:2 * E, B_PV, t * P:(t + 1) * P], WMK[:, t, :], w("ident"))
                last.then_inc(wt_ps, 1)
                ffn1_shared_out()
                for e in range(2):
                    expert1_in(e)
                    expert1_out(e)
                pe.wait_ge(lnsq_r, 2)
                pe.wait_ge(amp_r, 2)
                pe.wait_ge(l1_in, 16 * 6)
                n = 0
                for tile in range(T):
                    per = (4, 2, 1, 1)[tile]
                    for h0 in range(0, H, per):
                        s1_bank(n, tile, range(h0, h0 + per))
                        n += 1
                        for e, (at_in, _, at_out, _) in PASS1_AT.items():
                            if n == at_in:
                                expert1_in(e)
                            if n == at_out:
                                expert1_out(e)
                pe.wait_ge(s1_max, n)
                nc.tensor.transpose(PS[0:H * T, B_MISC, 0:P], M1[:, :], w("ident")).then_inc(nmt_ps, 1)
                expert1_in(5)
                expert1_out(5)
                pe.wait_ge(nm_in, 16)
                for gq in range(4):
                    half_, two = gq // 2, gq % 2
                    for j in range(4):
                        s2_banks(4 * gq + j, half_ * 8 + 2 * j + two)
                        for e, (at_in, _, at_out) in PASS2_AT.items():
                            if 4 * gq + j == at_in:
                                expert1_in(e)
                            if 4 * gq + j == at_out:
                                expert1_out(e)
                        if gq and j == 0:
                            pv1_group(gq - 1)
                pe.wait_ge(xn_next, 1)
                transpose_tiles(xt_next_ps, XZ, B_U)
                pv1_group(3)
                pe.wait_ge(y_add, E)
                pe.wait_ge(y_c, E)
                for t in range(T):
                    last = nc.tensor.transpose(bank(B_O, P, t * P), YT[:, t * P:(t + 1) * P], w("ident"))
                last.then_inc(yt_ps, 1)
                pe.wait_ge(ctx1, 2)
                for t in range(T):
                    for a in range(2):
                        last = nc.tensor.transpose(bank((B_MISC, B_H)[t // 2], P, (t % 2 * 2 + a) * P),
                                                   CT1[:, a, t * P:(t + 1) * P], w("ident"))
                    if t % 2:
                        last.then_inc(nat1_ps, 1)
                pe.wait_ge(cn1, 2)
                for t in range(T):
                    last = nc.tensor.transpose(bank(B_U, P, t * P), CN1[:, t, :], w("ident"))
                last.then_inc(back1_ps, 1)
                pe.wait_ge(ctt_r, 1)
                for t in range(T):
                    last = mm(bank(B_PV, P, t * P), CTT[:, t * P:(t + 1) * P], w("WoT1"), start=True, stop=True)
                last.then_inc(at1_ps, 1)
                end_sequence(pe, b)

        @block.scalar
        def _(act):
            A = nc.scalar.activation
            act.wait_ge(s_wa, 16)
            A(gate_e, w("alpha"), ACT.Exp, scale=-1.0).then_inc(s_gexp, 1)

            def ffn_tanh(s):
                act.wait_ge(hu_ps, s + 1)
                if s:
                    act.wait_ge(hh_ready, s)
                A(TH[:, :], bank(ffn_banks(s)[0]), ACT.Tanh, scale=0.5).then_inc(th_ready, 1)

            def exp_tile(v, kb):
                if kb == 0:
                    act.wait_ge(sub_dve, v + 1)
                else:
                    act.wait_ge(sub_pool, 3 * v + kb)
                tile = region((4 * v + kb) % RING * TILE, TILE)
                A(tile, tile, ACT.Exp, scale=1.0 / sqrt(HD)).then_inc(p_ready, 1)

            with act.Fori(0, B) as b:
                act.wait_ge(proj_q, 1)
                A(F3[:, 0, :], bank(B_H), ACT.Identity, bias=w("bq")).then_inc(qk_sb, 1)
                act.wait_ge(proj_k, 1)
                A(F3[:, 1, :], bank(B_U), ACT.Identity, bias=w("bk")).then_inc(qk_sb, 1)
                act.wait_ge(qk_sb, 2)
                A(PARTS[:, 0:2, 0, :], F3[:, 0:2, :], ACT.Copy).then_inc(hi_ready, 1)
                ffn_tanh(0)
                act.wait_ge(rest2_ready, 1)
                A(PARTS[:, 0:2, 1, :], R3[:, 0:2, :], ACT.Copy).then_inc(mid_ready, 1)
                act.wait_ge(kf_ready, 2)
                A(PARTS[:, 2, 0, :], F3[:, 2, :], ACT.Copy).then_inc(hi_ready, 2)
                act.wait_ge(qmin_ready, 1)
                A(QEX, QMIN, ACT.Exp).then_inc(qexp_ready, 1)
                act.wait_ge(rest_ready, 1)
                A(PARTS[:, 2, 1, :], R3[:, 2, :], ACT.Copy).then_inc(mid_ready, 1)
                act.wait_ge(parts_ready, 1)
                act.wait_ge(qeo_zero, 1)
                for a in range(2):
                    last = A(QEO[:, a, :, a::2], PARTS[:, 0, :, a::2], ACT.Copy)
                last.then_inc(qeo_ready, 1)
                ffn_tanh(1)
                ffn_tanh(2)
                act.wait_ge(rdm_ready, 1)
                A(e2[:, :], dm[:, :], ACT.Exp).then_inc(rexp_ready, 1)
                for s in range(3, FFN_BEFORE):
                    ffn_tanh(s)
                for i in range(NSLOT0):
                    if i < SLOTS0:
                        tile = region(i % RING * TILE, TILE).rearrange("p (h q) -> p h q", h=H)
                        if i >= RING:
                            act.wait_ge(pv_done, i - RING + 1)
                        for g in range(G2):
                            n = G2 * i + g
                            act.wait_ge(sc_ps, n + 1)
                            A(tile[:, :, g * NQ:(g + 1) * NQ], bank(B_S + n % NSB).rearrange("p (h q) -> p h q", h=H),
                              ACT.Copy).then_inc(sc_copied, 1)
                            if g == 0 and i - 1 in FFN_AT:
                                ffn_tanh(FFN_AT[i - 1])
                    if i >= SLOTS0 and i - 1 in FFN_AT:
                        ffn_tanh(FFN_AT[i - 1])
                    for v in range(NU):
                        if 0 <= i - T * v - AT_EXP < T:
                            exp_tile(v, i - T * v - AT_EXP)
                        if i == T * v + AT_EVAC:
                            act.wait_ge(pv_done, T * v + T)
                            if v >= 2:
                                act.wait_ge(nat_ps, v // 2)
                            A(CTX[:, :, v % 2 * UQ:(v % 2 + 1) * UQ], bank(B_PV, 2 * UQ).rearrange("p (a q) -> p a q", a=2),
                              ACT.Copy).then_inc(ctx_ready, 1)
                act.wait_ge(fo_used, E + 1)
                A(TH[:, :], ACC[:, :, :].rearrange("p t d -> p (t d)"), ACT.Tanh, scale=0.5).then_inc(ga_ready, 1)

                from_layer0_to_1(act, b)
                for n, t in enumerate(ORDER1):
                    act.wait_ge(phi_ps, n + 1)
                    A(TP[:, t, :], bank(B_S + n), ACT.Tanh).then_inc(tp_sb, 1)
                for n, t in enumerate(ORDER1):
                    act.wait_ge(amp_ps, n + 1)
                    A(NAB[:, t, :], bank(AMP_BANK[t]), ACT.Abs).then_inc(abz_r, 1)
                for n, t in enumerate(ORDER1):
                    act.wait_ge(abz_r, n + 1)
                    A(EX[:, t, :], NAB[:, t, :], ACT.Exp, scale=-1.0).then_inc(ex_r, 1)
                act.wait_ge(tp_sb, 2)
                A(ATP, TP, ACT.Abs).then_inc(abs_r, 1)
                act.wait_ge(lge_r, 1)
                A(EQ[:, :, :], KEY[:, :, :], ACT.Exp).then_inc(lgx_r, 1)

                def tanh1(s):
                    act.wait_ge(hu1_ps, s + 1)
                    if s:
                        act.wait_ge(h1_r, s)
                    A(TH[:, :], bank(B_H), ACT.Tanh, scale=0.5).then_inc(th1_r, 1)

                def expert_act(e):
                    act.wait_ge(hu1_ps, 3 + e)
                    if e == 0:
                        act.wait_ge(h1_r, 2)
                    else:
                        act.wait_ge(sig1_r, e)
                    A(TH[:, :], bank(B_H), ACT.Tanh, scale=0.5, bias=hb1[:, e:e + 1]).then_inc(th1_r, 1)
                    if e >= 2:
                        act.wait_ge(y_c, e - 1)
                    elif e == 0:
                        act.wait_ge(fo1_ps, 1)
                    A(C3[e % 2], bank(B_U), ACT.Identity, bias=w("b3", e, 1)).then_inc(c3_r, 1)
                    act.wait_ge(th1_r, 3 + e)
                    if e:
                        act.wait_ge(he_r, e)
                    A(AA[:, :], TH[:, :], ACT.Identity, scale=0.5, bias=halfc).then_inc(sig1_r, 1)

                tanh1(0)
                act.wait_ge(abs_r, 1)
                A(SI, TP, ACT.Sin, scale=pi).then_inc(cos_r, 1)
                A(CO, ATP, ACT.Sin, scale=-pi, bias=w("halfpi")).then_inc(cos_r, 1)
                for n, t in enumerate(ORDER1):
                    act.wait_ge(u_r, n + 1)
                    A(LNU[:, t, :], U1[:, t, :], ACT.Ln).then_inc(ln_r, 1)
                for n, t in enumerate(ORDER1):
                    act.wait_ge(amp_r, n + 1)
                    A(SQ[:, t, :], EX[:, t, :], ACT.Square).then_inc(sq_r, 1)
                for n, t in enumerate(ORDER1):
                    act.wait_ge(msq_ps, n + 1)
                    A(RT[:, t, :], bank(B_S + n), ACT.Ln, bias=epsc).then_inc(lnsq_r, 1)
                for n, t in enumerate(ORDER1):
                    act.wait_ge(lnsq_r, n + 1)
                    A(RT[:, t, :], RT[:, t, :], ACT.Exp, scale=-0.5, **({} if t else {"bias": qbias})).then_inc(rt_r, 1)
                tanh1(1)
                for n, t in enumerate(ORDER1):
                    act.wait_ge(cs_r, n + 1)
                    A(PARTS1[:, t, 0, :, :], CS4[:, t, :, :], ACT.Copy).then_inc(hi1_r, 1)
                for n, t in enumerate(ORDER1):
                    act.wait_ge(rest1_r, n + 1)
                    A(PARTS1[:, t, 1, :, :], R4[:, t, :, :], ACT.Copy).then_inc(mid1_r, 1)
                for e in range(6):
                    expert_act(e)

                def exp1(n):
                    for c, (at, width) in enumerate(((0, 512), (512, 384), (896, 384))):
                        act.wait_ge(s2_ps, 3 * n + c + 1)
                        if n >= 8 and c == 0:
                            act.wait_ge(pv1, n // 4 - 1)
                        A(PL[:, n // 4 % 2, n % 4, at:at + width], bank(B_S + c, width), ACT.Exp).then_inc(p1_r, 1)

                for gq in range(4):
                    for j in range(4):
                        exp1(4 * gq + j)
                        for e, (_, at_act, _) in PASS2_AT.items():
                            if 4 * gq + j == at_act:
                                expert_act(e)
                    if gq == 2:
                        act.wait_ge(pv1, 2)
                        A(CT1[:, 0, :], bank(B_PV), ACT.Copy).then_inc(ctx1, 1)
                act.wait_ge(pv1, 4)
                A(CT1[:, 1, :], bank(B_PV), ACT.Copy).then_inc(ctx1, 1)
                act.wait_ge(yt_ps, 1)
                act.wait_ge(he_r, E)
                A(TH[:, :], bank(B_O), ACT.Tanh, scale=0.5).then_inc(ga1, 1)
                end_sequence(act, b)

        @block.vector
        def _(dve):
            V = nc.vector
            steps = [0]

            def link(ins):
                steps[0] += 1
                ins.then_inc(chain_dve, 1)
                dve.wait_ge(chain_dve, steps[0])

            dve.wait_ge(s_wa, 16)
            dve.wait_ge(s_gexp, 1)
            link(V.tensor_scalar(gate_s, gate_e, 1.0, None, ALU.add))
            link(V.reciprocal(gate, gate_s))
            V.tensor_scalar(omg, gate, -1.0, 1.0, ALU.mult, ALU.add)
            V.tensor_scalar(GBV[:, :], w("bv"), gate, None, ALU.mult)
            V.tensor_scalar(qbias, w("sls"), -0.5 * log(HD), None, ALU.add)
            V.memset(epsc, 1e-6)
            V.memset(halfc, 0.5)
            V.memset(KS[ROWS:P, :, :, :], 1.0)
            V.memset(ET[ROWS:P, :], 0.0)
            V.tensor_scalar(hb1[:, :], w("b1"), 0.5, None, ALU.mult)
            V.tensor_copy(IDB[:, :], w("ident"))
            V.tensor_copy(MKN[:, :], w("maskn"))
            link(V.tensor_copy(MKT[:, :], w("maskt")))
            dve.wait_ge(s_et, 16)
            ep = HH[0:2 * HD, 0, :, :].rearrange("p a s -> p (a s)").bitcast(BF16)[:, 0:3 * S].rearrange("p (c s) -> p c s", c=3)
            e_f, e_r = TH[0:2 * HD, :], AA[0:2 * HD, :]
            link(V.tensor_copy(ep[:, 0, :], e_f))
            link(V.tensor_tensor(e_r, e_f, ep[:, 0, :], ALU.subtract))
            link(V.tensor_copy(ep[:, 1, :], e_r))
            V.tensor_tensor(ep[:, 2, :], e_r, ep[:, 1, :], ALU.subtract).then_inc(s_etp, 1)
            dve.wait_ge(s_etp, 1)
            dve.wait_ge(s_etd, 16)
            V.engine_nop().then_inc(s_pre_dve, 1)
            dve.wait_ge(s_pre_dve, 1)
            dve.wait_ge(s_pre_pool, 5)

            def norm_stats(done, src=X):
                for t in range(T):
                    last = V.bn_stats(st[:, t, :], src[:, t, :])
                link(last)
                for t in range(T):
                    last = V.bn_aggr(mv[:, t, :], st[:, t, :])
                link(last)
                V.tensor_scalar(ve[:, :], mv[:, :, 1], LN_EPS, None, ALU.add).then_inc(done, 1)

            def norm_apply(rstd, done, src=X, to=XN):
                dve.wait_ge(rstd, 1)
                for t in range(T):
                    last = V.tensor_scalar(to[:, t, :], src[:, t, :], mv[:, t, 0:1], rs[:, t:t + 1], ALU.subtract, ALU.mult)
                last.then_inc(done, 1)

            def set_v(ready, done):
                dve.wait_ge(ready, 1)
                v = bank(B_O).rearrange("p (a two d) -> p a two d", two=2, d=HD)
                o = VP[:, :, :, :].rearrange("p t (a two) c -> p (t a) two c", two=2)
                for two in range(2):
                    last = V.tensor_copy(o[:, :, two, 8 * two:8 * two + 8], v[:, :, two, :])
                last.then_inc(done, 1)

            def over(v):
                return v[:, :, None].to_broadcast([P, T, E])

            idx = w("idx")[:, None, :].to_broadcast([P, T, E])

            def first_max(a, m, oh):
                link(V.tensor_reduce(m, a, AX.X, ALU.max))
                link(V.tensor_tensor(KEY[:, :, :], a, over(m), ALU.is_equal))
                link(V.tensor_tensor(KEY[:, :, :], KEY[:, :, :], idx, ALU.mult))
                link(V.tensor_reduce(km[:, :], KEY[:, :, :], AX.X, ALU.max))
                link(V.tensor_tensor(oh, KEY[:, :, :], over(km), ALU.is_equal))

            def without(a, oh):
                link(V.scalar_tensor_tensor(out=a, in0=oh, scalar=-3e38, in1=a, op0=ALU.mult, op1=ALU.add))

            def split(full, rest, parts):
                link(V.tensor_copy(parts[0], full))
                link(V.tensor_tensor(rest, full, parts[0], ALU.subtract))
                link(V.tensor_copy(parts[1], rest))
                return V.tensor_tensor(parts[2], rest, parts[1], ALU.subtract)

            def ffn_hh(s):
                e, fi = s // 2, s % 2
                dve.wait_ge(th_ready, s + 1)
                link(V.scalar_tensor_tensor(out=AA[:, :], in0=TH[:, :], scalar=1.0, in1=bank(ffn_banks(s)[0]), op0=ALU.add, op1=ALU.mult))
                if e >= 2:
                    dve.wait_ge(fo_ps, e - 1)
                V.tensor_tensor(HH[:, e % 2, fi, :], AA[:, :], bank(ffn_banks(s)[1]), ALU.mult).then_inc(hh_ready, 1)
                dve.wait_ge(hh_ready, s + 1)

            def ffn_acc(e):
                dve.wait_ge(fo_ps, e + 1)
                if e == 0:
                    link(V.tensor_scalar(ACC[:, :, :].rearrange("p t d -> p (t d)"), bank(B_O), 0.5, None, ALU.mult))
                else:
                    for t in range(T):
                        last = V.scalar_tensor_tensor(out=ACC[:, t, :], in0=bank(B_O, P, t * P), scalar=W8[:, t, e - 1:e],
                                                      in1=ACC[:, t, :], op0=ALU.mult, op1=ALU.add)
                    link(last)
                V.engine_nop().then_inc(fo_used, 1)

            def ffn_dve(s):
                ffn_hh(s)
                if s >= 2 and s % 2 == 0:
                    ffn_acc(s // 2 - 1)

            def silu_mix(th_done, f, s_attn, done):
                dve.wait_ge(th_done, 1)
                link(V.scalar_tensor_tensor(out=AA[:, :], in0=TH[:, :], scalar=1.0, in1=f, op0=ALU.add, op1=ALU.mult))
                link(V.tensor_tensor(AA[:, :], AA[:, :], s_attn, ALU.mult))
                xf = X[:, :, :].rearrange("p t d -> p (t d)")
                return V.scalar_tensor_tensor(out=xf, in0=AA[:, :], scalar=0.5, in1=xf, op0=ALU.mult, op1=ALU.add)

            dve.wait_ge(x_first, 16)
            norm_stats(first_norm, XN)
            dve.wait_ge(first_norm, 2)
            norm_apply(first_norm, first_norm, XN, XZ)
            dve.wait_ge(first_norm, 4)
            V.tensor_copy(XT[:, :], bank(B_U)).then_inc(first_norm, 1)
            dve.wait_ge(first_norm, 5)
            dve.nop(nofuse=True)
            dve.sem_clear(chain_dve)
            with dve.Fori(0, B) as b:
                steps[0] = 0
                dve.wait_ge(hi_ready, 1)
                link(V.tensor_tensor(R3[:, 0:2, :], F3[:, 0:2, :], PARTS[:, 0:2, 0, :], ALU.subtract))
                V.engine_nop().then_inc(rest2_ready, 1)
                set_v(proj_v, v_set)
                ffn_dve(0)
                dve.wait_ge(mid_ready, 1)
                V.tensor_tensor(PARTS[:, 0:2, 2, :], R3[:, 0:2, :], PARTS[:, 0:2, 1, :], ALU.subtract).then_inc(parts_ready, 1)
                ffn_dve(1)
                dve.wait_ge(logit_ps, 1)
                V.tensor_copy(LG[:, :, :], bank(B_PV, T * E).rearrange("p (t e) -> p t e", e=E)).then_inc(logits_read, 1)
                dve.wait_ge(logits_read, 1)
                first_max(LG[:, :, :], m1[:, :], OH1[:, :, :])
                without(LG[:, :, :], OH1[:, :, :])
                first_max(LG[:, :, :], m2[:, :], OH2[:, :, :])
                V.tensor_tensor(dm[:, :], m2[:, :], m1[:, :], ALU.subtract).then_inc(rdm_ready, 1)
                ffn_dve(2)
                dve.wait_ge(rexp_ready, 1)
                link(V.tensor_scalar(w1[:, :], e2[:, :], 1.0, 2.0, ALU.add, ALU.mult))
                link(V.reciprocal(w1[:, :], w1[:, :]))
                link(V.tensor_tensor(w2[:, :], w1[:, :], e2[:, :], ALU.mult))
                link(V.tensor_tensor(OH1[:, :, :], OH1[:, :, :], over(w1), ALU.mult))
                link(V.tensor_tensor(OH2[:, :, :], OH2[:, :, :], over(w2), ALU.mult))
                link(V.tensor_tensor(W8[:, :, :], OH1[:, :, :], OH2[:, :, :], ALU.add))
                dve.wait_ge(glob_ps, 1)
                gl = [bank(B_S + a, 2 * (D + H)).rearrange("p (t c) -> p t c", t=2) for a in range(2)]
                den = RDN[:, :].rearrange("p (t h) -> p t h", t=T)
                for a in range(2):
                    last = V.tensor_scalar(den[:, 2 * a:2 * a + 2, :], gl[a][:, :, D:D + H], 1e-6, None, ALU.add)
                link(last)
                link(V.reciprocal(RDN[:, :], RDN[:, :]))
                link(V.tensor_scalar(RDN[:, :], RDN[:, :], omg, None, ALU.mult))
                for a in range(2):
                    last = V.tensor_tensor(G[:, 2 * a:2 * a + 2, :].rearrange("p t (h d) -> p t h d", h=H),
                                           gl[a][:, :, 0:D].rearrange("p t (h d) -> p t h d", h=H),
                                           den[:, 2 * a:2 * a + 2, :, None].to_broadcast([P, 2, H, HD]), ALU.mult)
                last.then_inc(gn_ready, 1)
                for s in range(3, FFN_BEFORE):
                    ffn_dve(s)
                dve.wait_ge(out_done, b * 16)
                dve.nop(nofuse=True)
                V.tensor_copy(X[:, :, :], XN[:, :, :]).then_inc(x_kept, 1)
                dve.wait_ge(x_kept, 1)
                for i in range(NSLOT0):
                    if i < SLOTS0:
                        u, kb = i // T, i % T
                        tile = region(i % RING * TILE, TILE)
                        dve.wait_ge(sc_copied, G2 * (i + 1))
                        if kb == 0 and u:
                            dve.wait_ge(m1_ready, u)
                        V.tensor_reduce(R1[:, kb, :], tile.rearrange("p (a c) -> p a c", c=32), AX.X, ALU.max,
                                        apply_transpose=True).then_inc(red_done, 1)
                        if kb == T - 1:
                            dve.wait_ge(red_done, i + 1)
                            if u:
                                dve.wait_ge(mt_ps, u)
                            V.tensor_reduce(M1[:, 0:H * G2], R1[:, :, :].rearrange("p k c -> p c k"), AX.X, ALU.max
                                            ).then_inc(m1_ready, 1)
                    for v in range(NU):
                        if i == T * v + AT_MAX:
                            dve.wait_ge(mt_ps, v + 1)
                            if v:
                                dve.wait_ge(dm_out, 16 * v)
                            V.tensor_reduce(M2[:, :], PS[0:H * G2, B_MISC, 0:P].rearrange("c (a i) -> c i a", i=NQ),
                                            AX.X, ALU.max).then_inc(m2_ready, 1)
                        if i == T * v + AT_SUB:
                            tile = region(T * v % RING * TILE, TILE)
                            dve.wait_ge(mb_in[v % 2], 16 * (v // 2 + 1))
                            V.tensor_tensor(tile, tile, MB[:, v % 2, :], ALU.subtract).then_inc(sub_dve, 1)
                    if i - 1 in FFN_AT:
                        ffn_hh(FFN_AT[i - 1])
                    if i - 3 in FFN_AT and FFN_AT[i - 3] >= 2 and FFN_AT[i - 3] % 2 == 0:
                        ffn_acc(FFN_AT[i - 3] // 2 - 1)
                    for c in range(T):
                        if i == 2 * T * c + AT_NATURAL:
                            dve.wait_ge(nat_ps, c + 1)
                            n = bank(B_MISC, 2 * P).rearrange("p (a two d) -> p a two d", two=4, d=HD)
                            rd = RDN[:, 0:H].rearrange("p (a two) -> p a two", two=2)
                            link(V.reciprocal(rd, n[:, :, 2:4, 0]))
                            link(V.tensor_scalar(RDN[:, 0:H], RDN[:, 0:H], gate, None, ALU.mult))
                            if c:
                                dve.wait_ge(back_ps, c)
                            cn = CN[:, :].rearrange("p (a two d) -> p a two d", two=2, d=HD)
                            link(V.tensor_tensor(cn, n[:, :, 0:2, :], rd[:, :, :, None].to_broadcast([P, H // 2, 2, HD]), ALU.mult))
                            if c == 0:
                                dve.wait_ge(g_ready, 1)
                            V.tensor_tensor(CN[:, :], CN[:, :], G[:, c, :], ALU.add).then_inc(cn_ready, 1)
                        if i == 2 * T * c + AT_BACK:
                            dve.wait_ge(back_ps, c + 1)
                            V.tensor_copy(CT[:, :], bank(B_MISC, P)).then_inc(ct_ready, 1)
                        if i == 2 * T * c + AT_OUT:
                            dve.wait_ge(at_ps, c + 1)
                            V.tensor_tensor(SS[:, c, :], bank(B_MISC, P), w("bo"), ALU.add).then_inc(ss_ready, 1)
                ffn_acc(E)
                dve.wait_ge(ss_ready, T)
                link(silu_mix(ga_ready, ACC[:, :, :].rearrange("p t d -> p (t d)"), SS[:, :, :].rearrange("p t d -> p (t d)"), None))

                from_layer0_to_1(dve, b)
                norm_stats(var1)
                norm_apply(rstd1, xn1)
                dve.wait_ge(xt_ps1, 1)
                V.tensor_copy(XT[:, :], bank(B_MISC)).then_inc(xt1, 1)
                dve.wait_ge(lg_ps1, 1)
                V.tensor_copy(LG[:, :, :], bank(B_PV, T * E).rearrange("p (t e) -> p t e", e=E)).then_inc(lg_read1, 1)
                dve.wait_ge(lg_read1, 1)
                link(V.tensor_reduce(m1[:, :], LG[:, :, :], AX.X, ALU.max))
                V.tensor_tensor(KEY[:, :, :], LG[:, :, :], over(m1), ALU.subtract).then_inc(lge_r, 1)
                for n, t in enumerate(ORDER1):
                    dve.wait_ge(ex_r, n + 1)
                    V.tensor_scalar(U1[:, t, :], EX[:, t, :], 1.0, None, ALU.add).then_inc(u_r, 1)
                for n, t in enumerate(ORDER1):
                    dve.wait_ge(u_r, n + 1)
                    V.scalar_tensor_tensor(out=C1[:, t, :], in0=U1[:, t, :], scalar=-1.0, in1=EX[:, t, :],
                                           op0=ALU.add, op1=ALU.subtract).then_inc(c1_r, 1)

                def shared_hh(s):
                    dve.wait_ge(th1_r, s + 1)
                    link(V.scalar_tensor_tensor(out=AA[:, :], in0=TH[:, :], scalar=1.0, in1=bank(B_H), op0=ALU.add, op1=ALU.mult))
                    link(V.tensor_scalar(AA[:, :], AA[:, :], 0.5, None, ALU.mult))
                    V.tensor_tensor(HH[:, 0, s, :], AA[:, :], bank(B_U), ALU.mult).then_inc(h1_r, 1)
                    dve.wait_ge(h1_r, s + 1)

                shared_hh(0)
                set_v(v_ps1, v_set1)
                dve.wait_ge(lgx_r, 1)
                link(V.tensor_reduce(m2[:, :], EQ[:, :, :], AX.X, ALU.add))
                link(V.reciprocal(m2[:, :], m2[:, :]))
                link(V.tensor_tensor(LG[:, :, :], EQ[:, :, :], over(m2), ALU.mult))
                link(V.tensor_copy(WM[:, :, :], LG[:, :, :]))
                first_max(LG[:, :, :], m1[:, :], OH1[:, :, :])
                for n, t in enumerate(ORDER1):
                    dve.wait_ge(ln_r, n + 1)
                    dve.wait_ge(c1_r, n + 1)
                    link(V.tensor_tensor(C1[:, t, :], LNU[:, t, :], C1[:, t, :], ALU.subtract))
                    V.scalar_tensor_tensor(out=EX[:, t, :], in0=bank(AMP_BANK[t]), scalar=0.0, in1=C1[:, t, :],
                                           op0=ALU.max, op1=ALU.add).then_inc(amp_r, 1)
                without(LG[:, :, :], OH1[:, :, :])
                first_max(LG[:, :, :], m2[:, :], OH2[:, :, :])
                link(V.tensor_tensor(WMK[:, :, E:2 * E], OH1[:, :, :], OH2[:, :, :], ALU.add))
                V.tensor_tensor(WMK[:, :, 0:E], WM[:, :, :], WMK[:, :, E:2 * E], ALU.mult).then_inc(wm_r, 1)
                dve.wait_ge(cos_r, 2)
                dve.wait_ge(amp_r, 2)
                for n, t in enumerate(ORDER1):
                    V.tensor_tensor(CS4[:, t, 0, :], EX[:, t, :], CO[:, t, :], ALU.mult)
                    last = V.tensor_tensor(CS4[:, t, 1, :], EX[:, t, :], SI[:, t, :], ALU.mult)
                link(last)
                for n, t in enumerate(ORDER1):
                    dve.wait_ge(rt_r, n + 1)
                    V.tensor_tensor(CS4[:, t, :, :], CS4[:, t, :, :], RT[:, t, None, :].to_broadcast([P, 2, S]), ALU.mult
                                    ).then_inc(cs_r, 1)
                dve.wait_ge(wt_ps, 1)
                V.tensor_copy(WT[:, :], PS[0:2 * E, B_PV, :]).then_inc(wt_r, 1)
                for n, t in enumerate(ORDER1):
                    dve.wait_ge(hi1_r, n + 1)
                    dve.wait_ge(cs_r, n + 1)
                    V.tensor_tensor(R4[:, t, :, :], CS4[:, t, :, :], PARTS1[:, t, 0, :, :], ALU.subtract).then_inc(rest1_r, 1)
                for n, t in enumerate(ORDER1):
                    dve.wait_ge(mid1_r, n + 1)
                    dve.wait_ge(rest1_r, n + 1)
                    V.tensor_tensor(PARTS1[:, t, 2, :, :], R4[:, t, :, :], PARTS1[:, t, 1, :, :], ALU.subtract).then_inc(parts1, 1)
                shared_hh(1)
                dve.wait_ge(fo1_ps, 1)
                V.tensor_copy(YT[:, :], bank(B_O)).then_inc(yn_r, 1)

                def expert_h(e):
                    dve.wait_ge(sig1_r, e + 1)
                    dve.wait_ge(fo1_ps, e + 1)
                    V.scalar_tensor_tensor(out=HE, in0=bank(B_H), scalar=w("b1", e, 1), in1=AA[:, :],
                                           op0=ALU.add, op1=ALU.mult).then_inc(he_r, 1)

                def expert_y(e):
                    dve.wait_ge(fo1_ps, e + 2)
                    dve.wait_ge(c3m_r, e + 1)
                    if e >= 2:
                        dve.wait_ge(y_add, e - 1)
                    V.scalar_tensor_tensor(out=CC[:, e % 2, :], in0=bank(B_O), scalar=w("b2", e, 1), in1=C3[e % 2],
                                           op0=ALU.add, op1=ALU.mult).then_inc(y_c, 1)

                for e in range(2):
                    expert_h(e)
                    expert_y(e)
                n = 0
                for tile in range(T):
                    per = (4, 2, 1, 1)[tile]
                    for h0 in range(0, H, per):
                        width = (tile + 1) * P
                        dve.wait_ge(s1_ps, n + 1)
                        V.tensor_reduce(M1[:, :].rearrange("p (h t) -> p h t", t=T)[:, h0:h0 + per, tile],
                                        bank(B_S + n % NSB, per * width).rearrange("p (a k) -> p a k", k=width),
                                        AX.X, ALU.max).then_inc(s1_max, 1)
                        n += 1
                        for e, (_, at_h, _, at_y) in PASS1_AT.items():
                            if n == at_h:
                                expert_h(e)
                            if n == at_y:
                                expert_y(e)
                dve.wait_ge(nmt_ps, 1)
                link(V.tensor_scalar(NM[:, :], PS[0:H * T, B_MISC, 0:P], -1.0, None, ALU.mult))
                split(NM[:, :], NR[:, :], [NMP[:, c, :] for c in range(3)]).then_inc(nm_r, 1)
                for e in range(5, E):
                    expert_h(e)
                    expert_y(e)
                dve.wait_ge(x_next, 16)
                norm_stats(var_next, XN)
                norm_apply(rstd_next, xn_next, XN, XZ)
                dve.wait_ge(xs_r, E)
                dve.wait_ge(xt_next_ps, 1)
                V.tensor_copy(XT[:, :], bank(B_U)).then_inc(xt_next, 1)
                rd1 = RDN[:, 0:2 * H].rearrange("p (a two) -> p a two", two=2)
                for a in range(2):
                    dve.wait_ge(nat1_ps, a + 1)
                    n1 = bank((B_MISC, B_H)[a]).rearrange("p (a two d) -> p a two d", two=4, d=HD)
                    link(V.reciprocal(rd1, n1[:, :, 2:4, 0]))
                    link(V.tensor_tensor(CN1[:, 2 * a:2 * a + 2, :].rearrange("p t (a two d) -> p (t a) two d", two=2, d=HD),
                                         n1[:, :, 0:2, :], rd1[:, :, :, None].to_broadcast([P, H, 2, HD]), ALU.mult))
                    V.engine_nop().then_inc(cn1, 1)
                dve.wait_ge(back1_ps, 1)
                V.tensor_copy(CTT, bank(B_U)).then_inc(ctt_r, 1)
                dve.wait_ge(ga1, 1)
                V.scalar_tensor_tensor(out=AA[:, :], in0=TH[:, :], scalar=1.0, in1=bank(B_O), op0=ALU.add, op1=ALU.mult
                                       ).then_inc(y1_r, 1)
                dve.wait_ge(y1_r, 1)
                dve.wait_ge(at1_ps, 1)
                link(V.tensor_tensor(AA[:, :], AA[:, :], bank(B_PV), ALU.mult))
                xf = X[:, :, :].rearrange("p t d -> p (t d)")
                V.scalar_tensor_tensor(out=xf, in0=AA[:, :], scalar=0.5, in1=xf, op0=ALU.mult, op1=ALU.add).then_inc(xo_r, 1)
                dve.wait_ge(xo_r, 1)
                end_sequence(dve, b)
                dve.sem_clear(chain_dve)


def kernel(**inputs):
    import concourse.bacc as bacc
    from concourse.bass_utils import run_bass_kernel_spmd as run

    g = {k: np.asarray(v) for k, v in inputs.items()}

    def col(v):
        return np.asarray(v).reshape(P, 1)

    by_dim = np.arange(D).reshape(H, HD).T.ravel()

    def a0(n):
        return g["L0_attn_" + n]

    def f0(n):
        return g["L0_ffn_" + n]

    def a1(n):
        return g["L1_attn_" + n]

    def f1(n):
        return g["L1_ffn_" + n]

    zero = np.zeros((), np.float32)
    mbd = np.zeros((P, P), np.float32)
    zh = np.zeros((P, H), np.float32)
    for h in range(H):
        r = slice(h * HD, h * HD + HD)
        mbd[r, r] = a0("M")[h]
        zh[r, h] = a0("z")[h]

    mean8 = np.kron(np.full((HD, HD), 1 / HD), np.eye(H)).astype(np.float32)
    maskn = np.triu(np.full((P, P), NEG, np.float32), 1)

    def rows(v):
        return np.broadcast_to(v[None, :], (P, v.shape[0]))

    def two(v):
        return v.reshape(2, P, -1).transpose(1, 0, 2).reshape(P, -1)

    rel = a0("rel_emb")
    parts = {
        "WqT": a0("Wq").T[:, by_dim], "WkT": a0("Wk").T[:, by_dim], "WvT": a0("Wv").T, "gate0": f0("gate_w"), "MZ": np.concatenate([mbd, zh], 1)[by_dim],
        "ident": np.eye(P, dtype=np.float32), "idx": rows(np.arange(E, 0, -1).astype(np.float32)),
        "bq": col(a0("bq")[by_dim]), "bk": col(a0("bk")[by_dim]), "bv": rows(a0("bv")),
        "e_near": col(np.repeat(rel[2 * REL], H)), "e_far": col(np.repeat(rel[0], H)),
        "alpha": np.broadcast_to(a0("gate_alpha").reshape(1, 1), (P, 1)), "sls": col(np.tile(a1("score_log_scale"), HD)),
        "halfpi": np.full((P, 1), pi / 2, np.float32),
        "b1": f1("b1").T, "b2": f1("b2").T, "b3": f1("b3").T, "mean8": mean8, "maskn": maskn, "maskt": maskn.T,
        "bo": rows(a0("bo")), "WoT": a0("Wo").T,
        "sw1": f0("sw1"), "sw2": f0("sw2"), "sw3": two(f0("sw3")),
        "ew1": f0("ew1").transpose(1, 0, 2).reshape(D, -1), "ew2": f0("ew2").transpose(1, 0, 2).reshape(D, -1),
        "ew3": f0("ew3").reshape(E, 2, P, D).transpose(2, 0, 1, 3).reshape(P, -1),
        "Wqa": a1("Wq_amp").T[:, by_dim], "Wka": a1("Wk_amp").T[:, by_dim], "Wqp": a1("Wq_phi").T[:, by_dim],
        "Wkp": a1("Wk_phi").T[:, by_dim], "Wv1": a1("Wv").T,
        "WoT1": a1("Wo").T, "gate1": f1("gate_w").T,
        "tw1": f1("w1").transpose(2, 0, 1).reshape(D, -1), "tw2": f1("w2").transpose(2, 0, 1).reshape(HID, -1),
        "tw3": f1("w3").transpose(2, 0, 1).reshape(D, -1),
        "tsw1": f1("sw1").T, "tsw2": f1("sw2").T, "tsw3": two(f1("sw3").T),
    }

    def pack(cols):
        return np.ascontiguousarray(np.concatenate([parts[n].reshape(P, k) for n, k in cols], 1, dtype=np.float32))

    j = np.arange(4 * P)
    etab = np.concatenate([rel[np.clip(q - (j - 2 * P), -REL, REL) + REL].T for q in range(2)], 0)
    x = a0("hidden_states").reshape(B * S, D)
    x = np.concatenate([x, x[:S]])
    arrays = {
        "x": x, "wa": pack(COLS_A), "wb": pack(COLS_B),
        "wc": pack(COLS_C), "etab": np.ascontiguousarray(etab),
    }
    nc = bacc.Bacc("TRN2", target_bir_lowering=False, num_devices=1)
    args = [nc.dram_tensor(n, a.shape, mybir.dt.from_np(a.dtype), kind="ExternalInput").ap() for n, a in arrays.items()]
    args.append(nc.dram_tensor("out", (B * S, D), F32, kind="ExternalOutput").ap())
    program(nc, *args)
    r = run(nc, [arrays], core_ids=[0])
    return r.results[0]["out"].reshape(B, S, D)
```

```python
from contextlib import ExitStack
from math import log, pi, sqrt

import numpy as np
import concourse.bass as bass
from concourse import mybir

F32 = mybir.dt.float32
BF16 = mybir.dt.bfloat16
ALU = mybir.AluOpType
ACT = mybir.ActivationFunctionType
AX = mybir.AxisListType

P = 128
B, S, D = 4, 512, 128
H, HD = 16, 8
T = S // P
E = 8
F0 = 256
HID = 128
REL = 128
NQ = 32
UQ = 64
NU = S // UQ
G2 = UQ // NQ
SLOTS = 6
ROWS = 2 * SLOTS * HD
Q_RUNS = ((0, 3), (3, 2), (5, 1))
K_RUNS = ((0, 3, 0), (3, 2, 1), (5, 1, 2))
RING = 14
TILE = H * UQ
NEG = -1e30
LN_EPS = 1e-5
BF16_ONES = float(np.array(0x3F803F80, np.uint32).view(np.float32))
X_GROUPS = (range(T - 1), range(T - 1, T))

B_H, B_U, B_O, B_PV, B_MISC, B_S = 0, 1, 2, 3, 4, 5
NSB = 3
AMP_BANK = (B_S + 2, B_MISC)

COLS_A = [("WqT", D), ("WkT", D), ("WvT", D), ("gate0", E), ("MZ", D + H), ("ident", P), ("idx", E),
          ("bq", 1), ("bk", 1), ("e_near", 1), ("e_far", 1), ("alpha", 1), ("sls", 1), ("halfpi", 1),
          ("b1", E), ("b2", E), ("b3", E), ("mean8", P), ("maskn", P), ("maskt", P), ("bo", D), ("bv", D),
          ("WoT", D), ("sw1", F0), ("sw2", F0), ("sw3", 2 * D)]
COLS_B = [("ew1", E * F0), ("ew2", E * F0), ("ew3", E * 2 * D)]
COLS_C = [("Wqa", D), ("Wka", D), ("Wqp", D), ("Wkp", D), ("Wv1", D), ("WoT1", D), ("gate1", E),
          ("tw1", E * HID), ("tw2", E * D), ("tw3", E * HID), ("tsw1", F0), ("tsw2", F0), ("tsw3", 2 * D)]


def ffn_banks(s):
    return (B_S + 2, B_MISC) if s < FFN_BEFORE and s % 2 else (B_H, B_U)


def expert_banks(e):
    return (B_S, B_S + 1) if e < WINDOW and e % 2 else (B_H, B_U)


BANKS1 = [(tile, h0, (4, 2, 1, 1)[tile]) for half_ in range(2) for tile in range(T)
          for h0 in range(8 * half_, 8 * half_ + 8, (4, 2, 1, 1)[tile])]


def bank1(n):
    return B_S + n % NSB if n < HALF_BANKS else (B_S, B_MISC)[n % 2]


def bank2(i):
    return (B_S + 1, B_S + 2)[i % 2] if i < 24 else (B_S + 1, B_S + 2, B_S, B_MISC)[i % 4]


def users_before(bank_of, n):
    return max([i + 1 for i in range(n) if bank_of(i) == bank_of(n)], default=0)


def offsets(cols):
    at, out = 0, {}
    for name, n in cols:
        out[name] = (at, n)
        at += n
    return out, at


OFF_A, NA = offsets(COLS_A)
OFF_B, NB = offsets(COLS_B)
OFF_C, NC = offsets(COLS_C)

SLOTS0 = NU * T
AT_MAX, AT_SUB, AT_EXP, AT_PV, AT_EVAC = 4, 9, 8, 9, 12
AT_NATURAL, AT_BACK, AT_OUT = 17, 18, 19
NSLOT0 = (NU - 2) * T + AT_OUT + 1
FFN_BEFORE = 10
ORDER1 = (1, 0)
HALF_BANKS = 22
NM_AT = (24, 44)
HEAD_AT = {(33, 35, 37, 38, 41, 43)[n] if n < 6 else 38 + n: n for n in range(16)}
NSLOT1 = 54
EXPERT_AT = {3: (2, 6, 9, 11), 4: (10, 14, 17, 19), 5: (20, 24, 27, 29), 6: (29, 33, 36, 38), 7: (45, 46, 47, 48)}
WINDOW = 3
FFN_AT = {4: 10, 8: 11, 12: 12, 17: 13, 21: 14, 25: 15, 29: 16, 33: 17}
FFN_LAST = 33
AT_MIX = FFN_LAST + 5


def program(nc, x, wa, wb, wc, etab, out):
    ctx = ExitStack()
    with ctx:
        def sb(name, shape, dt=F32):
            return ctx.enter_context(nc.sbuf_tensor(name, shape, dt))

        def sem(name):
            s = ctx.enter_context(nc.semaphore(name))
            return s

        of_layer = ([], [])

        def sem0(name):
            s = sem(name)
            of_layer[0].append(s)
            return s

        def sem1(name):
            s = sem(name)
            of_layer[1].append(s)
            return s

        WA = sb("WA", [P, NA])
        WB = sb("WB", [P, NB])
        WC = sb("WC", [P, NC])

        def w(name, a=0, n=None):
            for off, t in ((OFF_A, WA), (OFF_B, WB), (OFF_C, WC)):
                if name in off:
                    at, width = off[name]
                    return t[:, at + a:at + a + (width if n is None else n)]

        ET = sb("ET", [P, 4 * P], BF16)
        QBD = sb("QBD", [P, H // 2, 2, S], BF16)
        KS = sb("KS", [P, 2, H // 2, S], BF16)
        QR = sb("QR", [P, H, S], BF16)
        KL = KS[:, :, :, :].rearrange("p a b s -> p (a b) s")
        QL = QR
        VP = sb("VP", [P, T, H, 32])
        RG = sb("RG", [P, RING * TILE])
        MB = sb("MB", [P, 2, TILE])
        X = sb("X", [P, T, D])
        XN = sb("XN", [P, T, D])
        XT = sb("XT", [P, S])
        G = sb("G", [P, T, D])
        TH = sb("TH", [P, S])
        AA = sb("AA", [P, S])
        HH = sb("HH", [P, 2, 2, S])
        ACC = sb("ACC", [P, T, D])
        SS = sb("SS", [P, T, D])
        R1 = sb("R1", [P, T, H * G2])
        M1 = sb("M1", [P, H * T])
        M2 = sb("M2", [H * G2, NQ])
        NM = sb("NM", [H * T // 2, P])
        NR = sb("NR", [H * T // 2, P])
        NMP = sb("NMP", [H * T // 2, 2, 3, P], BF16)
        CTX = sb("CTX", [P, 2, P])
        RDN = sb("RDN", [P, 4 * H])
        CN = sb("CN", [P, D])
        CT = sb("CT", [P, P])
        GBV = sb("GBV", [P, D])
        IDB = sb("IDB", [P, P], BF16)
        MKN = sb("MKN", [P, P], BF16)
        MKT = sb("MKT", [P, P], BF16)
        half = sb("half", [P, T])
        st = sb("st", [P, T, 6])
        mv = sb("mv", [P, T, 2])
        ve = sb("ve", [P, T])
        rs = sb("rs", [P, T])
        cols = sb("cols", [P, 8])
        gate_e, gate_s, gate, omg, epsc, qbias, halfc = (cols[:, i:i + 1] for i in range(7))
        LG, EQ, KEY, OH1, OH2, W8, WM = (sb(f"rt{i}", [P, T, E]) for i in range(7))
        m1, m2, km, dm, e2, w1, w2 = (sb(f"rv{i}", [P, T]) for i in range(7))
        WMK = sb("WMK", [P, T, 2 * E])
        WT = SS[0:2 * E, :, :].rearrange("p t d -> p (t d)")
        hb1 = sb("hb1", [P, E])

        def region(at, n, dt=F32):
            v = RG[:, at:at + n]
            return v if dt is F32 else v.bitcast(dt)

        F3 = region(0, 3 * S).rearrange("p (a s) -> p a s", a=3)
        R3 = region(3 * S, 3 * S).rearrange("p (a s) -> p a s", a=3)
        PARTS = region(6 * S, 9 * S // 2, BF16).rearrange("p (a c s) -> p a c s", a=3, c=3)
        QEO = region(11 * S, 3 * S, BF16).rearrange("p (a c s) -> p a c s", a=2, c=3)
        QMIN, QEX, SG, QMAX = (region((14 + i) * S, S) for i in range(4))
        NAB, EX, U1, C1, LNU, TP, ATP, SQ, RT = (region(2 * S * i, 2 * S).rearrange("p (t s) -> p t s", t=2) for i in range(9))
        SI, CO = (region((22 + 2 * i) * S, 2 * S).rearrange("p (t s) -> p t s", t=2) for i in range(2))
        CS4 = region(18 * S, 4 * S).rearrange("p (t c s) -> p t c s", t=2, c=2)
        R4 = region(0, 4 * S).rearrange("p (t c s) -> p t c s", t=2, c=2)
        PARTS1 = region(4 * S, 6 * S, BF16).rearrange("p (t c u s) -> p t c u s", t=2, c=3, u=2)
        PCOL = (0, 512, 896, 1152)
        PH = 1280
        PL = region(0, 2 * 4 * PH).rearrange("p (b j n) -> p b j n", b=2, j=4)
        CT1 = region(20 * S, 2 * S).rearrange("p (a s) -> p a s", a=2)
        CN1 = region(22 * S, S).rearrange("p (t d) -> p t d", t=T)
        CTT = region(23 * S, S)
        XZ = region(24 * S, S).rearrange("p (t d) -> p t d", t=T)
        XS = region(26 * S, 2 * S).rearrange("p (a s) -> p a s", a=2)
        YT = G[:, :, :].rearrange("p t d -> p (t d)")
        C3 = (HH[:, 0, 0, :], ACC[:, :, :].rearrange("p t d -> p (t d)"))
        HE = HH[:, 0, 1, :]
        CC = HH[:, 1, :, :]

        e_full, e_rest = MB[0:2 * HD, 0, 0:S], MB[0:2 * HD, 0, S:2 * S]
        e_parts = MB[0:2 * HD, 1, :].bitcast(BF16)[:, 0:3 * S].rearrange("p (c s) -> p c s", c=3)

        def spread_of(e):
            if 2 <= e < 6:
                return region((6 + 2 * e) * S, 2 * S).rearrange("p (a s) -> p a s", a=2)
            return MB[:, e % 2, :].rearrange("p (a s) -> p a s", a=2)

        PS = ctx.enter_context(nc.psum_tensor("PS", [P, 8, 512], F32))

        def bank(i, n=512, a=0):
            return PS[:, i, a:a + n]

        d_q = nc.dram_tensor("d_q", [3, HD, H, S], BF16).ap()
        d_k = nc.dram_tensor("d_k", [2, SLOTS, HD, H, S], BF16).ap()
        d_e = nc.dram_tensor("d_e", [6, HD, H, S], BF16).ap()
        d_m = nc.dram_tensor("d_m", [2, H * G2, NQ], F32).ap()
        d_c = nc.dram_tensor("d_c", [2, 3, 2, HD, H, S], BF16).ap()
        d_n = nc.dram_tensor("d_n", [2, 3, H * T // 2, P], BF16).ap()
        d_w = nc.dram_tensor("d_w", [2 * E, S], F32).ap()
        d_t = nc.dram_tensor("d_t", [3, 2 * HD, 4 * P], BF16).ap()

        s_wa, s_wb, s_wc, s_et, s_etd, s_etl = (sem(n) for n in ("wa_in", "wb_in", "wc_in", "etab_in", "etab_out", "etab_set"))
        s_pre_pool, s_pre_dve, s_gexp, s_etp = (sem(n) for n in ("pool_set", "dve_set", "gate_exp", "etab_parts"))
        x_first, first_norm = sem("x_first_in"), sem("first_norm")
        s_ended, s_l0_ended, s_l1_cleared, out_done = (
            sem(n) for n in ("sequence_ended", "layer0_ended", "layer1_cleared", "out_written"))
        chain_dve = sem("dve_step")
        x_kept = sem0("x_kept")
        proj_q, proj_k, proj_v, logit_ps, qk_sb, v_set, logits_read = (
            sem0(n) for n in ("q_psum", "k_psum", "v_psum", "logits_psum", "qk_sbuf", "v_set", "logits_read"))
        qeo_zero, parts_ready, qeo_ready, dq_out, de_out, qk_in, rel_in = (
            sem0(n) for n in ("qeo_zero", "parts", "qeo", "parts_in_dram", "qeo_in_dram", "qk_stacked", "qrel_stacked"))
        qmin_ready, qexp_ready, sg_ready, glob_ps, g_ready = (sem0(n) for n in ("qmin", "qexp", "sigma", "global_psum", "global"))
        rdm_ready, rexp_ready = sem0("route_diff"), sem0("route_exp")
        hu_ps, th_ready, hh_ready, fo_ps, fo_used = (sem0(n) for n in ("hu_psum", "tanh", "hh", "ffn_psum", "ffn_added"))
        sc_ps, sc_copied, red_done, m1_ready, mt_ps, m2_ready = (
            sem0(n) for n in ("scores_psum", "scores_copied", "maxed", "max_of_keys", "max_transposed", "max_rows"))
        dm_out, mb_in0, mb_in1, sub_dve, sub_pool, p_ready, pv_done = (
            sem0(n) for n in ("max_in_dram", "max_spread_even", "max_spread_odd", "shifted_dve", "shifted_pool", "probs", "pv"))
        mb_in = (mb_in0, mb_in1)
        ctx_ready, nat_ps, cn_ready, back_ps, ct_ready, at_ps, ss_ready = (
            sem0(n) for n in ("ctx", "ctx_natural", "ctx_normed", "ctx_back_psum", "ctx_back", "attn_psum", "attn"))
        rest2_ready = sem0("rests_of_q_k")
        qmax_ready, kf_ready, hi_ready, rest_ready, mid_ready, kparts_ready, gn_ready = (
            sem0(n) for n in ("qmax", "k_far", "hi_parts", "rests", "mid_parts", "k_far_parts", "global_scaled"))
        ga_ready = sem0("silu_tanh0")
        var1, rstd1, xn1, xt_ps1, xt1 = (sem0(n) for n in ("var1", "rstd1", "xn1", "xt_psum1", "xt1"))
        amp_ps, phi_ps, v_ps1, lg_ps1, tp_sb, v_set1, lg_read1 = (
            sem1(n) for n in ("amp_psum", "phi_psum", "v_psum1", "logits_psum1", "phase", "v_set1", "logits_read1"))
        ex_r, u_r, ln_r, amp_r, sq_r, msq_ps, rt_r, abs_r, cos_r, parts1, dc_out, l1_in = (
            sem1(n) for n in ("exp_abs", "one_plus", "ln", "amp", "amp_sq", "meansq_psum", "rms", "phase_abs",
                              "cos_sin", "parts1", "parts1_in_dram", "stacked1"))
        lge_r, lgx_r, wm_r, wt_ps, wt_r, dw_out, wb_in0, wb_in1, wb_in2, wb_in3, xs_r = (
            sem1(n) for n in ("l1_route_diff", "l1_route_exp", "weights1", "weights_psum", "weights_t", "weights_in_dram",
                              "expert_spread0", "expert_spread1", "expert_spread2", "expert_spread3", "xs"))
        wb_in = (wb_in0, wb_in1, wb_in2, wb_in3)
        hu1_ps, th1_r, h1_r, fo1_ps, y_c, y_add, yt_ps, yn_r = (
            sem1(n) for n in ("hu1_psum", "tanh1", "hh1", "ffn1_psum", "expert_term", "y_added", "y_psum", "y_used"))
        s1_ps, s1_max, nmt_ps, nm_r, dn_out, nm_in0, nm_in1 = (
            sem1(n) for n in ("s1_psum", "s1_maxed", "max1_transposed", "neg_max", "neg_max_in_dram", "neg_max_in0", "neg_max_in1"))
        nm_in = (nm_in0, nm_in1)
        s2_ps, p1_r, pv1, ctx1, nat1_ps, cn1, back1_ps, ctt_r, at1_ps, ga1, xo_r = (
            sem1(n) for n in ("s2_psum", "probs1", "pv1", "ctx1", "ctx1_natural", "ctx1_normed", "ctx1_back_psum",
                              "ctx1_back", "attn1_psum", "gelu_tanh1", "x_out"))
        cs_r, qr_zero = sem1("cos_sin_scaled"), sem1("rows_above_zero")
        x_next, var_next, rstd_next, xn_next, xt_next_ps, xt_next = (
            sem1(n) for n in ("x_next_in", "var_next", "rstd_next", "xn_next", "xt_next_psum", "xt_next"))
        abz_r, hi1_r, rest1_r, mid1_r = (sem1(n) for n in ("amp_abs", "hi_parts1", "rests1", "mid_parts1"))
        c1_r, lnsq_r, dc_q, he_r, c3_r, c3m_r, sig1_r, y1_r = (
            sem1(n) for n in ("softplus_rest", "ln_meansq", "q_parts1_in_dram", "hidden1", "gate1_rows", "gate1_masked", "sigmoid1", "silu1"))

        def from_layer0_to_1(eng, b):
            eng.sem_inc(s_l0_ended, 1)
            eng.wait_ge(s_l1_cleared, b + 1)
            eng.nop(nofuse=True)

        def end_sequence(eng, b):
            eng.sem_inc(s_ended, 1)
            eng.wait_ge(s_ended, (b + 1) * 5)
            eng.nop(nofuse=True)

        block = ctx.enter_context(nc.Block())

        @block.sync
        def _(sp):
            sp.sem_inc(out_done, 16)
            sp.dma_start(XN[:, :, :], x[0:S, :].rearrange("(t p) d -> p t d", p=P)).then_inc(x_first, 16)
            sp.dma_start(WA[:, :], wa).then_inc(s_wa, 16)
            sp.dma_start(e_full, etab).then_inc(s_et, 16)
            sp.dma_start(WB[:, :], wb).then_inc(s_wb, 16)
            sp.wait_ge(s_etp, 1)
            sp.dma_start(d_t.rearrange("c r n -> r c n"), e_parts).then_inc(s_etd, 16)
            sp.wait_ge(s_etd, 16)
            for two in range(2):
                for first, n, part in K_RUNS:
                    for j in range(n):
                        r = two * SLOTS * HD + (first + j) * HD
                        sp.dma_start(ET[r:r + HD, :], d_t[part, two * HD:(two + 1) * HD, :]).then_inc(s_etl, 16)
            sp.dma_start(WC[:, :], wc).then_inc(s_wc, 16)
            with sp.Fori(0, B) as b:
                for s in of_layer[1]:
                    sp.sem_clear(s)
                sp.sem_inc(s_l1_cleared, 1)
                sp.wait_ge(parts_ready, 1)
                sp.dma_start(d_q.rearrange("c d h s -> (d h) c s"), PARTS[:, 0, :, :]).then_inc(dq_out, 16)
                for t in range(2):
                    if t:
                        sp.wait_ge(kparts_ready, 1)
                    for first, n, part in K_RUNS:
                        sp.dma_start(d_k[t, first:first + n].rearrange("c d h s -> (d h) c s"),
                                     PARTS[:, 1 + t, part:part + 1, :].to_broadcast([P, n, S])).then_inc(dq_out, 16)
                sp.wait_ge(qeo_ready, 1)
                sp.dma_start(d_e.rearrange("c d h s -> (d h) c s"), QEO.rearrange("p a c s -> p (a c) s")).then_inc(de_out, 16)
                sp.wait_ge(dq_out, 16 * 7)
                for two in range(2):
                    for first, n in Q_RUNS:
                        r = two * SLOTS * HD + first * HD
                        sp.dma_start(QBD[r:r + n * HD, :, two, :],
                                     d_q[0:n].rearrange("c d (a t) s -> t (c d) a s", t=2)[two]).then_inc(qk_in, 16)
                    r = two * SLOTS * HD
                    for t in range(2):
                        sp.dma_start(KS[r:r + SLOTS * HD, t, :, :],
                                     d_k[t].rearrange("c d (a t) s -> t (c d) a s", t=2)[two]).then_inc(qk_in, 16)
                sp.wait_ge(de_out, 16)
                for two in range(2):
                    for first, n in Q_RUNS:
                        r = two * SLOTS * HD + first * HD
                        sp.dma_start(QR[r:r + n * HD, :, :],
                                     d_e[3 * two:3 * two + n].rearrange("c d h s -> (c d) h s")).then_inc(rel_in, 16)
                for u in range(NU):
                    sp.wait_ge(m2_ready, u + 1)
                    sp.dma_start(d_m[u % 2], M2[:, :]).then_inc(dm_out, 16)
                    sp.wait_ge(dm_out, 16 * (u + 1))
                    if u >= 2:
                        sp.wait_ge(sub_dve, u - 1)
                        sp.wait_ge(sub_pool, 3 * (u - 1))
                    sp.dma_start(MB[:, u % 2, :], d_m[u % 2].rearrange("c i -> (c i)")[None, :].to_broadcast([P, TILE])
                                 ).then_inc(mb_in[u % 2], 16)
                sp.wait_ge(sub_dve, NU)
                sp.wait_ge(sub_pool, 3 * NU)
                sp.wait_ge(s_l0_ended, (b + 1) * 4)
                sp.nop(nofuse=True)
                for s in of_layer[0]:
                    sp.sem_clear(s)
                sp.wait_ge(wt_r, 1)
                sp.dma_start(d_w, WT[:, :]).then_inc(dw_out, 16)
                sp.wait_ge(dw_out, 16)

                def spread(e):
                    if e >= 4:
                        sp.wait_ge(xs_r, e - 3)
                    if e >= 6:
                        sp.wait_ge(c3m_r, e - 5)
                        sp.wait_ge(xs_r, e - 5)
                    for a in range(2):
                        sp.dma_start(spread_of(e)[:, a, :], d_w[a * E + e:a * E + e + 1, :].to_broadcast([P, S])
                                     ).then_inc(wb_in[e % 4], 16)

                spread(0)
                spread(1)
                for n, t in enumerate(ORDER1):
                    sp.wait_ge(parts1, n + 1)
                    sp.dma_start(d_c[t].rearrange("c u d h s -> (d h) (c u) s"),
                                 PARTS1[:, t, :, :, :].rearrange("p c u s -> p (c u) s")).then_inc((dc_q, dc_out)[t], 16)
                sp.wait_ge(dc_out, 16)
                for first, n, part in K_RUNS:
                    r = 2 * first * HD
                    sp.dma_start(KL[r:r + 2 * n * HD, :, :],
                                 d_c[1, part:part + 1].rearrange("c u d h s -> c (u d) (h s)")
                                 .to_broadcast([n, 2 * HD, H * S])).then_inc(l1_in, 16)
                spread(2)
                spread(3)
                sp.wait_ge(dc_q, 16)
                for first, n in Q_RUNS:
                    sp.dma_start(QL[2 * first * HD:2 * (first + n) * HD, :, :],
                                 d_c[0, 0:n].rearrange("c u d h s -> (c u d) h s")).then_inc(l1_in, 16)
                sp.dma_start(XN[:, :, :], x[bass.ds((b + 1) * S, S), :].rearrange("(t p) d -> p t d", p=P)).then_inc(x_next, 16)
                for e in range(4, E):
                    spread(e)
                for g in range(2):
                    sp.wait_ge(nm_r, g + 1)
                    sp.dma_start(d_n[g].rearrange("c r n -> r c n"), NMP[:, g, :, :]).then_inc(dn_out, 16)
                    sp.wait_ge(dn_out, 16 * (g + 1))
                    sp.dma_start(QL[ROWS:ROWS + 3, 8 * g:8 * g + 8, :], d_n[g].rearrange("c (h t) n -> c h (t n)", t=T)
                                 ).then_inc(nm_in[g], 16)
                sp.wait_ge(xo_r, 1)
                sp.dma_start(out[bass.ds(b * S, S), :].rearrange("(t p) d -> p t d", p=P), X[:, :, :]).then_inc(out_done, 16)
                end_sequence(sp, b)
            sp.wait_ge(out_done, 16 * (B + 1))

        @block.gpsimd
        def _(pool):
            nc.gpsimd.memset(half[:, :], -0.5).then_inc(s_pre_pool, 1)
            nc.gpsimd.memset(VP[:, :, :, :], 0.0).then_inc(s_pre_pool, 1)
            pool.wait_ge(s_pre_pool, 2)
            v2 = VP[:, :, :, :].rearrange("p t (a two) c -> p (t a) two c", two=2)
            for two in range(2):
                nc.gpsimd.memset(v2[:, :, two, 16 + 8 * two:24 + 8 * two], 1.0).then_inc(s_pre_pool, 1)
            pool.wait_ge(first_norm, 1)
            nc.gpsimd.tensor_tensor(rs[:, :], ve[:, :], half[:, :], ALU.pow).then_inc(first_norm, 1)
            nc.gpsimd.memset(QBD[:, :, :, :], 0.0).then_inc(s_pre_pool, 1)
            pool.wait_ge(s_pre_pool, 5)
            nc.gpsimd.memset(QR[ROWS:P, :, :].rearrange("p h s -> p (h s)").bitcast(F32), 0.0).then_inc(s_pre_pool, 1)
            pool.wait_ge(s_pre_pool, 6)
            with pool.Fori(0, B) as b:
                nc.gpsimd.memset(QEO.rearrange("p a c s -> p (a c s)").bitcast(F32), 0.0).then_inc(qeo_zero, 1)
                pool.wait_ge(qk_sb, 2)
                nc.gpsimd.tensor_scalar(F3[:, 2, 0:S // 2], F3[:, 1, 0:S // 2], w("e_near"), None, ALU.add).then_inc(kf_ready, 1)
                nc.gpsimd.tensor_scalar(F3[:, 2, S // 2:S], F3[:, 1, S // 2:S], w("e_far"), None, ALU.add).then_inc(kf_ready, 1)
                nc.gpsimd.tensor_scalar(QMIN, F3[:, 0, :], 0.0, None, ALU.min).then_inc(qmin_ready, 1)
                pool.wait_ge(hi_ready, 3)
                nc.gpsimd.tensor_tensor(R3[:, 2, :], F3[:, 2, :], PARTS[:, 2, 0, :], ALU.subtract).then_inc(rest_ready, 1)
                pool.wait_ge(mid_ready, 2)
                nc.gpsimd.tensor_tensor(PARTS[:, 2, 2, :], R3[:, 2, :], PARTS[:, 2, 1, :], ALU.subtract).then_inc(kparts_ready, 1)
                nc.gpsimd.tensor_scalar(QMAX, F3[:, 0, :], 0.0, None, ALU.max).then_inc(qmax_ready, 1)
                pool.wait_ge(qexp_ready, 1)
                pool.wait_ge(qmax_ready, 1)
                nc.gpsimd.tensor_tensor(SG, QMAX, QEX, ALU.add).then_inc(sg_ready, 1)
                pool.wait_ge(gn_ready, 1)
                nc.gpsimd.tensor_tensor(G[:, :, :], G[:, :, :], GBV[:, None, :].to_broadcast([P, T, D]), ALU.add).then_inc(g_ready, 1)
                for u in range(NU):
                    pool.wait_ge(mb_in[u % 2], 16 * (u // 2 + 1))
                    for kb in range(T - 1):
                        tile = region((T * u + kb) % RING * TILE, TILE)
                        pool.wait_ge(red_done, T * u + kb + 1)
                        nc.gpsimd.tensor_tensor(tile, tile, MB[:, u % 2, :], ALU.subtract).then_inc(sub_pool, 1)
                for n, tiles in enumerate(X_GROUPS):
                    a, z = tiles[0], tiles[-1] + 1
                    pool.wait_ge(var1, n + 1)
                    if n:
                        pool.wait_ge(rstd1, n)
                    nc.gpsimd.tensor_tensor(rs[:, a:z], ve[:, a:z], half[:, a:z], ALU.pow).then_inc(rstd1, 1)
                pool.wait_ge(xt1, 2)
                from_layer0_to_1(pool, b)
                def weighted(e):
                    pool.wait_ge(wb_in[e % 4], 32 * (e // 4 + 1))
                    if e >= 2:
                        pool.wait_ge(hu1_ps, 2 + e - 1)
                    nc.gpsimd.tensor_tensor(XS[:, e % 2, :], XT[:, :], spread_of(e)[:, 0, :], ALU.mult).then_inc(xs_r, 1)

                def added(e):
                    pool.wait_ge(y_c, e + 1)
                    if e:
                        pool.wait_ge(y_add, e)
                    nc.gpsimd.tensor_tensor(YT[:, :], YT[:, :], CC[:, e % 2, :], ALU.add).then_inc(y_add, 1)

                def masked(e):
                    pool.wait_ge(c3_r, e + 1)
                    nc.gpsimd.tensor_tensor(C3[e % 2], C3[e % 2], spread_of(e)[:, 1, :], ALU.mult).then_inc(c3m_r, 1)

                weighted(0)
                weighted(1)
                for e in range(E):
                    if e + 2 < E:
                        weighted(e + 2)
                    masked(e)
                    if e:
                        added(e - 1)
                added(E - 1)
                pool.wait_ge(var_next, 1)
                nc.gpsimd.tensor_tensor(rs[:, :], ve[:, :], half[:, :], ALU.pow).then_inc(rstd_next, 1)
                pool.wait_ge(rstd_next, 1)
                pool.wait_ge(s2_ps, 3 * H)
                nc.gpsimd.memset(QR[ROWS:P, :, :].rearrange("p h s -> p (h s)").bitcast(F32), 0.0).then_inc(qr_zero, 1)
                pool.wait_ge(qr_zero, 1)
                end_sequence(pool, b)

        @block.tensor
        def _(pe):
            mm = nc.tensor.matmul
            pe.wait_ge(s_wa, 16)
            
            def transpose_tiles(done, src=XN, to=B_MISC):
                for t in range(T):
                    last = nc.tensor.transpose(bank(to, P, t * P), src[:, t, :], w("ident"))
                last.then_inc(done, 1)

            def transpose_group(n):
                pe.wait_ge(xn1, n + 1)
                for t in X_GROUPS[n]:
                    last = nc.tensor.transpose(bank(B_S + 2, P, t * P), XN[:, t, :], w("ident"))
                last.then_inc(xt_ps1, 1)

            def ffn_hidden(s):
                e, fi = s // 2, s % 2
                if s > FFN_BEFORE:
                    pe.wait_ge(hh_ready, s)
                elif s >= 2:
                    pe.wait_ge(hh_ready, s - 1)
                mm(bank(ffn_banks(s)[0]), w("sw1", fi * P, P) if e == 0 else w("ew1", (e - 1) * F0 + fi * P, P), XT[:, :],
                   start=True, stop=True)

            def ffn_gate(s):
                e, fi = s // 2, s % 2
                mm(bank(ffn_banks(s)[1]), w("sw2", fi * P, P) if e == 0 else w("ew2", (e - 1) * F0 + fi * P, P), XT[:, :],
                   start=True, stop=True).then_inc(hu_ps, 1)

            def ffn_out(e, tiles=range(T)):
                if tiles[0] == 0:
                    pe.wait_ge(hh_ready, 2 * e + 2)
                    if e:
                        pe.wait_ge(fo_used, e)
                    else:
                        pe.wait_ge(v_set, 1)
                for t in tiles:
                    for fi in range(2):
                        a = w("sw3", fi * D, D) if e == 0 else w("ew3", ((e - 1) * 2 + fi) * D, D)
                        last = mm(bank(B_O, P, t * P), HH[:, e % 2, fi, t * P:(t + 1) * P], a, start=fi == 0, stop=fi == 1)
                if tiles[-1] == T - 1:
                    last.then_inc(fo_ps, 1)

            def out_after(s):
                return s // 2 - 1 if s >= 2 and s % 2 == 0 else None

            def ffn_one(s):
                ffn_hidden(s)
                ffn_gate(s)
                if out_after(s) is not None:
                    ffn_out(out_after(s))

            def ffn_piece(i, second):
                if i in FFN_AT:
                    (ffn_gate if second else ffn_hidden)(FFN_AT[i])
                if i - 1 in FFN_AT and out_after(FFN_AT[i - 1]) is not None:
                    ffn_out(out_after(FFN_AT[i - 1]), range(2, T) if second else range(2))
                if i == FFN_LAST + 2 and second:
                    ffn_out(E)

            def score_tile(i):
                u, kb = i // T, i % T
                far = abs(u * UQ // P - kb) >= 2
                for g in range(G2):
                    n = G2 * i + g
                    ps = bank(B_S + n % NSB)
                    q0 = u * UQ + g * NQ
                    if n >= NSB:
                        pe.wait_ge(sc_copied, n - NSB + 1)
                    elif n == NSB - 1:
                        pe.wait_ge(hh_ready, FFN_BEFORE)
                    for a in range(H // 2):
                        last = mm(ps[:, a * 2 * NQ:(a + 1) * 2 * NQ], KS[:, int(far), a, kb * P:(kb + 1) * P],
                                  QBD[:, a, :, q0:q0 + NQ], start=a == 0, stop=far and a == H // 2 - 1,
                                  skip_group_check=True)
                    if not far:
                        v = ps.rearrange("p (h q) -> p h q", h=H)
                        for j in range(NQ // 2):
                            at = kb * P - (q0 + 2 * j) + 2 * P
                            last = mm(v[:, :, 2 * j:2 * j + 2], ET[:, at:at + P], QR[:, :, q0 + 2 * j:q0 + 2 * j + 2],
                                      start=False, stop=j == NQ // 2 - 1, skip_group_check=True)
                    last.then_inc(sc_ps, 1)
                    if g == 0:
                        ffn_piece(i, False)

            def max_transpose(v):
                pe.wait_ge(m1_ready, v + 1)
                if v >= 4 and v % 2 == 0:
                    pe.wait_ge(ss_ready, (v - 4) // 2 + 1)
                elif v:
                    pe.wait_ge(m2_ready, v)
                nc.tensor.transpose(PS[0:H * G2, B_MISC, 0:P], M1[:, 0:H * G2], w("ident")).then_inc(mt_ps, 1)

            def pv(v, kb):
                pe.wait_ge(p_ready, T * v + kb + 1)
                if kb == 0:
                    if v:
                        pe.wait_ge(ctx_ready, v)
                    else:
                        pe.wait_ge(logits_read, 1)
                tile = region((T * v + kb) % RING * TILE, TILE).rearrange("p (h q) -> p h q", h=H)
                for half_ in range(2):
                    for two in range(2):
                        for j in range(4):
                            h = half_ * 8 + 2 * j + two
                            last = mm(PS[32 * j:32 * j + 32, B_PV, half_ * UQ:(half_ + 1) * UQ], VP[:, kb, h, :], tile[:, h, :],
                                      start=kb == 0 and half_ == 0 and two == 0, stop=kb == T - 1, skip_group_check=True)
                last.then_inc(pv_done, 1)

            def natural(c):
                pe.wait_ge(ctx_ready, 2 * c + 2)
                if c < T - 1:
                    pe.wait_ge(m2_ready, 2 * c + 4)
                else:
                    pe.wait_ge(ss_ready, c)
                for a in range(2):
                    last = nc.tensor.transpose(bank(B_MISC, P, a * P), CTX[:, a, :], w("ident"))
                last.then_inc(nat_ps, 1)

            def back(c):
                pe.wait_ge(cn_ready, c + 1)
                nc.tensor.transpose(bank(B_MISC, P), CN[:, :], w("ident")).then_inc(back_ps, 1)

            def attn_out(c):
                pe.wait_ge(ct_ready, c + 1)
                mm(bank(B_MISC, P), CT[:, :], w("WoT"), start=True, stop=True).then_inc(at_ps, 1)

            def ffn1_shared(s):
                pe.wait_ge(s_wc, 16)
                if s:
                    pe.wait_ge(h1_r, s)
                mm(bank(B_H), w("tsw1", s * P, P), XT[:, :], start=True, stop=True)
                mm(bank(B_U), w("tsw2", s * P, P), XT[:, :], start=True, stop=True).then_inc(hu1_ps, 1)

            def ffn1_shared_out():
                pe.wait_ge(h1_r, 2)
                pe.wait_ge(v_set1, 1)
                mm(bank(B_O), w("tsw3", 0, D), HH[:, 0, 0, :], start=True, stop=False)
                mm(bank(B_O), w("tsw3", D, D), HH[:, 0, 1, :], start=False, stop=True).then_inc(fo1_ps, 1)

            def expert1_in(e):
                pe.wait_ge(xs_r, e + 1)
                if e == 0:
                    pe.wait_ge(h1_r, 2)
                elif e == 1:
                    pe.wait_ge(lnsq_r, 2)
                else:
                    pe.wait_ge(he_r, e - 1 if e <= WINDOW else e)
                    pe.wait_ge(c3_r, e - 1 if e <= WINDOW else e)
                mm(bank(expert_banks(e)[0]), w("tw1", e * HID, HID), XS[:, e % 2, :], start=True, stop=True)
                mm(bank(expert_banks(e)[1]), w("tw3", e * HID, HID), XS[:, e % 2, :], start=True, stop=True).then_inc(hu1_ps, 1)

            def expert1_out(e):
                pe.wait_ge(he_r, e + 1)
                pe.wait_ge(y_c, e) if e else pe.wait_ge(yn_r, 1)
                mm(bank(B_O), w("tw2", e * D, D), HE, start=True, stop=True).then_inc(fo1_ps, 1)

            def s1_bank(n):
                tile, h0, heads = BANKS1[n]
                if n:
                    before = users_before(bank1, n)
                    if before:
                        pe.wait_ge(s1_max, before)
                width = (tile + 1) * P
                ps = bank(bank1(n))
                for a in range(heads):
                    h = h0 + a
                    o = ps[:, a * width:(a + 1) * width]
                    mm(o, QL[:, h, tile * P:(tile + 1) * P], KL[:, h, 0:width], start=a == 0, stop=False,
                       skip_group_check=True)
                    last = mm(o[:, tile * P:width], IDB[:, :], MKN[:, :], start=False, stop=True, skip_group_check=True)
                last.then_inc(s1_ps, 1)

            def turn_maxima(g):
                pe.wait_ge(s1_max, HALF_BANKS * (g + 1))
                pe.wait_ge(wt_r, 1)
                if g:
                    pe.wait_ge(nm_r, 1)
                nc.tensor.transpose(PS[0:H * T // 2, (B_PV, B_S)[g], 0:P], M1[:, g * H * T // 2:(g + 1) * H * T // 2], w("ident")
                                    ).then_inc(nmt_ps, 1)

            def s2_banks(n, h):
                if n == 0:
                    pe.wait_ge(s1_max, HALF_BANKS)
                if n == 8:
                    pe.wait_ge(s1_max, 2 * HALF_BANKS)
                    pe.wait_ge(nm_r, 2)
                for c, kbs in enumerate(((0,), (1,), (2, 3))):
                    i = 3 * n + c
                    before = users_before(bank2, i)
                    if before:
                        pe.wait_ge(p1_r, before)
                    at = 0
                    for kb in kbs:
                        width = S - kb * P
                        o = bank(bank2(i), width, at)
                        mm(o, KL[:, h, kb * P:(kb + 1) * P], QL[:, h, kb * P:S], start=at == 0, stop=False,
                           skip_group_check=True)
                        last = mm(o[:, 0:P], IDB[:, :], MKT[:, :], start=False, stop=True, skip_group_check=True)
                        at += width
                    last.then_inc(s2_ps, 1)

            def pv1_group(gq):
                half_, two = gq // 2, gq % 2
                pe.wait_ge(p1_r, 12 * (gq + 1))
                if gq == 2:
                    pe.wait_ge(ctx1, 1)
                if gq == 0:
                    pe.wait_ge(nm_r, 1)
                for kb in range(T):
                    for j in range(4):
                        h = half_ * 8 + 2 * j + two
                        last = mm(PS[32 * j:32 * j + 32, B_PV, kb * P:S], VP[:, kb, h, :],
                                  PL[:, gq % 2, j, PCOL[kb]:PCOL[kb] + S - kb * P],
                                  start=two == 0 and kb == 0, stop=two == 1 and kb == T - 1, skip_group_check=True)
                last.then_inc(pv1, 1)

            pe.wait_ge(first_norm, 3)
            transpose_tiles(first_norm, XZ, B_U)
            pe.wait_ge(first_norm, 5)
            with pe.Fori(0, B) as b:
                mm(bank(B_H), w("WqT"), XT[:, :], start=True, stop=True).then_inc(proj_q, 1)
                mm(bank(B_U), w("WkT"), XT[:, :], start=True, stop=True).then_inc(proj_k, 1)
                for t in range(T):
                    last = mm(bank(B_O, P, t * P), XT[:, t * P:(t + 1) * P], w("WvT"), start=True, stop=True)
                last.then_inc(proj_v, 1)
                for t in range(T):
                    last = mm(bank(B_PV, E, t * E), XT[:, t * P:(t + 1) * P], w("gate0"), start=True, stop=True)
                last.then_inc(logit_ps, 1)
                pe.wait_ge(qk_sb, 2)
                ffn_one(0)
                ffn_one(1)
                pe.wait_ge(s_wb, 16)
                ffn_one(2)
                pe.wait_ge(sg_ready, 1)
                for t in range(T):
                    last = mm(bank(B_S + t // 2, D + H, t % 2 * (D + H)), SG[:, t * P:(t + 1) * P], w("MZ"), start=True, stop=True)
                last.then_inc(glob_ps, 1)
                for s in range(3, FFN_BEFORE):
                    ffn_one(s)
                pe.wait_ge(gn_ready, 1)
                pe.wait_ge(s_etl, 16 * 12)
                pe.wait_ge(qk_in, 16 * (6 + 4))
                pe.wait_ge(rel_in, 16 * 6)
                pe.wait_ge(s_pre_pool, 6)
                pe.wait_ge(s_pre_dve, 1)
                for i in range(NSLOT0):
                    if i < SLOTS0:
                        score_tile(i)
                    else:
                        ffn_piece(i, False)
                    ffn_piece(i, True)
                    for v in range(NU):
                        if i == T * v + AT_MAX:
                            max_transpose(v)
                        if 0 <= i - T * v - AT_PV < T:
                            pv(v, i - T * v - AT_PV)
                    for c in range(T):
                        if i == 2 * T * c + AT_NATURAL:
                            natural(c)
                        if i == 2 * T * c + AT_BACK:
                            back(c)
                        if i == 2 * T * c + AT_OUT:
                            attn_out(c)
                    if i == AT_MIX + 2:
                        transpose_group(0)
                transpose_group(1)
                pe.wait_ge(xt1, 2)

                from_layer0_to_1(pe, b)
                pe.wait_ge(s_wc, 16)
                for n, t in enumerate(ORDER1):
                    mm(bank(B_S + n), w(("Wqp", "Wkp")[t]), XT[:, :], start=True, stop=True).then_inc(phi_ps, 1)
                for n, t in enumerate(ORDER1):
                    mm(bank(AMP_BANK[t]), w(("Wqa", "Wka")[t]), XT[:, :], start=True, stop=True).then_inc(amp_ps, 1)
                for t in range(T):
                    last = mm(bank(B_PV, E, t * E), XT[:, t * P:(t + 1) * P], w("gate1"), start=True, stop=True)
                last.then_inc(lg_ps1, 1)
                ffn1_shared(0)
                for t in range(T):
                    last = mm(bank(B_O, P, t * P), XT[:, t * P:(t + 1) * P], w("Wv1"), start=True, stop=True)
                last.then_inc(v_ps1, 1)
                ffn1_shared(1)
                for n, t in enumerate(ORDER1):
                    pe.wait_ge(tp_sb, n + 1)
                    pe.wait_ge(sq_r, n + 1)
                    mm(bank(B_S + n), w("mean8"), SQ[:, t, :], start=True, stop=True).then_inc(msq_ps, 1)
                pe.wait_ge(wm_r, 1)
                for t in range(T):
                    last = nc.tensor.transpose(PS[0:2 * E, B_PV, t * P:(t + 1) * P], WMK[:, t, :], w("ident"))
                last.then_inc(wt_ps, 1)
                ffn1_shared_out()
                expert1_in(0)
                for e in range(1, WINDOW):
                    expert1_in(e)
                    expert1_out(e - 1)
                expert1_out(WINDOW - 1)
                pe.wait_ge(lnsq_r, 2)
                pe.wait_ge(amp_r, 2)
                pe.wait_ge(c3_r, WINDOW)
                pe.wait_ge(l1_in, 16 * 6)
                for i in range(NSLOT1):
                    if i < 2 * HALF_BANKS:
                        s1_bank(i)
                    for g in range(2):
                        if i == NM_AT[g]:
                            turn_maxima(g)
                    if i in HEAD_AT:
                        n = HEAD_AT[i]
                        if n % 8 == 0:
                            pe.wait_ge(nm_in[n // 8], 16)
                        s2_banks(n, n // 8 * 8 + n % 4 * 2 + n // 4 % 2)
                        if n and n % 4 == 0:
                            pv1_group(n // 4 - 1)
                    for e, (at_in, _, at_out, _) in EXPERT_AT.items():
                        if i == at_in:
                            expert1_in(e)
                        if i == at_out:
                            expert1_out(e)
                pe.wait_ge(xn_next, 1)
                transpose_tiles(xt_next_ps, XZ, B_U)
                pv1_group(3)
                pe.wait_ge(y_add, E)
                pe.wait_ge(y_c, E)
                for t in range(T):
                    last = nc.tensor.transpose(bank(B_O, P, t * P), YT[:, t * P:(t + 1) * P], w("ident"))
                last.then_inc(yt_ps, 1)
                pe.wait_ge(ctx1, 2)
                for t in range(T):
                    for a in range(2):
                        last = nc.tensor.transpose(bank((B_MISC, B_H)[t // 2], P, (t % 2 * 2 + a) * P),
                                                   CT1[:, a, t * P:(t + 1) * P], w("ident"))
                    if t % 2:
                        last.then_inc(nat1_ps, 1)
                pe.wait_ge(cn1, 2)
                for t in range(T):
                    last = nc.tensor.transpose(bank(B_U, P, t * P), CN1[:, t, :], w("ident"))
                last.then_inc(back1_ps, 1)
                pe.wait_ge(ctt_r, 1)
                for t in range(T):
                    last = mm(bank(B_PV, P, t * P), CTT[:, t * P:(t + 1) * P], w("WoT1"), start=True, stop=True)
                last.then_inc(at1_ps, 1)
                end_sequence(pe, b)

        @block.scalar
        def _(act):
            A = nc.scalar.activation
            act.wait_ge(s_wa, 16)
            A(gate_e, w("alpha"), ACT.Exp, scale=-1.0).then_inc(s_gexp, 1)

            def ffn_tanh(s):
                act.wait_ge(hu_ps, s + 1)
                if s:
                    act.wait_ge(hh_ready, s)
                A(TH[:, :], bank(ffn_banks(s)[0]), ACT.Tanh, scale=0.5).then_inc(th_ready, 1)

            def exp_tile(v, kb):
                if kb == T - 1:
                    act.wait_ge(sub_dve, v + 1)
                else:
                    act.wait_ge(sub_pool, (T - 1) * v + kb + 1)
                tile = region((4 * v + kb) % RING * TILE, TILE)
                A(tile, tile, ACT.Exp, scale=1.0 / sqrt(HD)).then_inc(p_ready, 1)

            with act.Fori(0, B) as b:
                act.wait_ge(proj_q, 1)
                A(F3[:, 0, :], bank(B_H), ACT.Identity, bias=w("bq")).then_inc(qk_sb, 1)
                act.wait_ge(proj_k, 1)
                A(F3[:, 1, :], bank(B_U), ACT.Identity, bias=w("bk")).then_inc(qk_sb, 1)
                act.wait_ge(qk_sb, 2)
                A(PARTS[:, 0:2, 0, :], F3[:, 0:2, :], ACT.Copy).then_inc(hi_ready, 1)
                ffn_tanh(0)
                act.wait_ge(rest2_ready, 1)
                A(PARTS[:, 0:2, 1, :], R3[:, 0:2, :], ACT.Copy).then_inc(mid_ready, 1)
                act.wait_ge(kf_ready, 2)
                A(PARTS[:, 2, 0, :], F3[:, 2, :], ACT.Copy).then_inc(hi_ready, 2)
                act.wait_ge(qmin_ready, 1)
                A(QEX, QMIN, ACT.Exp).then_inc(qexp_ready, 1)
                act.wait_ge(rest_ready, 1)
                A(PARTS[:, 2, 1, :], R3[:, 2, :], ACT.Copy).then_inc(mid_ready, 1)
                act.wait_ge(parts_ready, 1)
                act.wait_ge(qeo_zero, 1)
                for a in range(2):
                    last = A(QEO[:, a, :, a::2], PARTS[:, 0, :, a::2], ACT.Copy)
                last.then_inc(qeo_ready, 1)
                ffn_tanh(1)
                ffn_tanh(2)
                act.wait_ge(rdm_ready, 1)
                A(e2[:, :], dm[:, :], ACT.Exp).then_inc(rexp_ready, 1)
                for s in range(3, FFN_BEFORE):
                    ffn_tanh(s)
                for i in range(NSLOT0):
                    if i < SLOTS0:
                        tile = region(i % RING * TILE, TILE).rearrange("p (h q) -> p h q", h=H)
                        if i >= RING:
                            act.wait_ge(pv_done, i - RING + 1)
                        for g in range(G2):
                            n = G2 * i + g
                            act.wait_ge(sc_ps, n + 1)
                            A(tile[:, :, g * NQ:(g + 1) * NQ], bank(B_S + n % NSB).rearrange("p (h q) -> p h q", h=H),
                              ACT.Copy).then_inc(sc_copied, 1)
                            if g == 0 and i - 1 in FFN_AT:
                                ffn_tanh(FFN_AT[i - 1])
                    if i >= SLOTS0 and i - 1 in FFN_AT:
                        ffn_tanh(FFN_AT[i - 1])
                    if i == AT_MIX - 1:
                        act.wait_ge(fo_used, E + 1)
                        A(TH[:, :], ACC[:, :, :].rearrange("p t d -> p (t d)"), ACT.Tanh, scale=0.5).then_inc(ga_ready, 1)
                    for v in range(NU):
                        if 0 <= i - T * v - AT_EXP < T:
                            exp_tile(v, i - T * v - AT_EXP)
                        if i == T * v + AT_EVAC:
                            act.wait_ge(pv_done, T * v + T)
                            if v >= 2:
                                act.wait_ge(nat_ps, v // 2)
                            A(CTX[:, :, v % 2 * UQ:(v % 2 + 1) * UQ], bank(B_PV, 2 * UQ).rearrange("p (a q) -> p a q", a=2),
                              ACT.Copy).then_inc(ctx_ready, 1)

                from_layer0_to_1(act, b)
                for n, t in enumerate(ORDER1):
                    act.wait_ge(phi_ps, n + 1)
                    A(TP[:, t, :], bank(B_S + n), ACT.Tanh).then_inc(tp_sb, 1)
                for n, t in enumerate(ORDER1):
                    act.wait_ge(amp_ps, n + 1)
                    A(NAB[:, t, :], bank(AMP_BANK[t]), ACT.Abs).then_inc(abz_r, 1)
                for n, t in enumerate(ORDER1):
                    act.wait_ge(abz_r, n + 1)
                    A(EX[:, t, :], NAB[:, t, :], ACT.Exp, scale=-1.0).then_inc(ex_r, 1)
                act.wait_ge(tp_sb, 2)
                A(ATP, TP, ACT.Abs).then_inc(abs_r, 1)
                act.wait_ge(lge_r, 1)
                A(EQ[:, :, :], KEY[:, :, :], ACT.Exp).then_inc(lgx_r, 1)

                def tanh1(s):
                    act.wait_ge(hu1_ps, s + 1)
                    if s:
                        act.wait_ge(h1_r, s)
                    A(TH[:, :], bank(B_H), ACT.Tanh, scale=0.5).then_inc(th1_r, 1)

                def expert_act(e):
                    act.wait_ge(hu1_ps, 3 + e)
                    if e == 0:
                        act.wait_ge(h1_r, 2)
                    else:
                        act.wait_ge(sig1_r, e)
                    A(TH[:, :], bank(expert_banks(e)[0]), ACT.Tanh, scale=0.5, bias=hb1[:, e:e + 1]).then_inc(th1_r, 1)
                    if e >= 2:
                        act.wait_ge(y_c, e - 1)
                    elif e == 0:
                        act.wait_ge(fo1_ps, 1)
                    A(C3[e % 2], bank(expert_banks(e)[1]), ACT.Identity, bias=w("b3", e, 1)).then_inc(c3_r, 1)
                    act.wait_ge(th1_r, 3 + e)
                    if e:
                        act.wait_ge(he_r, e)
                    A(AA[:, :], TH[:, :], ACT.Identity, scale=0.5, bias=halfc).then_inc(sig1_r, 1)

                tanh1(0)
                act.wait_ge(abs_r, 1)
                A(SI, TP, ACT.Sin, scale=pi).then_inc(cos_r, 1)
                A(CO, ATP, ACT.Sin, scale=-pi, bias=w("halfpi")).then_inc(cos_r, 1)
                for n, t in enumerate(ORDER1):
                    act.wait_ge(u_r, n + 1)
                    A(LNU[:, t, :], U1[:, t, :], ACT.Ln).then_inc(ln_r, 1)
                for n, t in enumerate(ORDER1):
                    act.wait_ge(amp_r, n + 1)
                    A(SQ[:, t, :], EX[:, t, :], ACT.Square).then_inc(sq_r, 1)
                for n, t in enumerate(ORDER1):
                    act.wait_ge(msq_ps, n + 1)
                    A(RT[:, t, :], bank(B_S + n), ACT.Ln, bias=epsc).then_inc(lnsq_r, 1)
                for n, t in enumerate(ORDER1):
                    act.wait_ge(lnsq_r, n + 1)
                    A(RT[:, t, :], RT[:, t, :], ACT.Exp, scale=-0.5, **({} if t else {"bias": qbias})).then_inc(rt_r, 1)
                tanh1(1)
                for n, t in enumerate(ORDER1):
                    act.wait_ge(cs_r, n + 1)
                    A(PARTS1[:, t, 0, :, :], CS4[:, t, :, :], ACT.Copy).then_inc(hi1_r, 1)
                for n, t in enumerate(ORDER1):
                    act.wait_ge(rest1_r, n + 1)
                    A(PARTS1[:, t, 1, :, :], R4[:, t, :, :], ACT.Copy).then_inc(mid1_r, 1)
                for e in range(WINDOW):
                    expert_act(e)

                def exp1(n):
                    for c, (at, width) in enumerate(((0, 512), (512, 384), (896, 384))):
                        act.wait_ge(s2_ps, 3 * n + c + 1)
                        if n >= 8 and c == 0:
                            act.wait_ge(pv1, n // 4 - 1)
                        elif n == 4 and c == 0:
                            act.wait_ge(c3m_r, 6)
                            act.wait_ge(xs_r, 6)
                        A(PL[:, n // 4 % 2, n % 4, at:at + width], bank(bank2(3 * n + c), width), ACT.Exp).then_inc(p1_r, 1)

                for i in range(NSLOT1):
                    if i in HEAD_AT:
                        exp1(HEAD_AT[i])
                        if HEAD_AT[i] == 11:
                            act.wait_ge(pv1, 2)
                            A(CT1[:, 0, :], bank(B_PV), ACT.Copy).then_inc(ctx1, 1)
                    for e, (at_in, _, _, _) in EXPERT_AT.items():
                        if i == at_in:
                            expert_act(e)
                act.wait_ge(pv1, 4)
                A(CT1[:, 1, :], bank(B_PV), ACT.Copy).then_inc(ctx1, 1)
                act.wait_ge(yt_ps, 1)
                act.wait_ge(he_r, E)
                A(TH[:, :], bank(B_O), ACT.Tanh, scale=0.5).then_inc(ga1, 1)
                end_sequence(act, b)

        @block.vector
        def _(dve):
            V = nc.vector
            steps = [0]

            def link(ins):
                steps[0] += 1
                ins.then_inc(chain_dve, 1)
                dve.wait_ge(chain_dve, steps[0])

            def norm_stats(done, src=X):
                for t in range(T):
                    last = V.bn_stats(st[:, t, :], src[:, t, :])
                link(last)
                for t in range(T):
                    last = V.bn_aggr(mv[:, t, :], st[:, t, :])
                link(last)
                V.tensor_scalar(ve[:, :], mv[:, :, 1], LN_EPS, None, ALU.add).then_inc(done, 1)

            def norm_apply(rstd, done, src=X, to=XN):
                dve.wait_ge(rstd, 1)
                for t in range(T):
                    last = V.tensor_scalar(to[:, t, :], src[:, t, :], mv[:, t, 0:1], rs[:, t:t + 1], ALU.subtract, ALU.mult)
                last.then_inc(done, 1)

            def set_v(ready, done):
                dve.wait_ge(ready, 1)
                v = bank(B_O).rearrange("p (a two d) -> p a two d", two=2, d=HD)
                o = VP[:, :, :, :].rearrange("p t (a two) c -> p (t a) two c", two=2)
                for two in range(2):
                    last = V.tensor_copy(o[:, :, two, 8 * two:8 * two + 8], v[:, :, two, :])
                last.then_inc(done, 1)

            def over(v):
                return v[:, :, None].to_broadcast([P, T, E])

            idx = w("idx")[:, None, :].to_broadcast([P, T, E])

            def first_max(a, m, oh):
                link(V.tensor_reduce(m, a, AX.X, ALU.max))
                link(V.tensor_tensor(KEY[:, :, :], a, over(m), ALU.is_equal))
                link(V.tensor_tensor(KEY[:, :, :], KEY[:, :, :], idx, ALU.mult))
                link(V.tensor_reduce(km[:, :], KEY[:, :, :], AX.X, ALU.max))
                link(V.tensor_tensor(oh, KEY[:, :, :], over(km), ALU.is_equal))

            def without(a, oh):
                link(V.scalar_tensor_tensor(out=a, in0=oh, scalar=-3e38, in1=a, op0=ALU.mult, op1=ALU.add))

            def split(full, rest, parts):
                link(V.tensor_copy(parts[0], full))
                link(V.tensor_tensor(rest, full, parts[0], ALU.subtract))
                link(V.tensor_copy(parts[1], rest))
                return V.tensor_tensor(parts[2], rest, parts[1], ALU.subtract)

            def ffn_hh(s):
                e, fi = s // 2, s % 2
                dve.wait_ge(th_ready, s + 1)
                link(V.scalar_tensor_tensor(out=AA[:, :], in0=TH[:, :], scalar=1.0, in1=bank(ffn_banks(s)[0]), op0=ALU.add, op1=ALU.mult))
                if e >= 2:
                    dve.wait_ge(fo_ps, e - 1)
                V.tensor_tensor(HH[:, e % 2, fi, :], AA[:, :], bank(ffn_banks(s)[1]), ALU.mult).then_inc(hh_ready, 1)
                dve.wait_ge(hh_ready, s + 1)

            def ffn_acc(e):
                dve.wait_ge(fo_ps, e + 1)
                if e == 0:
                    link(V.tensor_scalar(ACC[:, :, :].rearrange("p t d -> p (t d)"), bank(B_O), 0.5, None, ALU.mult))
                else:
                    for t in range(T):
                        last = V.scalar_tensor_tensor(out=ACC[:, t, :], in0=bank(B_O, P, t * P), scalar=W8[:, t, e - 1:e],
                                                      in1=ACC[:, t, :], op0=ALU.mult, op1=ALU.add)
                    link(last)
                V.engine_nop().then_inc(fo_used, 1)

            def ffn_dve(s):
                ffn_hh(s)
                if s >= 2 and s % 2 == 0:
                    ffn_acc(s // 2 - 1)

            def mix_and_stats(n):
                tiles = X_GROUPS[n]
                dve.wait_ge(ss_ready, tiles[-1] + 1)
                a, z = tiles[0], tiles[-1] + 1
                aa = AA[:, :].rearrange("p (t d) -> p t d", t=T)
                link(V.tensor_tensor(SS[:, a:z, :], SS[:, a:z, :], aa[:, a:z, :], ALU.mult))
                link(V.scalar_tensor_tensor(out=X[:, a:z, :], in0=SS[:, a:z, :], scalar=0.5, in1=X[:, a:z, :],
                                            op0=ALU.mult, op1=ALU.add))
                for t in tiles:
                    last = V.bn_stats(st[:, t, :], X[:, t, :])
                link(last)
                for t in tiles:
                    last = V.bn_aggr(mv[:, t, :], st[:, t, :])
                link(last)
                V.tensor_scalar(ve[:, a:z], mv[:, a:z, 1], LN_EPS, None, ALU.add).then_inc(var1, 1)

            def norm_group(n):
                dve.wait_ge(rstd1, n + 1)
                for t in X_GROUPS[n]:
                    last = V.tensor_scalar(XN[:, t, :], X[:, t, :], mv[:, t, 0:1], rs[:, t:t + 1], ALU.subtract, ALU.mult)
                last.then_inc(xn1, 1)

            def xt_group(n):
                dve.wait_ge(xt_ps1, n + 1)
                a, z = X_GROUPS[n][0] * P, (X_GROUPS[n][-1] + 1) * P
                V.tensor_copy(XT[:, a:z], PS[:, B_S + 2, a:z]).then_inc(xt1, 1)

            dve.wait_ge(x_first, 16)
            norm_stats(first_norm, XN)
            dve.wait_ge(first_norm, 2)
            norm_apply(first_norm, first_norm, XN, XZ)
            dve.wait_ge(first_norm, 4)
            V.tensor_copy(XT[:, :], bank(B_U)).then_inc(first_norm, 1)
            dve.wait_ge(first_norm, 5)
            dve.wait_ge(s_et, 16)
            link(V.tensor_copy(e_parts[:, 0, :], e_full))
            link(V.tensor_tensor(e_rest, e_full, e_parts[:, 0, :], ALU.subtract))
            link(V.tensor_copy(e_parts[:, 1, :], e_rest))
            V.tensor_tensor(e_parts[:, 2, :], e_rest, e_parts[:, 1, :], ALU.subtract).then_inc(s_etp, 1)
            dve.wait_ge(s_wa, 16)
            dve.wait_ge(s_gexp, 1)
            link(V.tensor_scalar(gate_s, gate_e, 1.0, None, ALU.add))
            link(V.reciprocal(gate, gate_s))
            V.tensor_scalar(omg, gate, -1.0, 1.0, ALU.mult, ALU.add)
            V.tensor_scalar(GBV[:, :], w("bv"), gate, None, ALU.mult)
            V.tensor_scalar(qbias, w("sls"), -0.5 * log(HD), None, ALU.add)
            V.memset(epsc, 1e-6)
            V.memset(halfc, 0.5)
            V.tensor_scalar(hb1[:, :], w("b1"), 0.5, None, ALU.mult)
            V.tensor_copy(IDB[:, :], w("ident"))
            V.tensor_copy(MKN[:, :], w("maskn"))
            link(V.tensor_copy(MKT[:, :], w("maskt")))
            V.memset(ET[ROWS:P, :], 0.0)
            link(V.memset(KS[ROWS:P, :, :, :].rearrange("p a b s -> p (a b s)").bitcast(F32), BF16_ONES))
            V.engine_nop().then_inc(s_pre_dve, 1)
            dve.wait_ge(s_pre_pool, 4)
            dve.nop(nofuse=True)
            dve.sem_clear(chain_dve)
            with dve.Fori(0, B) as b:
                steps[0] = 0
                dve.wait_ge(hi_ready, 1)
                link(V.tensor_tensor(R3[:, 0:2, :], F3[:, 0:2, :], PARTS[:, 0:2, 0, :], ALU.subtract))
                V.engine_nop().then_inc(rest2_ready, 1)
                set_v(proj_v, v_set)
                ffn_dve(0)
                dve.wait_ge(mid_ready, 1)
                V.tensor_tensor(PARTS[:, 0:2, 2, :], R3[:, 0:2, :], PARTS[:, 0:2, 1, :], ALU.subtract).then_inc(parts_ready, 1)
                ffn_dve(1)
                dve.wait_ge(logit_ps, 1)
                V.tensor_copy(LG[:, :, :], bank(B_PV, T * E).rearrange("p (t e) -> p t e", e=E)).then_inc(logits_read, 1)
                dve.wait_ge(logits_read, 1)
                first_max(LG[:, :, :], m1[:, :], OH1[:, :, :])
                without(LG[:, :, :], OH1[:, :, :])
                first_max(LG[:, :, :], m2[:, :], OH2[:, :, :])
                V.tensor_tensor(dm[:, :], m2[:, :], m1[:, :], ALU.subtract).then_inc(rdm_ready, 1)
                ffn_dve(2)
                dve.wait_ge(rexp_ready, 1)
                link(V.tensor_scalar(w1[:, :], e2[:, :], 1.0, 2.0, ALU.add, ALU.mult))
                link(V.reciprocal(w1[:, :], w1[:, :]))
                link(V.tensor_tensor(w2[:, :], w1[:, :], e2[:, :], ALU.mult))
                link(V.tensor_tensor(OH1[:, :, :], OH1[:, :, :], over(w1), ALU.mult))
                link(V.tensor_tensor(OH2[:, :, :], OH2[:, :, :], over(w2), ALU.mult))
                link(V.tensor_tensor(W8[:, :, :], OH1[:, :, :], OH2[:, :, :], ALU.add))
                dve.wait_ge(glob_ps, 1)
                gl = [bank(B_S + a, 2 * (D + H)).rearrange("p (t c) -> p t c", t=2) for a in range(2)]
                den = RDN[:, :].rearrange("p (t h) -> p t h", t=T)
                for a in range(2):
                    last = V.tensor_scalar(den[:, 2 * a:2 * a + 2, :], gl[a][:, :, D:D + H], 1e-6, None, ALU.add)
                link(last)
                link(V.reciprocal(RDN[:, :], RDN[:, :]))
                link(V.tensor_scalar(RDN[:, :], RDN[:, :], omg, None, ALU.mult))
                for a in range(2):
                    last = V.tensor_tensor(G[:, 2 * a:2 * a + 2, :].rearrange("p t (h d) -> p t h d", h=H),
                                           gl[a][:, :, 0:D].rearrange("p t (h d) -> p t h d", h=H),
                                           den[:, 2 * a:2 * a + 2, :, None].to_broadcast([P, 2, H, HD]), ALU.mult)
                last.then_inc(gn_ready, 1)
                for s in range(3, FFN_BEFORE):
                    ffn_dve(s)
                dve.wait_ge(out_done, (b + 1) * 16)
                dve.nop(nofuse=True)
                V.tensor_copy(X[:, :, :], XN[:, :, :]).then_inc(x_kept, 1)
                dve.wait_ge(x_kept, 1)
                for i in range(NSLOT0):
                    if i < SLOTS0:
                        u, kb = i // T, i % T
                        tile = region(i % RING * TILE, TILE)
                        dve.wait_ge(sc_copied, G2 * (i + 1))
                        if kb == 0 and u:
                            dve.wait_ge(m1_ready, u)
                        V.tensor_reduce(R1[:, kb, :], tile.rearrange("p (a c) -> p a c", c=32), AX.X, ALU.max,
                                        apply_transpose=True).then_inc(red_done, 1)
                        if kb == T - 1:
                            dve.wait_ge(red_done, i + 1)
                            if u:
                                dve.wait_ge(mt_ps, u)
                            V.tensor_reduce(M1[:, 0:H * G2], R1[:, :, :].rearrange("p k c -> p c k"), AX.X, ALU.max
                                            ).then_inc(m1_ready, 1)
                    for v in range(NU):
                        if i == T * v + AT_MAX:
                            dve.wait_ge(mt_ps, v + 1)
                            if v:
                                dve.wait_ge(dm_out, 16 * v)
                            V.tensor_reduce(M2[:, :], PS[0:H * G2, B_MISC, 0:P].rearrange("c (a i) -> c i a", i=NQ),
                                            AX.X, ALU.max).then_inc(m2_ready, 1)
                        if i == T * v + AT_SUB:
                            tile = region((T * v + T - 1) % RING * TILE, TILE)
                            dve.wait_ge(mb_in[v % 2], 16 * (v // 2 + 1))
                            V.tensor_tensor(tile, tile, MB[:, v % 2, :], ALU.subtract).then_inc(sub_dve, 1)
                    if i - 1 in FFN_AT:
                        ffn_hh(FFN_AT[i - 1])
                    if i - 3 in FFN_AT and FFN_AT[i - 3] >= 2 and FFN_AT[i - 3] % 2 == 0:
                        ffn_acc(FFN_AT[i - 3] // 2 - 1)
                    for c in range(T):
                        if i == 2 * T * c + AT_NATURAL:
                            dve.wait_ge(nat_ps, c + 1)
                            n = bank(B_MISC, 2 * P).rearrange("p (a two d) -> p a two d", two=4, d=HD)
                            rd = RDN[:, 0:H].rearrange("p (a two) -> p a two", two=2)
                            link(V.reciprocal(rd, n[:, :, 2:4, 0]))
                            link(V.tensor_scalar(RDN[:, 0:H], RDN[:, 0:H], gate, None, ALU.mult))
                            if c:
                                dve.wait_ge(back_ps, c)
                            cn = CN[:, :].rearrange("p (a two d) -> p a two d", two=2, d=HD)
                            link(V.tensor_tensor(cn, n[:, :, 0:2, :], rd[:, :, :, None].to_broadcast([P, H // 2, 2, HD]), ALU.mult))
                            if c == 0:
                                dve.wait_ge(g_ready, 1)
                            V.tensor_tensor(CN[:, :], CN[:, :], G[:, c, :], ALU.add).then_inc(cn_ready, 1)
                        if i == 2 * T * c + AT_BACK:
                            dve.wait_ge(back_ps, c + 1)
                            V.tensor_copy(CT[:, :], bank(B_MISC, P)).then_inc(ct_ready, 1)
                        if i == 2 * T * c + AT_OUT:
                            dve.wait_ge(at_ps, c + 1)
                            V.tensor_tensor(SS[:, c, :], bank(B_MISC, P), w("bo"), ALU.add).then_inc(ss_ready, 1)
                    if i == FFN_LAST + 3:
                        ffn_acc(E)
                    if i == AT_MIX:
                        dve.wait_ge(ga_ready, 1)
                        link(V.scalar_tensor_tensor(out=AA[:, :], in0=TH[:, :], scalar=1.0,
                                                    in1=ACC[:, :, :].rearrange("p t d -> p (t d)"), op0=ALU.add, op1=ALU.mult))
                        mix_and_stats(0)
                    if i == AT_MIX + 1:
                        norm_group(0)
                    if i == AT_MIX + 3:
                        xt_group(0)
                mix_and_stats(1)
                norm_group(1)
                xt_group(1)

                from_layer0_to_1(dve, b)
                dve.wait_ge(lg_ps1, 1)
                V.tensor_copy(LG[:, :, :], bank(B_PV, T * E).rearrange("p (t e) -> p t e", e=E)).then_inc(lg_read1, 1)
                dve.wait_ge(lg_read1, 1)
                link(V.tensor_reduce(m1[:, :], LG[:, :, :], AX.X, ALU.max))
                V.tensor_tensor(KEY[:, :, :], LG[:, :, :], over(m1), ALU.subtract).then_inc(lge_r, 1)
                for n, t in enumerate(ORDER1):
                    dve.wait_ge(ex_r, n + 1)
                    V.tensor_scalar(U1[:, t, :], EX[:, t, :], 1.0, None, ALU.add).then_inc(u_r, 1)
                for n, t in enumerate(ORDER1):
                    dve.wait_ge(u_r, n + 1)
                    V.scalar_tensor_tensor(out=C1[:, t, :], in0=U1[:, t, :], scalar=-1.0, in1=EX[:, t, :],
                                           op0=ALU.add, op1=ALU.subtract).then_inc(c1_r, 1)

                def shared_hh(s):
                    dve.wait_ge(th1_r, s + 1)
                    link(V.scalar_tensor_tensor(out=AA[:, :], in0=TH[:, :], scalar=1.0, in1=bank(B_H), op0=ALU.add, op1=ALU.mult))
                    link(V.tensor_scalar(AA[:, :], AA[:, :], 0.5, None, ALU.mult))
                    V.tensor_tensor(HH[:, 0, s, :], AA[:, :], bank(B_U), ALU.mult).then_inc(h1_r, 1)
                    dve.wait_ge(h1_r, s + 1)

                shared_hh(0)
                set_v(v_ps1, v_set1)
                dve.wait_ge(lgx_r, 1)
                link(V.tensor_reduce(m2[:, :], EQ[:, :, :], AX.X, ALU.add))
                link(V.reciprocal(m2[:, :], m2[:, :]))
                link(V.tensor_tensor(LG[:, :, :], EQ[:, :, :], over(m2), ALU.mult))
                link(V.tensor_copy(WM[:, :, :], LG[:, :, :]))
                first_max(LG[:, :, :], m1[:, :], OH1[:, :, :])
                for n, t in enumerate(ORDER1):
                    dve.wait_ge(ln_r, n + 1)
                    dve.wait_ge(c1_r, n + 1)
                    link(V.tensor_tensor(C1[:, t, :], LNU[:, t, :], C1[:, t, :], ALU.subtract))
                    V.scalar_tensor_tensor(out=EX[:, t, :], in0=bank(AMP_BANK[t]), scalar=0.0, in1=C1[:, t, :],
                                           op0=ALU.max, op1=ALU.add).then_inc(amp_r, 1)
                without(LG[:, :, :], OH1[:, :, :])
                first_max(LG[:, :, :], m2[:, :], OH2[:, :, :])
                link(V.tensor_tensor(WMK[:, :, E:2 * E], OH1[:, :, :], OH2[:, :, :], ALU.add))
                V.tensor_tensor(WMK[:, :, 0:E], WM[:, :, :], WMK[:, :, E:2 * E], ALU.mult).then_inc(wm_r, 1)
                dve.wait_ge(cos_r, 2)
                dve.wait_ge(amp_r, 2)
                for n, t in enumerate(ORDER1):
                    V.tensor_tensor(CS4[:, t, 0, :], EX[:, t, :], CO[:, t, :], ALU.mult)
                    last = V.tensor_tensor(CS4[:, t, 1, :], EX[:, t, :], SI[:, t, :], ALU.mult)
                link(last)
                for n, t in enumerate(ORDER1):
                    dve.wait_ge(rt_r, n + 1)
                    V.tensor_tensor(CS4[:, t, :, :], CS4[:, t, :, :], RT[:, t, None, :].to_broadcast([P, 2, S]), ALU.mult
                                    ).then_inc(cs_r, 1)
                dve.wait_ge(wt_ps, 1)
                V.tensor_copy(WT[:, :], PS[0:2 * E, B_PV, :]).then_inc(wt_r, 1)
                for n, t in enumerate(ORDER1):
                    dve.wait_ge(hi1_r, n + 1)
                    dve.wait_ge(cs_r, n + 1)
                    V.tensor_tensor(R4[:, t, :, :], CS4[:, t, :, :], PARTS1[:, t, 0, :, :], ALU.subtract).then_inc(rest1_r, 1)
                for n, t in enumerate(ORDER1):
                    dve.wait_ge(mid1_r, n + 1)
                    dve.wait_ge(rest1_r, n + 1)
                    V.tensor_tensor(PARTS1[:, t, 2, :, :], R4[:, t, :, :], PARTS1[:, t, 1, :, :], ALU.subtract).then_inc(parts1, 1)
                shared_hh(1)
                dve.wait_ge(fo1_ps, 1)
                V.tensor_copy(YT[:, :], bank(B_O)).then_inc(yn_r, 1)

                def expert_h(e):
                    dve.wait_ge(sig1_r, e + 1)
                    dve.wait_ge(fo1_ps, e + 1)
                    V.scalar_tensor_tensor(out=HE, in0=bank(expert_banks(e)[0]), scalar=w("b1", e, 1), in1=AA[:, :],
                                           op0=ALU.add, op1=ALU.mult).then_inc(he_r, 1)

                def expert_y(e):
                    dve.wait_ge(fo1_ps, e + 2)
                    dve.wait_ge(c3m_r, e + 1)
                    if e >= 2:
                        dve.wait_ge(y_add, e - 1)
                    V.scalar_tensor_tensor(out=CC[:, e % 2, :], in0=bank(B_O), scalar=w("b2", e, 1), in1=C3[e % 2],
                                           op0=ALU.add, op1=ALU.mult).then_inc(y_c, 1)

                expert_h(0)
                for e in range(1, WINDOW):
                    expert_h(e)
                    expert_y(e - 1)
                expert_y(WINDOW - 1)
                for i in range(NSLOT1):
                    if i < 2 * HALF_BANKS:
                        tile, h0, heads = BANKS1[i]
                        width = (tile + 1) * P
                        dve.wait_ge(s1_ps, i + 1)
                        V.tensor_reduce(M1[:, :].rearrange("p (h t) -> p h t", t=T)[:, h0:h0 + heads, tile],
                                        bank(bank1(i), heads * width).rearrange("p (a k) -> p a k", k=width),
                                        AX.X, ALU.max).then_inc(s1_max, 1)
                    for g in range(2):
                        if i == NM_AT[g] + (1 - g):
                            dve.wait_ge(nmt_ps, g + 1)
                            link(V.tensor_scalar(NM[:, :], PS[0:H * T // 2, (B_PV, B_S)[g], 0:P], -1.0, None, ALU.mult))
                            split(NM[:, :], NR[:, :], [NMP[:, g, c, :] for c in range(3)]).then_inc(nm_r, 1)
                            dve.wait_ge(nm_r, g + 1)
                    for e, (_, at_h, _, at_y) in EXPERT_AT.items():
                        if i == at_h:
                            expert_h(e)
                        if i == at_y:
                            expert_y(e)
                dve.wait_ge(x_next, 16)
                norm_stats(var_next, XN)
                norm_apply(rstd_next, xn_next, XN, XZ)
                dve.wait_ge(xs_r, E)
                dve.wait_ge(xt_next_ps, 1)
                V.tensor_copy(XT[:, :], bank(B_U)).then_inc(xt_next, 1)
                rd1 = RDN[:, 0:2 * H].rearrange("p (a two) -> p a two", two=2)
                for a in range(2):
                    dve.wait_ge(nat1_ps, a + 1)
                    n1 = bank((B_MISC, B_H)[a]).rearrange("p (a two d) -> p a two d", two=4, d=HD)
                    link(V.reciprocal(rd1, n1[:, :, 2:4, 0]))
                    link(V.tensor_tensor(CN1[:, 2 * a:2 * a + 2, :].rearrange("p t (a two d) -> p (t a) two d", two=2, d=HD),
                                         n1[:, :, 0:2, :], rd1[:, :, :, None].to_broadcast([P, H, 2, HD]), ALU.mult))
                    V.engine_nop().then_inc(cn1, 1)
                dve.wait_ge(back1_ps, 1)
                V.tensor_copy(CTT, bank(B_U)).then_inc(ctt_r, 1)
                dve.wait_ge(ga1, 1)
                V.scalar_tensor_tensor(out=AA[:, :], in0=TH[:, :], scalar=1.0, in1=bank(B_O), op0=ALU.add, op1=ALU.mult
                                       ).then_inc(y1_r, 1)
                dve.wait_ge(y1_r, 1)
                dve.wait_ge(at1_ps, 1)
                link(V.tensor_tensor(AA[:, :], AA[:, :], bank(B_PV), ALU.mult))
                xf = X[:, :, :].rearrange("p t d -> p (t d)")
                V.scalar_tensor_tensor(out=xf, in0=AA[:, :], scalar=0.5, in1=xf, op0=ALU.mult, op1=ALU.add).then_inc(xo_r, 1)
                dve.wait_ge(xo_r, 1)
                end_sequence(dve, b)
                dve.sem_clear(chain_dve)


def kernel(**inputs):
    import concourse.bacc as bacc
    from concourse.bass_utils import run_bass_kernel_spmd as run

    g = {k: np.asarray(v) for k, v in inputs.items()}

    def col(v):
        return np.asarray(v).reshape(P, 1)

    by_dim = np.arange(D).reshape(H, HD).T.ravel()

    def a0(n):
        return g["L0_attn_" + n]

    def f0(n):
        return g["L0_ffn_" + n]

    def a1(n):
        return g["L1_attn_" + n]

    def f1(n):
        return g["L1_ffn_" + n]

    zero = np.zeros((), np.float32)
    mbd = np.zeros((P, P), np.float32)
    zh = np.zeros((P, H), np.float32)
    for h in range(H):
        r = slice(h * HD, h * HD + HD)
        mbd[r, r] = a0("M")[h]
        zh[r, h] = a0("z")[h]

    mean8 = np.kron(np.full((HD, HD), 1 / HD), np.eye(H)).astype(np.float32)
    maskn = np.triu(np.full((P, P), NEG, np.float32), 1)

    def rows(v):
        return np.broadcast_to(v[None, :], (P, v.shape[0]))

    def two(v):
        return v.reshape(2, P, -1).transpose(1, 0, 2).reshape(P, -1)

    rel = a0("rel_emb")
    parts = {
        "WqT": a0("Wq").T[:, by_dim], "WkT": a0("Wk").T[:, by_dim], "WvT": a0("Wv").T, "gate0": f0("gate_w"), "MZ": np.concatenate([mbd, zh], 1)[by_dim],
        "ident": np.eye(P, dtype=np.float32), "idx": rows(np.arange(E, 0, -1).astype(np.float32)),
        "bq": col(a0("bq")[by_dim]), "bk": col(a0("bk")[by_dim]), "bv": rows(a0("bv")),
        "e_near": col(np.repeat(rel[2 * REL], H)), "e_far": col(np.repeat(rel[0], H)),
        "alpha": np.broadcast_to(a0("gate_alpha").reshape(1, 1), (P, 1)), "sls": col(np.tile(a1("score_log_scale"), HD)),
        "halfpi": np.full((P, 1), pi / 2, np.float32),
        "b1": f1("b1").T, "b2": f1("b2").T, "b3": f1("b3").T, "mean8": mean8, "maskn": maskn, "maskt": maskn.T,
        "bo": rows(a0("bo")), "WoT": a0("Wo").T,
        "sw1": f0("sw1"), "sw2": f0("sw2"), "sw3": two(f0("sw3")),
        "ew1": f0("ew1").transpose(1, 0, 2).reshape(D, -1), "ew2": f0("ew2").transpose(1, 0, 2).reshape(D, -1),
        "ew3": f0("ew3").reshape(E, 2, P, D).transpose(2, 0, 1, 3).reshape(P, -1),
        "Wqa": a1("Wq_amp").T[:, by_dim], "Wka": a1("Wk_amp").T[:, by_dim], "Wqp": a1("Wq_phi").T[:, by_dim],
        "Wkp": a1("Wk_phi").T[:, by_dim], "Wv1": a1("Wv").T,
        "WoT1": a1("Wo").T, "gate1": f1("gate_w").T,
        "tw1": f1("w1").transpose(2, 0, 1).reshape(D, -1), "tw2": f1("w2").transpose(2, 0, 1).reshape(HID, -1),
        "tw3": f1("w3").transpose(2, 0, 1).reshape(D, -1),
        "tsw1": f1("sw1").T, "tsw2": f1("sw2").T, "tsw3": two(f1("sw3").T),
    }

    def pack(cols):
        return np.ascontiguousarray(np.concatenate([parts[n].reshape(P, k) for n, k in cols], 1, dtype=np.float32))

    j = np.arange(4 * P)
    etab = np.concatenate([rel[np.clip(q - (j - 2 * P), -REL, REL) + REL].T for q in range(2)], 0)
    x = a0("hidden_states").reshape(B * S, D)
    x = np.concatenate([x, x[:S]])
    arrays = {
        "x": x, "wa": pack(COLS_A), "wb": pack(COLS_B),
        "wc": pack(COLS_C), "etab": np.ascontiguousarray(etab),
    }
    nc = bacc.Bacc("TRN2", target_bir_lowering=False, num_devices=1)
    args = [nc.dram_tensor(n, a.shape, mybir.dt.from_np(a.dtype), kind="ExternalInput").ap() for n, a in arrays.items()]
    args.append(nc.dram_tensor("out", (B * S, D), F32, kind="ExternalOutput").ap())
    program(nc, *args)
    r = run(nc, [arrays], core_ids=[0])
    return r.results[0]["out"].reshape(B, S, D)
```
